# Optimizing a Trainium2 kernel written in Bass

```python
import numpy as np
import jax
import jax.numpy as jnp

def _softmax(x, axis=-1):
    return jax.nn.softmax(x, axis=axis)

def _gelu(x):
    return jax.nn.gelu(x, approximate=True)

def _silu(x):
    return jax.nn.silu(x)

def _sigmoid(x):
    return jax.nn.sigmoid(x)

def _layernorm(x, axis=-1, eps=1e-05):
    m = jnp.mean(x, axis=axis, keepdims=True)
    v = jnp.var(x, axis=axis, keepdims=True)
    return (x - m) / jnp.sqrt(v + eps)

def _scatter_add(tgt, idx, src, axis=0):
    return tgt.at[idx].add(src)

def _segment_sum(src, seg, n):
    return jax.ops.segment_sum(src, seg, n)
kernel_name = 'mk_adaln_attn_ffn_d2_seqx_r8_2a09cc'

def setup_inputs(seed: int=0):
    np.random.seed(seed)
    _w = jnp.asarray

    def _rec_inputs():
        import jax
        import jax.numpy as jnp
        _rk = jax.random.key(seed)
        x = -7.109e-05 + 0.9999 * jax.random.normal(jax.random.fold_in(_rk, 1), (32, 32, 256), jnp.float32)
        _lenS = 32 - jax.random.randint(jax.random.fold_in(_rk, 7), (32,), 0, max(1, 32 // 4) + 1, jnp.int32)
        _lenS2 = 32 - jax.random.randint(jax.random.fold_in(_rk, 8), (32,), 0, max(1, 32 // 4) + 1, jnp.int32)
        itok_B_1_198 = jax.random.randint(jax.random.fold_in(_rk, 11), (32,), 1, 199, jnp.int32)
        itok_B_0_7 = jax.random.randint(jax.random.fold_in(_rk, 12), (32,), 0, 8, jnp.int32)
        cond_1 = jax.random.uniform(jax.random.fold_in(_rk, 13), (32, 1), jnp.float32, 0.0, 1.37214)
        itok_Bx257_0_4111 = jax.random.randint(jax.random.fold_in(_rk, 14), (32, 257), 0, 514, jnp.int32)
        itok_B_37_3939 = jax.random.randint(jax.random.fold_in(_rk, 15), (32,), 37, 3940, jnp.int32)
        return (x, itok_B_1_198, itok_B_0_7, cond_1, itok_Bx257_0_4111, itok_B_37_3939)
    x, itok_B_1_198, itok_B_0_7, cond_1, itok_Bx257_0_4111, itok_B_37_3939 = _rec_inputs()

    def _L0_cond_setup():
        import jax, jax.numpy as jnp
        import numpy as np
        B, C, T = (128, 32, 256)
        S, D = (200, 32)
        key = jax.random.key(seed)
        k1, k2, k3 = jax.random.split(key, 3)
        x = jax.random.normal(k1, (B, C, T), dtype=jnp.float32)
        conditions = jax.random.randint(k2, (B,), 0, S, dtype=jnp.int64)
        weights = jax.random.normal(k3, (S, C, D), dtype=jnp.float32) / jnp.sqrt(jnp.float32(C))
        return {'x': x, 'conditions': conditions, 'weights': weights}
    _L0_cond_all = _L0_cond_setup()
    _L0_cond_in = {k: v for k, v in _L0_cond_all.items() if k in ('weights',)}
    del _L0_cond_all

    def _L0_attn_setup():
        import jax, jax.numpy as jnp
        import numpy as np
        D_MODEL = 256
        N_HEADS = 16
        D_HEAD = D_MODEL // N_HEADS
        B, S = (2, 256)
        EPS = 1e-05

        def _mhsa(X, ln_g, ln_b, Wq, bq, Wk, bk, Wv, bv, Wo, bo):
            n_ctx = X.shape[-2]
            mu = jnp.mean(X, axis=-1, keepdims=True)
            var = jnp.mean(jnp.square(X - mu), axis=-1, keepdims=True)
            Xn = (X - mu) * jax.lax.rsqrt(var + EPS) * ln_g + ln_b

            def split_heads(t):
                return t.reshape(t.shape[:-1] + (N_HEADS, D_HEAD)).swapaxes(-2, -3)
            Q = split_heads(Xn @ Wq + bq)
            K = split_heads(Xn @ Wk + bk)
            V = split_heads(Xn @ Wv + bv)
            scores = jnp.einsum('bhqd,bhkd->bhqk', Q, K) / jnp.sqrt(jnp.float32(D_HEAD))
            causal = jnp.tril(jnp.ones((n_ctx, n_ctx), dtype=bool))
            scores = jnp.where(causal, scores, jnp.float32(-jnp.inf))
            A = jax.nn.softmax(scores, axis=-1)
            AV = jnp.einsum('bhqk,bhkd->bhqd', A, V)
            AV = AV.swapaxes(-2, -3).reshape(X.shape[:-1] + (D_MODEL,))
            return AV @ Wo + bo
        key = jax.random.key(seed)
        ks = jax.random.split(key, 10)
        sd = 1.0 / np.sqrt(D_MODEL)
        inp = {'X': jax.random.normal(ks[0], (B, S, D_MODEL), dtype=jnp.float32), 'ln_g': jnp.ones((D_MODEL,), jnp.float32), 'ln_b': jnp.zeros((D_MODEL,), jnp.float32), 'Wq': jax.random.uniform(ks[1], (D_MODEL, D_MODEL), jnp.float32, -sd, sd), 'bq': jax.random.uniform(ks[2], (D_MODEL,), jnp.float32, -sd, sd), 'Wk': jax.random.uniform(ks[3], (D_MODEL, D_MODEL), jnp.float32, -sd, sd), 'bk': jax.random.uniform(ks[4], (D_MODEL,), jnp.float32, -sd, sd), 'Wv': jax.random.uniform(ks[5], (D_MODEL, D_MODEL), jnp.float32, -sd, sd), 'bv': jax.random.uniform(ks[6], (D_MODEL,), jnp.float32, -sd, sd), 'Wo': jax.random.uniform(ks[7], (D_MODEL, D_MODEL), jnp.float32, -sd, sd), 'bo': jax.random.uniform(ks[8], (D_MODEL,), jnp.float32, -sd, sd)}
        return inp
    _L0_attn_all = _L0_attn_setup()
    _L0_attn_in = {k: v for k, v in _L0_attn_all.items() if k in ('ln_g', 'ln_b', 'Wq', 'bq', 'Wk', 'bk', 'Wv', 'bv', 'Wo', 'bo')}
    del _L0_attn_all

    def _L0_cond2_setup():
        import jax, jax.numpy as jnp
        import numpy as np

        def _lora_linear(x, W, A, B, adapter_indices):
            base = jnp.einsum('bsd,df->bsf', x, W)
            Ai = A[adapter_indices]
            Bi = B[adapter_indices]
            lora = jnp.einsum('bsr,brf->bsf', jnp.einsum('bsd,bdr->bsr', x, Ai), Bi)
            return base + lora
        key = jax.random.key(seed)
        ks = jax.random.split(key, 10)
        H, I, N, R = (256, 1024, 8, 16)
        B, S = (4, 256)
        std_h = 1.0 / np.sqrt(H)
        std_i = 1.0 / np.sqrt(I)
        x = jax.random.normal(ks[0], (B, S, H), dtype=jnp.float32)
        adapter_indices = jax.random.randint(ks[1], (B,), 0, N, dtype=jnp.int32)
        Wg = jax.random.normal(ks[2], (H, I), dtype=jnp.float32) * std_h
        Wu = jax.random.normal(ks[3], (H, I), dtype=jnp.float32) * std_h
        Wd = jax.random.normal(ks[4], (I, H), dtype=jnp.float32) * std_i
        Ag = jax.random.normal(ks[5], (N, H, R), dtype=jnp.float32) * std_h
        Bg = jnp.zeros((N, R, I), dtype=jnp.float32) + 0.01
        Au = jax.random.normal(ks[6], (N, H, R), dtype=jnp.float32) * std_h
        Bu = jnp.zeros((N, R, I), dtype=jnp.float32) + 0.01
        Ad = jax.random.normal(ks[7], (N, I, R), dtype=jnp.float32) * std_i
        Bd = jnp.zeros((N, R, H), dtype=jnp.float32) + 0.01
        return {'x': x, 'Wg': Wg, 'Wu': Wu, 'Wd': Wd, 'Ag': Ag, 'Bg': Bg, 'Au': Au, 'Bu': Bu, 'Ad': Ad, 'Bd': Bd, 'adapter_indices': adapter_indices}
    _L0_cond2_all = _L0_cond2_setup()
    _L0_cond2_in = {k: v for k, v in _L0_cond2_all.items() if k in ('Wg', 'Wu', 'Wd', 'Ag', 'Bg', 'Au', 'Bu', 'Ad', 'Bd')}
    del _L0_cond2_all

    def _L0_ffn_setup():
        import jax, jax.numpy as jnp
        import numpy as np
        DIM_IN = 256
        DIM_HIDDEN = 1024
        key = jax.random.key(seed)
        k_x, k_g, k_u, k_d = jax.random.split(key, 4)
        s_in = 1.0 / np.sqrt(DIM_IN)
        s_hid = 1.0 / np.sqrt(DIM_HIDDEN)
        x = jax.random.normal(k_x, (4, 256, DIM_IN), dtype=jnp.float32)
        w_gate = jax.random.uniform(k_g, (DIM_HIDDEN, DIM_IN), jnp.float32, -s_in, s_in)
        w_up = jax.random.uniform(k_u, (DIM_HIDDEN, DIM_IN), jnp.float32, -s_in, s_in)
        w_down = jax.random.uniform(k_d, (DIM_IN, DIM_HIDDEN), jnp.float32, -s_hid, s_hid)
        return {'x': x, 'w_gate': w_gate, 'w_up': w_up, 'w_down': w_down}
    _L0_ffn_all = _L0_ffn_setup()
    _L0_ffn_in = {k: v for k, v in _L0_ffn_all.items() if k in ('w_gate', 'w_up', 'w_down')}
    del _L0_ffn_all

    def _L1_cond_setup():
        import jax, jax.numpy as jnp
        import numpy as np
        B, S, D_MODEL, NHEAD = (4, 256, 256, 16)
        HEAD_DIM = D_MODEL // NHEAD
        key = jax.random.key(seed)
        ks = jax.random.split(key, 6)
        scale = 1.0 / np.sqrt(D_MODEL)
        return {'hidden_states': jax.random.normal(ks[0], (B, S, D_MODEL), dtype=jnp.float32), 'attention_precision': jax.random.uniform(ks[1], (B, 1, 1), dtype=jnp.float32, minval=0.5, maxval=2.0), 'Wq': jax.random.normal(ks[2], (D_MODEL, D_MODEL), dtype=jnp.float32) * scale, 'Wk': jax.random.normal(ks[3], (D_MODEL, D_MODEL), dtype=jnp.float32) * scale, 'Wv': jax.random.normal(ks[4], (D_MODEL, D_MODEL), dtype=jnp.float32) * scale, 'Wo': jax.random.normal(ks[5], (D_MODEL, D_MODEL), dtype=jnp.float32) * scale}
    _L1_cond_all = _L1_cond_setup()
    _L1_cond_in = {k: v for k, v in _L1_cond_all.items() if k in ('Wq', 'Wk', 'Wv', 'Wo')}
    del _L1_cond_all

    def _L1_attn_setup():
        import jax, jax.numpy as jnp
        import numpy as np
        B, S, HID = (4, 512, 256)
        H, NB = (16, 4)
        D = HID // H
        EPS = 1e-06

        def elu_plus_one(x):
            return jax.nn.elu(x) + 1.0

        def _reference_tuple_inner(hidden_states, Wq, Wk, Wv, Wo, bank_weights, memories, memory_norms):
            b, s, _ = hidden_states.shape

            def proj(W):
                return (hidden_states @ W.T).reshape(b, s, H, D).transpose(0, 2, 1, 3)
            q, k, v = (proj(Wq), proj(Wk), proj(Wv))
            sigma_q = elu_plus_one(q)
            a_unnorm = jnp.einsum('bhsd,nhde->nbhse', sigma_q, memories)
            norm = jnp.einsum('bhsd,nhd->nbhs', sigma_q, memory_norms)
            a = a_unnorm / jnp.clip(norm, EPS, None)[..., None]
            active = (memory_norms.sum(axis=(1, 2)) >= EPS).astype(a.dtype)
            a = a * active[:, None, None, None, None]
            weights = jax.nn.softmax(bank_weights, axis=-1)
            combined = jnp.einsum('nbhse,hn->bhse', a, weights)
            sigma_k = elu_plus_one(k)
            mem0, norm0 = (memories[0], memory_norms[0])
            retr = jnp.einsum('bhsd,hde->bhse', sigma_k, mem0)
            knorm = jnp.clip(jnp.einsum('bhsd,hd->bhs', sigma_k, norm0), EPS, None)
            delta_v = v - retr / knorm[..., None]
            mem_update = jnp.einsum('bhsd,bhse->hde', sigma_k, delta_v) / (b * s)
            new_mem0 = jax.lax.stop_gradient(mem0 + mem_update)
            new_norm0 = jax.lax.stop_gradient(norm0 + sigma_k.sum(axis=(0, 2)) / b)
            out = combined.transpose(0, 2, 1, 3).reshape(b, s, HID) @ Wo.T
            return (out, new_mem0, new_norm0)
        key = jax.random.key(seed)
        ks = jax.random.split(key, 8)
        return {'hidden_states': jax.random.normal(ks[0], (B, S, HID), jnp.float32), 'Wq': jax.random.normal(ks[1], (HID, HID), jnp.float32) * 0.02, 'Wk': jax.random.normal(ks[2], (HID, HID), jnp.float32) * 0.02, 'Wv': jax.random.normal(ks[3], (HID, HID), jnp.float32) * 0.02, 'Wo': jax.random.normal(ks[4], (HID, HID), jnp.float32) * 0.02, 'bank_weights': jax.random.normal(ks[5], (H, NB), jnp.float32) * 0.02, 'memories': jax.random.uniform(ks[6], (NB, H, D, D), jnp.float32), 'memory_norms': jax.random.uniform(ks[7], (NB, H, D), jnp.float32)}
    _L1_attn_all = _L1_attn_setup()
    _L1_attn_in = {k: v for k, v in _L1_attn_all.items() if k in ('Wq', 'Wk', 'Wv', 'Wo', 'bank_weights', 'memories', 'memory_norms')}
    del _L1_attn_all

    def _L1_cond2_setup():
        import jax, jax.numpy as jnp
        import numpy as np
        H, G, HD = (8, 4, 32)
        GSZ = H // G
        BLOCK = 16
        WINDOW = 128
        SCALE = 256.0 ** (-0.5)
        EPS = 1e-06
        THETA = 10000.0
        B, T, D = (16, 4, 256)
        NBLK = 257

        def _rms(x, scale):
            var = jnp.mean(x * x, axis=-1, keepdims=True)
            return x * jax.lax.rsqrt(var + EPS) * (1.0 + scale)

        def _rope(x, pos):
            half = HD // 2
            inv = 1.0 / THETA ** (jnp.arange(half, dtype=jnp.float32) / half)
            ang = pos[:, :, None].astype(jnp.float32) * inv
            cos = jnp.cos(ang)[:, None, :, :]
            sin = jnp.sin(ang)[:, None, :, :]
            x1, x2 = (x[..., :half], x[..., half:])
            return jnp.concatenate([x1 * cos - x2 * sin, x2 * cos + x1 * sin], axis=-1)
        key = jax.random.key(seed)
        ks = jax.random.split(key, 10)
        inv_d = 1.0 / np.sqrt(D)
        return {'x': jax.random.normal(ks[0], (B, T, D), jnp.float32), 'Wq': jax.random.normal(ks[1], (H * HD, D), jnp.float32) * inv_d, 'Wk': jax.random.normal(ks[2], (G * HD, D), jnp.float32) * inv_d, 'Wv': jax.random.normal(ks[3], (G * HD, D), jnp.float32) * inv_d, 'Wo': jax.random.normal(ks[4], (D, H * HD), jnp.float32) * inv_d, 'q_norm_scale': jax.random.normal(ks[5], (HD,), jnp.float32) * 0.02, 'k_norm_scale': jax.random.normal(ks[6], (HD,), jnp.float32) * 0.02, 'k_blocks': jax.random.normal(ks[7], (B * NBLK, G, BLOCK, HD), jnp.float32), 'v_blocks': jax.random.normal(ks[8], (B * NBLK, G, BLOCK, HD), jnp.float32), 'block_tables': jnp.arange(B * NBLK, dtype=jnp.int32).reshape(B, NBLK), 'kv_lens': jax.random.randint(ks[9], (B,), 0, 512, dtype=jnp.int32)}
    _L1_cond2_all = _L1_cond2_setup()
    _L1_cond2_in = {k: v for k, v in _L1_cond2_all.items() if k in ('Wq', 'Wk', 'Wv', 'Wo', 'q_norm_scale', 'k_norm_scale', 'k_blocks', 'v_blocks')}
    del _L1_cond2_all

    def _L1_ffn_setup():
        import jax, jax.numpy as jnp
        import numpy as np
        TOPK = 2
        NORM_TOPK = True
        SCALE = 1.0
        EPS = 1e-09
        key = jax.random.key(seed)
        ks = jax.random.split(key, 9)
        h, i, E = (256, 128, 16)
        std = 0.02
        return {'x': jax.random.normal(ks[0], (1, 256, h), jnp.float32), 'Wr': jax.random.normal(ks[1], (E, h), jnp.float32) * std, 'bias': jnp.zeros((E,), jnp.float32), 'Wg': jax.random.normal(ks[2], (E, h, i), jnp.float32) * std, 'Wu': jax.random.normal(ks[3], (E, h, i), jnp.float32) * std, 'Wd': jax.random.normal(ks[4], (E, i, h), jnp.float32) * std, 'sWg': jax.random.normal(ks[5], (h, i), jnp.float32) * std, 'sWu': jax.random.normal(ks[6], (h, i), jnp.float32) * std, 'sWd': jax.random.normal(ks[7], (i, h), jnp.float32) * std}
    _L1_ffn_all = _L1_ffn_setup()
    _L1_ffn_in = {k: v for k, v in _L1_ffn_all.items() if k in ('Wr', 'bias', 'Wg', 'Wu', 'Wd', 'sWg', 'sWu', 'sWd')}
    del _L1_ffn_all
    return {'x': x, 'itok_B_1_198': itok_B_1_198, 'itok_B_0_7': itok_B_0_7, 'cond_1': cond_1, 'itok_Bx257_0_4111': itok_Bx257_0_4111, 'itok_B_37_3939': itok_B_37_3939, 'L0_cond_weights': _L0_cond_in['weights'], 'L0_attn_ln_g': _L0_attn_in['ln_g'], 'L0_attn_ln_b': _L0_attn_in['ln_b'], 'L0_attn_Wq': _L0_attn_in['Wq'], 'L0_attn_bq': _L0_attn_in['bq'], 'L0_attn_Wk': _L0_attn_in['Wk'], 'L0_attn_bk': _L0_attn_in['bk'], 'L0_attn_Wv': _L0_attn_in['Wv'], 'L0_attn_bv': _L0_attn_in['bv'], 'L0_attn_Wo': _L0_attn_in['Wo'], 'L0_attn_bo': _L0_attn_in['bo'], 'L0_cond2_Wg': _L0_cond2_in['Wg'], 'L0_cond2_Wu': _L0_cond2_in['Wu'], 'L0_cond2_Wd': _L0_cond2_in['Wd'], 'L0_cond2_Ag': _L0_cond2_in['Ag'], 'L0_cond2_Bg': _L0_cond2_in['Bg'], 'L0_cond2_Au': _L0_cond2_in['Au'], 'L0_cond2_Bu': _L0_cond2_in['Bu'], 'L0_cond2_Ad': _L0_cond2_in['Ad'], 'L0_cond2_Bd': _L0_cond2_in['Bd'], 'L0_ffn_w_gate': _L0_ffn_in['w_gate'], 'L0_ffn_w_up': _L0_ffn_in['w_up'], 'L0_ffn_w_down': _L0_ffn_in['w_down'], 'L1_cond_Wq': _L1_cond_in['Wq'], 'L1_cond_Wk': _L1_cond_in['Wk'], 'L1_cond_Wv': _L1_cond_in['Wv'], 'L1_cond_Wo': _L1_cond_in['Wo'], 'L1_attn_Wq': _L1_attn_in['Wq'], 'L1_attn_Wk': _L1_attn_in['Wk'], 'L1_attn_Wv': _L1_attn_in['Wv'], 'L1_attn_Wo': _L1_attn_in['Wo'], 'L1_attn_bank_weights': _L1_attn_in['bank_weights'], 'L1_attn_memories': _L1_attn_in['memories'], 'L1_attn_memory_norms': _L1_attn_in['memory_norms'], 'L1_cond2_Wq': _L1_cond2_in['Wq'], 'L1_cond2_Wk': _L1_cond2_in['Wk'], 'L1_cond2_Wv': _L1_cond2_in['Wv'], 'L1_cond2_Wo': _L1_cond2_in['Wo'], 'L1_cond2_q_norm_scale': _L1_cond2_in['q_norm_scale'], 'L1_cond2_k_norm_scale': _L1_cond2_in['k_norm_scale'], 'L1_cond2_k_blocks': _L1_cond2_in['k_blocks'], 'L1_cond2_v_blocks': _L1_cond2_in['v_blocks'], 'L1_ffn_Wr': _L1_ffn_in['Wr'], 'L1_ffn_bias': _L1_ffn_in['bias'], 'L1_ffn_Wg': _L1_ffn_in['Wg'], 'L1_ffn_Wu': _L1_ffn_in['Wu'], 'L1_ffn_Wd': _L1_ffn_in['Wd'], 'L1_ffn_sWg': _L1_ffn_in['sWg'], 'L1_ffn_sWu': _L1_ffn_in['sWu'], 'L1_ffn_sWd': _L1_ffn_in['sWd']}

def reference(x, itok_B_1_198, itok_B_0_7, cond_1, itok_Bx257_0_4111, itok_B_37_3939, L0_cond_weights, L0_attn_ln_g, L0_attn_ln_b, L0_attn_Wq, L0_attn_bq, L0_attn_Wk, L0_attn_bk, L0_attn_Wv, L0_attn_bv, L0_attn_Wo, L0_attn_bo, L0_cond2_Wg, L0_cond2_Wu, L0_cond2_Wd, L0_cond2_Ag, L0_cond2_Bg, L0_cond2_Au, L0_cond2_Bu, L0_cond2_Ad, L0_cond2_Bd, L0_ffn_w_gate, L0_ffn_w_up, L0_ffn_w_down, L1_cond_Wq, L1_cond_Wk, L1_cond_Wv, L1_cond_Wo, L1_attn_Wq, L1_attn_Wk, L1_attn_Wv, L1_attn_Wo, L1_attn_bank_weights, L1_attn_memories, L1_attn_memory_norms, L1_cond2_Wq, L1_cond2_Wk, L1_cond2_Wv, L1_cond2_Wo, L1_cond2_q_norm_scale, L1_cond2_k_norm_scale, L1_cond2_k_blocks, L1_cond2_v_blocks, L1_ffn_Wr, L1_ffn_bias, L1_ffn_Wg, L1_ffn_Wu, L1_ffn_Wd, L1_ffn_sWg, L1_ffn_sWu, L1_ffn_sWd):
    import jax
    import jax.numpy as jnp

    def _L0_cond_ref(x, conditions, weights):
        import jax, jax.numpy as jnp
        import numpy as np
        B, C, T = (128, 32, 256)
        S, D = (200, 32)
        w = weights[conditions]
        return jnp.einsum('bct,bcd->bdt', x, w)

    def _L0_attn_ref(X, ln_g, ln_b, Wq, bq, Wk, bk, Wv, bv, Wo, bo):
        import jax, jax.numpy as jnp
        import numpy as np
        D_MODEL = 256
        N_HEADS = 16
        D_HEAD = D_MODEL // N_HEADS
        B, S = (2, 256)
        EPS = 1e-05

        def _mhsa(X, ln_g, ln_b, Wq, bq, Wk, bk, Wv, bv, Wo, bo):
            n_ctx = X.shape[-2]
            mu = jnp.mean(X, axis=-1, keepdims=True)
            var = jnp.mean(jnp.square(X - mu), axis=-1, keepdims=True)
            Xn = (X - mu) * jax.lax.rsqrt(var + EPS) * ln_g + ln_b

            def split_heads(t):
                return t.reshape(t.shape[:-1] + (N_HEADS, D_HEAD)).swapaxes(-2, -3)
            Q = split_heads(Xn @ Wq + bq)
            K = split_heads(Xn @ Wk + bk)
            V = split_heads(Xn @ Wv + bv)
            scores = jnp.einsum('bhqd,bhkd->bhqk', Q, K) / jnp.sqrt(jnp.float32(D_HEAD))
            causal = jnp.tril(jnp.ones((n_ctx, n_ctx), dtype=bool))
            scores = jnp.where(causal, scores, jnp.float32(-jnp.inf))
            A = jax.nn.softmax(scores, axis=-1)
            AV = jnp.einsum('bhqk,bhkd->bhqd', A, V)
            AV = AV.swapaxes(-2, -3).reshape(X.shape[:-1] + (D_MODEL,))
            return AV @ Wo + bo
        return _mhsa(X, ln_g, ln_b, Wq, bq, Wk, bk, Wv, bv, Wo, bo)

    def _L0_cond2_ref(x, Wg, Wu, Wd, Ag, Bg, Au, Bu, Ad, Bd, adapter_indices):
        import jax, jax.numpy as jnp
        import numpy as np

        def _lora_linear(x, W, A, B, adapter_indices):
            base = jnp.einsum('bsd,df->bsf', x, W)
            Ai = A[adapter_indices]
            Bi = B[adapter_indices]
            lora = jnp.einsum('bsr,brf->bsf', jnp.einsum('bsd,bdr->bsr', x, Ai), Bi)
            return base + lora
        gate = _lora_linear(x, Wg, Ag, Bg, adapter_indices)
        up = _lora_linear(x, Wu, Au, Bu, adapter_indices)
        h = jax.nn.silu(gate) * up
        return _lora_linear(h, Wd, Ad, Bd, adapter_indices)

    def _L0_ffn_ref(x, w_gate, w_up, w_down):
        import jax, jax.numpy as jnp
        import numpy as np
        DIM_IN = 256
        DIM_HIDDEN = 1024
        gate = jnp.einsum('bsd,hd->bsh', x, w_gate)
        up = jnp.einsum('bsd,hd->bsh', x, w_up)
        gated = jax.nn.silu(gate) * up
        return jnp.einsum('bsh,dh->bsd', gated, w_down)

    def _L1_cond_ref(hidden_states, attention_precision, Wq, Wk, Wv, Wo):
        import jax, jax.numpy as jnp
        import numpy as np
        B, S, D_MODEL, NHEAD = (4, 256, 256, 16)
        HEAD_DIM = D_MODEL // NHEAD
        b, s, _ = hidden_states.shape

        def proj(x, W):
            y = jnp.einsum('bsd,ed->bse', x, W)
            return y.reshape(b, s, NHEAD, HEAD_DIM).transpose(0, 2, 1, 3)
        q = proj(hidden_states, Wq)
        k = proj(hidden_states, Wk)
        v = proj(hidden_states, Wv)
        beta = jnp.minimum(attention_precision, 4.0)[:, None]
        q = q * beta
        scores = jnp.einsum('bhqd,bhkd->bhqk', q, k) / np.sqrt(HEAD_DIM)
        causal = jnp.tril(jnp.ones((s, s), dtype=bool))
        scores = jnp.where(causal, scores, jnp.finfo(scores.dtype).min)
        attn = jax.nn.softmax(scores, axis=-1)
        out = jnp.einsum('bhqk,bhkd->bhqd', attn, v)
        out = out.transpose(0, 2, 1, 3).reshape(b, s, D_MODEL)
        return jnp.einsum('bsd,ed->bse', out, Wo)

    def _L1_attn_ref(hidden_states, Wq, Wk, Wv, Wo, bank_weights, memories, memory_norms):
        import jax, jax.numpy as jnp
        import numpy as np
        B, S, HID = (4, 512, 256)
        H, NB = (16, 4)
        D = HID // H
        EPS = 1e-06

        def elu_plus_one(x):
            return jax.nn.elu(x) + 1.0

        def _reference_tuple_inner(hidden_states, Wq, Wk, Wv, Wo, bank_weights, memories, memory_norms):
            b, s, _ = hidden_states.shape

            def proj(W):
                return (hidden_states @ W.T).reshape(b, s, H, D).transpose(0, 2, 1, 3)
            q, k, v = (proj(Wq), proj(Wk), proj(Wv))
            sigma_q = elu_plus_one(q)
            a_unnorm = jnp.einsum('bhsd,nhde->nbhse', sigma_q, memories)
            norm = jnp.einsum('bhsd,nhd->nbhs', sigma_q, memory_norms)
            a = a_unnorm / jnp.clip(norm, EPS, None)[..., None]
            active = (memory_norms.sum(axis=(1, 2)) >= EPS).astype(a.dtype)
            a = a * active[:, None, None, None, None]
            weights = jax.nn.softmax(bank_weights, axis=-1)
            combined = jnp.einsum('nbhse,hn->bhse', a, weights)
            sigma_k = elu_plus_one(k)
            mem0, norm0 = (memories[0], memory_norms[0])
            retr = jnp.einsum('bhsd,hde->bhse', sigma_k, mem0)
            knorm = jnp.clip(jnp.einsum('bhsd,hd->bhs', sigma_k, norm0), EPS, None)
            delta_v = v - retr / knorm[..., None]
            mem_update = jnp.einsum('bhsd,bhse->hde', sigma_k, delta_v) / (b * s)
            new_mem0 = jax.lax.stop_gradient(mem0 + mem_update)
            new_norm0 = jax.lax.stop_gradient(norm0 + sigma_k.sum(axis=(0, 2)) / b)
            out = combined.transpose(0, 2, 1, 3).reshape(b, s, HID) @ Wo.T
            return (out, new_mem0, new_norm0)
        return _reference_tuple_inner(hidden_states, Wq, Wk, Wv, Wo, bank_weights, memories, memory_norms)[0]

    def _L1_cond2_ref(x, Wq, Wk, Wv, Wo, q_norm_scale, k_norm_scale, k_blocks, v_blocks, block_tables, kv_lens):
        import jax, jax.numpy as jnp
        import numpy as np
        H, G, HD = (8, 4, 32)
        GSZ = H // G
        BLOCK = 16
        WINDOW = 128
        SCALE = 256.0 ** (-0.5)
        EPS = 1e-06
        THETA = 10000.0
        B, T, D = (16, 4, 256)
        NBLK = 257

        def _rms(x, scale):
            var = jnp.mean(x * x, axis=-1, keepdims=True)
            return x * jax.lax.rsqrt(var + EPS) * (1.0 + scale)

        def _rope(x, pos):
            half = HD // 2
            inv = 1.0 / THETA ** (jnp.arange(half, dtype=jnp.float32) / half)
            ang = pos[:, :, None].astype(jnp.float32) * inv
            cos = jnp.cos(ang)[:, None, :, :]
            sin = jnp.sin(ang)[:, None, :, :]
            x1, x2 = (x[..., :half], x[..., half:])
            return jnp.concatenate([x1 * cos - x2 * sin, x2 * cos + x1 * sin], axis=-1)
        Bx, Tx, _ = x.shape
        q = jnp.einsum('btd,od->bto', x, Wq).reshape(Bx, Tx, H, HD).transpose(0, 2, 1, 3)
        k = jnp.einsum('btd,od->bto', x, Wk).reshape(Bx, Tx, G, HD).transpose(0, 2, 1, 3)
        v = jnp.einsum('btd,od->bto', x, Wv).reshape(Bx, Tx, G, HD).transpose(0, 2, 1, 3)
        q = _rms(q, q_norm_scale)
        k = _rms(k, k_norm_scale)
        pos = kv_lens[:, None] + jnp.arange(Tx, dtype=jnp.int32)
        q = _rope(q, pos)
        k = _rope(k, pos)
        slot = pos // BLOCK
        off = pos % BLOCK
        blk = jnp.take_along_axis(block_tables, slot, axis=1)
        k_blocks = k_blocks.at[blk, :, off, :].set(k.transpose(0, 2, 1, 3))
        v_blocks = v_blocks.at[blk, :, off, :].set(v.transpose(0, 2, 1, 3))
        k_all = k_blocks[block_tables].transpose(0, 2, 1, 3, 4).reshape(Bx, G, -1, HD)
        v_all = v_blocks[block_tables].transpose(0, 2, 1, 3, 4).reshape(Bx, G, -1, HD)
        S = k_all.shape[2]
        qg = q.reshape(Bx, G, GSZ, Tx, HD)
        scores = jnp.einsum('bghtd,bgsd->bghts', qg, k_all) * SCALE
        kpos = jnp.arange(S, dtype=jnp.int32)
        allowed = (kpos[None, None, :] <= pos[:, :, None]) & (kpos[None, None, :] > pos[:, :, None] - WINDOW)
        scores = jnp.where(allowed[:, None, None, :, :], scores, -jnp.inf)
        p = jax.nn.softmax(scores, axis=-1)
        o = jnp.einsum('bghts,bgsd->bghtd', p, v_all).reshape(Bx, H, Tx, HD)
        o = o.transpose(0, 2, 1, 3).reshape(Bx, Tx, H * HD)
        return jnp.einsum('bto,do->btd', o, Wo)

    def _L1_ffn_ref(x, Wr, bias, Wg, Wu, Wd, sWg, sWu, sWd):
        import jax, jax.numpy as jnp
        import numpy as np
        TOPK = 2
        NORM_TOPK = True
        SCALE = 1.0
        EPS = 1e-09
        b, s, h = x.shape
        E = Wr.shape[0]
        xt = x.reshape(b * s, h)
        logits = xt @ Wr.T + bias
        probs = jax.nn.softmax(logits, axis=-1)
        topk_val, topk_idx = jax.lax.top_k(probs, TOPK)
        if NORM_TOPK:
            w = topk_val / (jnp.sum(topk_val, axis=-1, keepdims=True) + EPS)
        else:
            w = topk_val
        w = w * SCALE
        g = jnp.einsum('th,ehi->tei', xt, Wg)
        u = jnp.einsum('th,ehi->tei', xt, Wu)
        y = jnp.einsum('tei,eih->teh', jax.nn.silu(g) * u, Wd)
        oh = jax.nn.one_hot(topk_idx, E, dtype=x.dtype)
        routed = jnp.einsum('tke,tk,teh->th', oh, w, y)
        shared = jax.nn.silu(xt @ sWg) * (xt @ sWu) @ sWd
        return (routed + shared).reshape(b, s, h)
    x = x + _L0_attn_ref(_L0_cond_ref(x, itok_B_1_198, L0_cond_weights), L0_attn_ln_g, L0_attn_ln_b, L0_attn_Wq, L0_attn_bq, L0_attn_Wk, L0_attn_bk, L0_attn_Wv, L0_attn_bv, L0_attn_Wo, L0_attn_bo)
    x = x + _L0_ffn_ref(_L0_cond2_ref(x, L0_cond2_Wg, L0_cond2_Wu, L0_cond2_Wd, L0_cond2_Ag, L0_cond2_Bg, L0_cond2_Au, L0_cond2_Bu, L0_cond2_Ad, L0_cond2_Bd, itok_B_0_7), L0_ffn_w_gate, L0_ffn_w_up, L0_ffn_w_down)
    x = x + _L1_attn_ref(_L1_cond_ref(x, cond_1[:, None, :], L1_cond_Wq, L1_cond_Wk, L1_cond_Wv, L1_cond_Wo), L1_attn_Wq, L1_attn_Wk, L1_attn_Wv, L1_attn_Wo, L1_attn_bank_weights, L1_attn_memories, L1_attn_memory_norms)
    x = x + _L1_ffn_ref(_L1_cond2_ref(x, L1_cond2_Wq, L1_cond2_Wk, L1_cond2_Wv, L1_cond2_Wo, L1_cond2_q_norm_scale, L1_cond2_k_norm_scale, L1_cond2_k_blocks, L1_cond2_v_blocks, itok_Bx257_0_4111, itok_B_37_3939), L1_ffn_Wr, L1_ffn_bias, L1_ffn_Wg, L1_ffn_Wu, L1_ffn_Wd, L1_ffn_sWg, L1_ffn_sWu, L1_ffn_sWd)
    return x

_drawn_inputs = setup_inputs


def setup_inputs(seed=0):
    import zlib

    import numpy as np

    out = dict(_drawn_inputs(seed))
    spreads = {'L0_attn_ln_g': (1.0, 0.2),
     'L0_attn_ln_b': (0.0, 0.1),
     'L0_cond2_Bg': (0.009999999776482582, 0.2),
     'L0_cond2_Bu': (0.009999999776482582, 0.2),
     'L0_cond2_Bd': (0.009999999776482582, 0.2),
     'L1_ffn_bias': (0.0, 0.1)}
    factors = {}
    for name, (base, spread) in spreads.items():
        noise = np.random.default_rng([zlib.crc32(name.encode()), seed]).standard_normal(out[name].shape)
        drawn = base * np.exp(spread * noise) if base else spread * noise
        out[name] = jnp.asarray(drawn.astype(out[name].dtype))
    for name, factor in factors.items():
        out[name] = (out[name] * factor).astype(out[name].dtype)
    return out
```

```python
from contextlib import ExitStack

import numpy as np

import concourse.bass as bass
from concourse import mybir

F32 = mybir.dt.float32
I32 = mybir.dt.int32
U32 = mybir.dt.uint32
ALU = mybir.AluOpType
ACT = mybir.ActivationFunctionType
AXX = mybir.AxisListType.X

P = 128
B, S, D = 32, 32, 256
T = B * S
KC = D // P
NT = T // P
HALF = T // 2
NH, HD = 16, 16
HID = 1024
NAD, RANK = 8, 16
NBANK = 4
NE = 16
GRP, PHD = 4, 32
BLK, WIN, NSLOT = 16, 128, 257
NKEY = WIN + S
NU = (NKEY + BLK - 1) // BLK + 1
KVROWS = 16 * NSLOT * BLK
NGT = B + B * S // P
NWR = 4
NEG = -1.0e30
BIG = float(2 ** 17)
STEP = float(2 ** 100)
PI = float(np.pi)


def constants():
    p = np.arange(P)
    c = {}
    c["ident"] = np.eye(P, dtype=np.float32)
    m = np.where(np.arange(S)[None, :] > (p % S)[:, None], NEG, 0.0).astype(np.float32)
    c["causal"] = np.tile(m, (1, NH))
    c["parity"] = ((p[:, None] // HD) % 2 == np.arange(2)[None, :]).astype(np.float32)
    c["adapter"] = (p[:, None] // RANK).astype(np.float32)
    c["quad"] = (p[:, None] // 32 == np.arange(4)[None, :]).astype(np.float32)
    j = np.arange(NKEY)[None, :]
    t = (p % S)[:, None]
    c["band"] = np.where((j >= t) & (j <= t + WIN - 1), 0.0, NEG).astype(np.float32)
    c["jstep"] = np.broadcast_to(j.astype(np.float32) * np.float32(STEP), (P, NKEY))
    c["tok"] = t.astype(np.float32)
    half = PHD // 2
    inv = np.float32(1.0) / np.float32(10000.0) ** (np.arange(half, dtype=np.float32) / np.float32(half))
    c["inv"] = np.broadcast_to(inv.astype(np.float32)[None, :], (P, half))
    c["ones"] = np.ones((P, P), np.float32)
    c["e16"] = np.broadcast_to(np.arange(NE, dtype=np.float32)[None, :], (P, NE))
    sel = np.zeros((P, NBANK, KC, P), np.float32)
    for n in range(NBANK):
        for h in range(NH):
            cc, r = divmod(h * HD, P)
            sel[n * NH + h, n, cc, r:r + HD] = 1.0
    c["slots"] = np.broadcast_to(np.arange(NSLOT, dtype=np.float32)[None, :], (P, NSLOT))
    c["jnum"] = np.broadcast_to(j.astype(np.float32), (P, NKEY))
    c["unum"] = np.broadcast_to(np.arange(NU, dtype=np.float32)[None, :], (P, NU))
    c["seqeq"] = (p[:, None] == np.arange(B)[None, :]).astype(np.float32)
    c["seqmod"] = (p[:, None] % 4 == np.arange(4)[None, :]).astype(np.float32)
    c["seqdiv"] = (p[:, None] // 4 == np.arange(B // 4)[None, :]).astype(np.float32)
    c["seq32"] = (p[:, None] * 32).astype(np.float32)
    c["wslot"] = np.broadcast_to((16.0 * np.arange(NU - NWR, NU)).astype(np.float32)[None, :], (P, NWR))
    c["sel"] = sel.reshape(P, NBANK * KC * P)
    return c


def chunks(w):
    k = w.shape[0] // P
    return w.reshape(k, P, -1).transpose(1, 0, 2).reshape(P, -1)


def rows(v):
    return np.broadcast_to(v.reshape(1, -1), (P, v.size))


def layout(i):
    f = {}
    x = i["x"]
    f["x_tok"] = chunks(x.reshape(T, D))
    f["x_feat"] = chunks(x.reshape(T, D).T)
    f["mix_table"] = i["L0_cond_weights"].reshape(-1, 32)
    small = dict(constants())
    small["ln_g"], small["ln_b"] = chunks(i["L0_attn_ln_g"][:, None]), chunks(i["L0_attn_ln_b"][:, None])
    for n in ("bq", "bk", "bo"):
        small[n] = chunks(i["L0_attn_" + n][:, None])
    small["bv"] = rows(i["L0_attn_bv"])
    small["temp"] = np.repeat(i["cond_1"].reshape(B // 4, 4), 32, axis=1).T
    small["qscale"], small["kscale"] = rows(i["L1_cond2_q_norm_scale"]), rows(i["L1_cond2_k_norm_scale"])
    small["rbias"] = rows(i["L1_ffn_bias"])
    bw = i["L1_attn_bank_weights"]
    z = np.zeros((P, NBANK), np.float32)
    z[:64] = np.tile(bw, (NBANK, 1))
    small["bw_all"] = z
    z = np.zeros((P, 1), np.float32)
    z[:64, 0] = bw.T.reshape(-1)
    small["bw_own"] = z
    nrm = i["L1_attn_memory_norms"]
    z = np.zeros((P, NH * HD), np.float32)
    z[:64] = np.repeat(nrm.reshape(NBANK, -1), NH, axis=0)
    small["norm_all"] = z
    at, cols = {}, []
    n = 0
    for k, v in small.items():
        at[k] = (n, n + v.shape[1])
        n += v.shape[1]
        cols.append(v)
    f["small"] = np.concatenate(cols, axis=1)
    ints = [np.repeat(i["itok_B_1_198"].reshape(B // 4, 4), 32, axis=1).T,
            np.repeat(i["itok_B_37_3939"].reshape(B // 4, 4), 32, axis=1).T,
            rows(i["itok_B_0_7"])]
    pad = np.zeros((P, 1 + B + NSLOT), i["itok_B_37_3939"].dtype)
    pad[:B, 0] = i["itok_B_37_3939"]
    pad[:, 1:1 + B] = rows(i["itok_B_37_3939"])
    pad[:B, 1 + B:] = i["itok_Bx257_0_4111"]
    chan = np.broadcast_to((np.arange(P) % 32)[:, None], (P, NT)).astype(pad.dtype)
    f["ints"] = np.concatenate(ints + [pad, chan], axis=1)
    f["wA"] = np.concatenate([chunks(i["L0_attn_" + n]) for n in ("Wq", "Wk", "Wv", "Wo")], axis=1)
    f["wB"] = np.concatenate([chunks(i["L1_cond_" + n].T) for n in ("Wq", "Wk", "Wv", "Wo")], axis=1)
    ad = i["L0_cond2_Ag"], i["L0_cond2_Au"], i["L0_cond2_Ad"]
    ag, au, adn = [chunks(a.transpose(1, 0, 2).reshape(a.shape[1], -1)) for a in ad]
    bg, bu, bd = [i["L0_cond2_" + n].reshape(NAD * RANK, -1) for n in ("Bg", "Bu", "Bd")]
    f["wF"] = np.concatenate([ag, au, chunks(i["L0_cond2_Wg"]), chunks(i["L0_cond2_Wu"]), bg, bu,
                              chunks(i["L0_cond2_Wd"]), adn, bd], axis=1)
    f["wG"] = np.concatenate([chunks(i["L0_ffn_w_gate"].T), chunks(i["L0_ffn_w_up"].T),
                              chunks(i["L0_ffn_w_down"].T)], axis=1)
    mem = i["L1_attn_memories"]
    bdm = np.zeros((P, NBANK, KC, P), np.float32)
    nrc = np.zeros((P, KC, NBANK * NH), np.float32)
    for h in range(NH):
        c, r = divmod(h * HD, P)
        bdm[r:r + HD, :, c, r:r + HD] = mem[:, h].transpose(1, 0, 2)
        nrc[r:r + HD, c, h::NH] = nrm[:, h].T
    f["wL"] = np.concatenate([chunks(i["L1_attn_Wq"].T), chunks(i["L1_attn_Wo"].T),
                              bdm.reshape(P, -1), nrc.reshape(P, -1)], axis=1)
    wq = i["L1_cond2_Wq"].reshape(GRP, 2, PHD, D).transpose(1, 0, 2, 3).reshape(D, D)
    wo = i["L1_cond2_Wo"].reshape(D, GRP, 2, PHD).transpose(0, 2, 1, 3).reshape(D, D)
    proj = np.concatenate([wq, i["L1_cond2_Wk"], i["L1_cond2_Wv"]], axis=0).T
    f["wP"] = np.concatenate([chunks(proj), chunks(wo.T)], axis=1)
    kv = [i["L1_cond2_" + n].transpose(0, 2, 1, 3).reshape(KVROWS, GRP * PHD) for n in ("k_blocks", "v_blocks")]
    f["cache"] = np.concatenate(kv, axis=1)
    gate = np.concatenate([i["L1_ffn_Wg"].transpose(1, 0, 2).reshape(D, -1), i["L1_ffn_sWg"]], axis=1)
    up = np.concatenate([i["L1_ffn_Wu"].transpose(1, 0, 2).reshape(D, -1), i["L1_ffn_sWu"]], axis=1)
    down = np.concatenate([i["L1_ffn_Wd"].reshape(-1, D), i["L1_ffn_sWd"]], axis=0)
    f["wR"] = chunks(i["L1_ffn_Wr"].T)
    f["wE"] = np.concatenate([chunks(gate), chunks(up), chunks(down)], axis=1)
    return f, at


def program(nc, small_at, x_tok_d, x_feat_d, mix_table, small_d, ints_d, wA_d, wB_d, wF_d, wG_d, wL_d, wP_d,
            cache, wR_d, wE_d, out):
    new_kv = nc.dram_tensor("new_kv", [T, 2 * P], F32).ap()
    route_d = nc.dram_tensor("route", [NE, T], F32).ap()

    with ExitStack() as ctx:
        sems = {}

        def sem(name):
            if name not in sems:
                sems[name] = ctx.enter_context(nc.semaphore(name))
            return sems[name]

        def sb(name, cols, dt=F32):
            return ctx.enter_context(nc.sbuf_tensor(name, [P, cols], dt))

        small = sb("small", small_d.shape[1])
        ints = sb("ints", ints_d.shape[1], I32)
        xT = sb("xT", KC * T)[:, :].rearrange("p (c t) -> p c t", c=KC)
        wbig = sb("wbig", wF_d.shape[1] + wG_d.shape[1])
        wmid = sb("wmid", wA_d.shape[1] + wB_d.shape[1] + wL_d.shape[1])
        wpage = wbig[:, wE_d.shape[1]:wE_d.shape[1] + wP_d.shape[1]]
        wrt = sb("wrt", wR_d.shape[1])
        work = sb("work", 21504)
        prep = sb("prep", 2048)
        prepi = sb("prepi", 640, I32)
        ps = ctx.enter_context(nc.psum_tensor("ps", [P, 8, 512], F32))

        def const(name):
            a, b = small_at[name]
            return small[:, a:b]

        def cut(t, at, n):
            return t[:, at:at + n]

        ident = const("ident")
        xnT = cut(work, 0, 2048).rearrange("p (c t) -> p c t", c=KC)
        attT = xnT
        yT = cut(work, 2048, 2048).rearrange("p (c t) -> p c t", c=KC)
        kpar = cut(work, 4096, 4096).rearrange("p (c a t) -> p c a t", c=KC, a=2)
        qT = cut(work, 8192, 2048).rearrange("p (c t) -> p c t", c=KC)
        scor = cut(work, 10240, 1536).rearrange("p (r x) -> p r x", r=3)
        prob = cut(work, 11776, 1536).rearrange("p (r x) -> p r x", r=3)
        vpar = cut(work, 13312, 4096).rearrange("p (g a h d) -> p g a h d", g=NT, a=2, h=8)
        pdiag = cut(work, 17408, 4096).rearrange("p (r h q) -> p r h q", r=2, h=NH)
        x_tok = cut(work, 4096, 2048).rearrange("p (g f) -> p g f", g=NT)
        xn_tok = cut(work, 6144, 2048).rearrange("p (g f) -> p g f", g=NT)
        mix_w = cut(work, 8192, 256).rearrange("p (g f) -> p g f", g=NT)

        at = [0]

        def small_buf(n):
            at[0] += n
            return cut(prep, at[0] - n, n)

        stats = small_buf(NT * 6).rearrange("p (g s) -> p g s", g=NT)
        meanvar = small_buf(NT * 2).rearrange("p (g s) -> p g s", g=NT)
        rstd = small_buf(NT)
        ati = [0]

        def int_buf(n):
            ati[0] += n
            return cut(prepi, ati[0] - n, n)

        mix_rows = int_buf(NT)
        admask = small_buf(B)
        temps = small_buf(NT)
        amax = small_buf(NT * NH).rearrange("p (g h) -> p g h", g=NT)
        asum = small_buf(NT * NH).rearrange("p (g h) -> p g h", g=NT)
        arec = small_buf(NT * NH).rearrange("p (g h) -> p g h", g=NT)
        cosb = small_buf(NT * 16).rearrange("p (g f) -> p g f", g=NT)
        sinb = small_buf(NT * 16).rearrange("p (g f) -> p g f", g=NT)
        key_row = small_buf(NGT)
        key_rowi = int_buf(NGT)
        new_row = small_buf(NGT)
        new_rowi = int_buf(NGT)
        thr = small_buf(B)
        coef = small_buf(1)
        rms = small_buf(NT * 12)
        ang = small_buf(NT * 16)
        angk = small_buf(NT * 16)
        angc = small_buf(NT * 16)
        tokpos = small_buf(NT)

        gated = cut(work, 4096, 1024).rearrange("p (r x) -> p r x", r=2)
        hid = cut(work, 5120, 1536).rearrange("p (r x) -> p r x", r=3)
        zlow = cut(work, 6656, 2048).rearrange("p (m t) -> p m t", m=2)
        zdown = cut(work, 8704, 512)
        rawact = cut(work, 6656, 1024).rearrange("p (r x) -> p r x", r=2)
        share = cut(work, 7680, 2048).rearrange("p (r x) -> p r x", r=4)
        class Attention:

            def __init__(self, tag, inp, w_at, in_ready, load, biased, out_to):
                self.tag, self.inp, self.in_ready, self.load, self.biased, self.out_to = (
                    tag, inp, in_ready, load, biased, out_to)
                w = cut(wmid, w_at, 2048).rearrange("p (m c o) -> p m c o", m=4, c=KC)
                self.wq, self.wk, self.wv, self.wo = [w[:, m] for m in range(4)]

            def s(self, name):
                return sem(self.tag + "_" + name)

            def tensor(self, pe):
                s, inp = self.s, self.inp
                pe.wait_ge(sem(self.load), 16)
                pe.wait_ge(sem(self.in_ready[0]), self.in_ready[1])
                for c in range(KC):
                    for n in range(2):
                        for k in range(KC):
                            mm = nc.tensor.matmul(ps[:, 2 * c + n, :], self.wk[:, k, c * P:(c + 1) * P],
                                                  inp[:, k, n * HALF:(n + 1) * HALF], start=(k == 0), stop=(k == KC - 1))
                        mm.then_inc(s("k_done"), 1)
                for c in range(KC):
                    for n in range(2):
                        for k in range(KC):
                            mm = nc.tensor.matmul(ps[:, 4 + 2 * c + n, :], self.wq[:, k, c * P:(c + 1) * P],
                                                  inp[:, k, n * HALF:(n + 1) * HALF], start=(k == 0), stop=(k == KC - 1))
                        mm.then_inc(s("q_done"), 1)
                for g in range(NT):
                    if g % 2 == 0:
                        pe.wait_ge(s("k_kept"), 2 * (g // 2) + 2)
                    for k in range(KC):
                        mm = nc.tensor.matmul(ps[:, g // 2, (g % 2) * D:(g % 2 + 1) * D], inp[:, k, g * P:(g + 1) * P],
                                              self.wv[:, k, :], start=(k == 0), stop=(k == KC - 1))
                    if g % 2:
                        mm.then_inc(s("v_done"), 1)
                for hf in range(2):
                    pe.wait_ge(s("q_kept"), 4)
                    pe.wait_ge(s("k_kept"), 8)
                    if hf:
                        pe.wait_ge(s("v_kept"), 8)
                    for g4 in range(4):
                        for c in range(KC):
                            for pr in range(4):
                                for j in range(4):
                                    t0 = (4 * (4 * hf + g4) + j) * S
                                    mm = nc.tensor.matmul(
                                        ps[32 * j:32 * j + 32, 4 * (1 - hf) + pr, (2 * g4 + c) * 64:(2 * g4 + c + 1) * 64],
                                        qT[32 * pr:32 * pr + 32, c, t0:t0 + S], kpar[32 * pr:32 * pr + 32, c, :, t0:t0 + S],
                                        start=True, stop=True)
                    mm.then_inc(s("scores_done"), 1)
                for g in range(NT):
                    pe.wait_ge(s("p_ready"), 4 * (g + 1))
                    if g == 0:
                        pe.wait_ge(s("scaled"), 4)
                        pe.wait_ge(s("v_kept"), 8)
                    if g >= 4:
                        pe.wait_ge(s("o_kept"), g - 3)
                    for c in range(KC):
                        for pr in range(4):
                            for a in range(2):
                                mm = nc.tensor.matmul(ps[32 * pr:32 * pr + 32, 4 + g % 4, c * P:(c + 1) * P],
                                                      vpar[:, g, a, 4 * c + pr, :], pdiag[:, g % 2, 4 * pr + 2 * c + a, :],
                                                      start=(a == 0), stop=(a == 1))
                    mm.then_inc(s("pv_done"), 1)
                pe.wait_ge(s("o_kept"), NT)
                for c in range(KC):
                    for n in range(2):
                        for k in range(KC):
                            mm = nc.tensor.matmul(ps[:, 2 * c + n, :], self.wo[:, k, c * P:(c + 1) * P],
                                                  attT[:, k, n * HALF:(n + 1) * HALF], start=(k == 0), stop=(k == KC - 1))
                        mm.then_inc(s("proj_done"), 1)

            def vector(self, dve):
                s = self.s
                for c in range(KC):
                    for n in range(2):
                        dve.wait_ge(s("k_done"), 2 * c + n + 1)
                        for a in range(2):
                            o = kpar[:, c, a, n * HALF:(n + 1) * HALF]
                            par = const("parity")[:, a:a + 1]
                            if self.biased:
                                nc.vector.tensor_scalar(o, ps[:, 2 * c + n, :], const("bk")[:, c:c + 1], par,
                                                        ALU.add, ALU.mult).then_inc(s("k_kept"), 1)
                            else:
                                nc.vector.tensor_scalar(o, ps[:, 2 * c + n, :], par, None, ALU.mult).then_inc(s("k_kept"), 1)
                dve.wait_ge(sem("zeroed"), 2)
                for i in range(4):
                    dve.wait_ge(s("v_done"), i + 1)
                    v = ps[:, i, :].rearrange("p (g h a d) -> p g h a d", g=2, h=8, a=2)
                    bv = const("bv").rearrange("p (h a d) -> p h a d", h=8, a=2)
                    for a in range(2):
                        if self.biased:
                            for g in range(2):
                                ins = nc.vector.tensor_tensor(vpar[:, 2 * i + g, a, :, a * HD:(a + 1) * HD],
                                                              v[:, g, :, a, :], bv[:, :, a, :], ALU.add)
                            ins.then_inc(s("v_kept"), 1)
                        else:
                            nc.vector.tensor_copy(vpar[:, 2 * i:2 * i + 2, a, :, a * HD:(a + 1) * HD],
                                                  v[:, :, :, a, :]).then_inc(s("v_kept"), 1)

                def up_to_exponent(g):
                    hf, g4, r = g // 4, g % 4, g % 3
                    dve.wait_ge(s("scores_done"), hf + 1)
                    if g >= 3:
                        dve.wait_ge(s("exp_done"), g - 2)
                    scale = 0.25 if self.biased else temps[:, g:g + 1]
                    o = scor[:, r, :].rearrange("p (b x) -> p b x", b=4)
                    nc.vector.scalar_tensor_tensor(o, ps[:, 4 * (1 - hf):4 * (1 - hf) + 4, g4 * P:(g4 + 1) * P], scale,
                                                   const("causal").rearrange("p (b x) -> p b x", b=4),
                                                   ALU.mult, ALU.add).then_inc(s("scaled"), 1)
                    dve.wait_ge(s("scaled"), g + 1)
                    sc = scor[:, r, :].rearrange("p (h k) -> p h k", h=NH)
                    nc.vector.tensor_reduce(amax[:, g, :], sc, AXX, ALU.max).then_inc(s("max_done"), 1)
                    dve.wait_ge(s("max_done"), g + 1)
                    nc.vector.tensor_tensor(sc, sc, amax[:, g, :].unsqueeze(2).to_broadcast([P, NH, S]),
                                            ALU.subtract).then_inc(s("shifted"), 1)

                def from_exponent(g):
                    r = g % 3
                    dve.wait_ge(s("exp_done"), g + 1)
                    pr = prob[:, r, :].rearrange("p (h k) -> p h k", h=NH)
                    nc.vector.tensor_reduce(asum[:, g, :], pr, AXX, ALU.add).then_inc(s("sum_done"), 1)
                    dve.wait_ge(s("sum_done"), g + 1)
                    nc.vector.reciprocal(arec[:, g, :], asum[:, g, :]).then_inc(s("rec_done"), 1)
                    dve.wait_ge(s("rec_done"), g + 1)
                    nc.vector.tensor_tensor(pr, pr, arec[:, g, :].unsqueeze(2).to_broadcast([P, NH, S]),
                                            ALU.mult).then_inc(s("normed"), 1)
                    dve.wait_ge(s("normed"), g + 1)
                    if g >= 2:
                        dve.wait_ge(s("pv_done"), g - 1)
                    for j in range(4):
                        q = slice(32 * j, 32 * j + 32)
                        nc.vector.transpose(pdiag[q, g % 2, :, q], pr[q]).then_inc(s("p_ready"), 1)

                for g in range(NT + 1):
                    if g < NT:
                        up_to_exponent(g)
                    if g >= 1:
                        from_exponent(g - 1)
                for c in range(KC):
                    for n in range(2):
                        dve.wait_ge(s("proj_done"), 2 * c + n + 1)
                        to = self.out_to[:, c, n * HALF:(n + 1) * HALF]
                        if self.biased:
                            if c == 0 and n == 0:
                                dve.wait_ge(sem("ld_x_feat"), 16)
                            nc.vector.scalar_tensor_tensor(to, ps[:, 2 * c + n, :], const("bo")[:, c:c + 1], to,
                                                           ALU.add, ALU.add).then_inc(s("out"), 1)
                        else:
                            nc.vector.tensor_copy(to, ps[:, 2 * c + n, :]).then_inc(s("out"), 1)

            def scalar(self, act):
                s = self.s
                for c in range(KC):
                    for n in range(2):
                        act.wait_ge(s("q_done"), 2 * c + n + 1)
                        bias = const("bq")[:, c:c + 1] if self.biased else 0.0
                        nc.scalar.activation(qT[:, c, n * HALF:(n + 1) * HALF], ps[:, 4 + 2 * c + n, :], ACT.Identity,
                                             bias=bias).then_inc(s("q_kept"), 1)

                def keep_output(g):
                    act.wait_ge(s("pv_done"), g + 1)
                    nc.scalar.activation(attT[:, :, g * P:(g + 1) * P],
                                         ps[:, 4 + g % 4, 0:D].rearrange("p (c t) -> p c t", c=KC),
                                         ACT.Copy).then_inc(s("o_kept"), 1)

                for g in range(NT):
                    act.wait_ge(s("shifted"), g + 1)
                    if g >= 3:
                        act.wait_ge(s("p_ready"), 4 * (g - 2))
                    nc.scalar.activation(prob[:, g % 3, :], scor[:, g % 3, :], ACT.Exp).then_inc(s("exp_done"), 1)
                    if g >= 2:
                        keep_output(g - 2)
                keep_output(NT - 2)
                keep_output(NT - 1)

        class Gated:

            def __init__(self, tag, inp, gate, up, down, nj, in_ready, load, lora=None, routed=0, add=True,
                         out_to=None, extra_tensor=None, extra_vector=None, extra_scalar=None):
                self.tag, self.inp, self.gate, self.up, self.down, self.nj = tag, inp, gate, up, down, nj
                self.in_ready, self.load, self.lora, self.routed = in_ready, load, lora, routed
                self.add, self.out_to = add, out_to
                self.extra_tensor, self.extra_vector, self.extra_scalar = extra_tensor, extra_vector, extra_scalar
                self.units = [(n, j) for n in range(2) for j in range(nj)]

            def s(self, name):
                return sem(self.tag + "_" + name)

            def acc(self, n, oc):
                return ps[:, oc if self.lora else 2 * n + oc, :]

            def tensor(self, pe):
                s, inp = self.s, self.inp
                pe.wait_ge(sem(self.load), 16)
                pe.wait_ge(sem(self.in_ready[0]), self.in_ready[1])
                if self.lora:
                    for m in range(2):
                        for n in range(2):
                            for k in range(KC):
                                mm = nc.tensor.matmul(ps[:, 4 + 2 * m + n, :], self.lora["first"][m][:, k, :],
                                                      inp[:, k, n * HALF:(n + 1) * HALF], start=(k == 0), stop=(k == KC - 1))
                            mm.then_inc(s("z_done"), 1)

                def down(i):
                    n, j = self.units[i]
                    pe.wait_ge(s("h_ready"), i + 1)
                    if j == 0 and n == 1:
                        if self.lora:
                            pe.wait_ge(s("out"), 2)
                        elif self.extra_tensor:
                            pe.wait_ge(sem("route_kept"), 2)
                    last = j == self.nj - 1
                    h = hid[:, i % 3, :]
                    for oc in range(KC):
                        mm = nc.tensor.matmul(self.acc(n, oc), self.down[:, j, oc * P:(oc + 1) * P], h,
                                              start=(j == 0), stop=(last and not self.lora))
                    if self.lora:
                        mm = nc.tensor.matmul(ps[:, 2, :], self.lora["down_first"][:, j, :], h, start=(j == 0), stop=last)
                    mm.then_inc(s("down_done"), 1)
                    if self.lora and last:
                        pe.wait_ge(s("zd_ready"), n + 1)
                        for oc in range(KC):
                            mm = nc.tensor.matmul(self.acc(n, oc), self.lora["down_second"][:, oc * P:(oc + 1) * P],
                                                  zdown[:, :], start=False, stop=True)
                        mm.then_inc(s("sum_done"), 1)

                for i, (n, j) in enumerate(self.units):
                    if self.lora and i == 0:
                        pe.wait_ge(s("z_ready"), 4)
                    if i >= 2:
                        pe.wait_ge(s("h_ready"), i - 1)
                    for m, w in enumerate((self.gate, self.up)):
                        o = ps[:, 4 + 2 * (i % 2) + m, :]
                        for k in range(KC):
                            mm = nc.tensor.matmul(o, w[:, k, j * P:(j + 1) * P], inp[:, k, n * HALF:(n + 1) * HALF],
                                                  start=(k == 0), stop=(k == KC - 1 and not self.lora))
                        if self.lora:
                            mm = nc.tensor.matmul(o, self.lora["second"][m][:, j * P:(j + 1) * P],
                                                  zlow[:, m, n * HALF:(n + 1) * HALF], start=False, stop=True)
                        mm.then_inc(s("gate_done" if m == 0 else "up_done"), 1)
                    if self.extra_tensor:
                        self.extra_tensor(pe, i)
                    if i >= 1:
                        down(i - 1)
                down(len(self.units) - 1)

            def vector(self, dve):
                s = self.s
                if self.lora:
                    for m in range(2):
                        for n in range(2):
                            dve.wait_ge(s("z_done"), 2 * m + n + 1)
                            nc.vector.tensor_tensor(
                                zlow[:, m, n * HALF:(n + 1) * HALF].rearrange("p (b t) -> p b t", t=S),
                                ps[:, 4 + 2 * m + n, :].rearrange("p (b t) -> p b t", t=S),
                                admask[:, 16 * n:16 * n + 16].unsqueeze(2).to_broadcast([P, 16, S]),
                                ALU.mult).then_inc(s("z_ready"), 1)
                for i, (n, j) in enumerate(self.units):
                    dve.wait_ge(s("up_done"), i + 1)
                    dve.wait_ge(s("act_ready"), i + 1)
                    if i >= 3:
                        dve.wait_ge(s("down_done"), i - 2)
                    src = gated[:, i % 2, :]
                    nc.vector.tensor_tensor(hid[:, i % 3, :], ps[:, 5 + 2 * (i % 2), :], src, ALU.mult).then_inc(s("h_ready"), 1)
                    if self.extra_vector:
                        self.extra_vector(dve, i)
                    if self.lora and j == self.nj - 1:
                        dve.wait_ge(s("down_done"), i + 1)
                        nc.vector.tensor_tensor(zdown[:, :].rearrange("p (b t) -> p b t", t=S),
                                                ps[:, 2, :].rearrange("p (b t) -> p b t", t=S),
                                                admask[:, 16 * n:16 * n + 16].unsqueeze(2).to_broadcast([P, 16, S]),
                                                ALU.mult).then_inc(s("zd_ready"), 1)
                    if j == self.nj - 1:
                        if self.lora:
                            dve.wait_ge(s("sum_done"), n + 1)
                        else:
                            dve.wait_ge(s("down_done"), i + 1)
                        for oc in range(KC):
                            to = self.out_to[:, oc, n * HALF:(n + 1) * HALF]
                            if self.add:
                                nc.vector.tensor_tensor(to, self.acc(n, oc), to, ALU.add).then_inc(s("out"), 1)
                            else:
                                nc.vector.tensor_copy(to, self.acc(n, oc)).then_inc(s("out"), 1)

            def scalar(self, act):
                s = self.s
                for i, (n, j) in enumerate(self.units):
                    act.wait_ge(s("gate_done"), i + 1)
                    if i >= 2:
                        act.wait_ge(s("h_ready"), i - 1)
                    dst = rawact[:, i % 2, :] if self.routed else gated[:, i % 2, :]
                    nc.scalar.activation(dst, ps[:, 4 + 2 * (i % 2), :], ACT.Silu).then_inc(
                        s("raw_ready" if self.routed else "act_ready"), 1)
                    if self.extra_scalar:
                        self.extra_scalar(act, i)

            def gpsimd(self, pool):
                s = self.s
                for i, (n, j) in enumerate(self.units):
                    pool.wait_ge(s("raw_ready"), i + 1)
                    if i >= 2:
                        pool.wait_ge(s("h_ready"), i - 1)
                    if j < self.routed:
                        r = n * self.routed + j
                        pool.wait_ge(sem(f"share{r % 4}"), 16 * (r // 4 + 1))
                        nc.gpsimd.tensor_tensor(gated[:, i % 2, :], rawact[:, i % 2, :], share[:, r % 4, :],
                                                ALU.mult).then_inc(s("act_ready"), 1)
                    else:
                        nc.gpsimd.tensor_copy(gated[:, i % 2, :], rawact[:, i % 2, :]).then_inc(s("act_ready"), 1)

        tmp_at = [9216]

        def tmp(n, rows=B):
            tmp_at[0] += n
            return work[0:rows, tmp_at[0] - n:tmp_at[0]]

        tab, first, tw, ulen, base, rr = tmp(NSLOT), tmp(NU), tmp(NU), tmp(1), tmp(1), tmp(1)
        upos, ublk, uoff, krow = tmp(NKEY), tmp(NKEY), tmp(NKEY), tmp(NKEY)
        eq_at = tmp_at[0]
        eq = tmp(NU * NKEY).rearrange("p (s j) -> p s j", s=NU)
        last32 = tmp(P).rearrange("p (q j) -> p q j", q=4)
        spread = tmp(3 * B * NWR).rearrange("p (k b s) -> p k b s", k=3, b=B)
        t0w, b16, wlo, whi, wval, wtm = tmp(NWR), tmp(NWR), tmp(NWR), tmp(NWR), tmp(NWR), tmp(NWR)
        writer = tmp(3 * B * NWR, P).rearrange("p (k x) -> p k x", k=3)
        wbest = tmp(NGT, P)
        wneg = tmp(NGT, P)
        WT = 5
        m1 = work[:, eq_at:eq_at + WT * B * NWR].rearrange("p (i x) -> p i x", i=WT)
        m2 = work[:, eq_at + WT * B * NWR:eq_at + 2 * WT * B * NWR].rearrange("p (i x) -> p i x", i=WT)
        assert tmp_at[0] <= 13312 and 2 * WT * B * NWR <= NU * NKEY
        basei, uposi, ublki = int_buf(2), int_buf(NKEY), int_buf(NKEY)
        len_b = ints[0:B, 16 + B:17 + B]
        tab_b = ints[0:B, 17 + 2 * B:17 + 2 * B + NSLOT]

        def row(name, n=None):
            c = const(name)[0:B, :]
            return c if n is None else c[:, 0:n]

        def prep_steps(dve):
            ts, tt, stt = nc.vector.tensor_scalar, nc.vector.tensor_tensor, nc.vector.scalar_tensor_tensor

            yield lambda: ts(ulen, len_b, float(1 - WIN), None, ALU.add)
            yield lambda: ts(basei[0:B, 0:1], len_b, float(1 - WIN), None, ALU.add)
            yield lambda: ts(basei[0:B, 1:2], basei[0:B, 0:1], 4, None, ALU.arith_shift_right)
            yield lambda: nc.vector.tensor_copy(base, basei[0:B, 1:2])
            yield lambda: stt(rr, base, -16.0, ulen, ALU.mult, ALU.add)
            yield lambda: nc.vector.tensor_copy(tab, tab_b)
            yield lambda: ts(first, row("unum"), base, 0.0, ALU.add, ALU.max)
            yield lambda: ts(first, first, float(NSLOT - 1), None, ALU.min)
            for u in range(NU):
                yield lambda u=u: stt(eq[:, 0:2, :].rearrange("p a b -> p (a b)")[:, 0:NSLOT], row("slots"),
                                      first[:, u:u + 1], tab, ALU.is_equal, ALU.mult, accum_out=tw[:, u:u + 1])
            yield lambda: ts(upos, row("jnum"), rr, None, ALU.add)
            yield lambda: nc.vector.tensor_copy(uposi[0:B], upos)
            yield lambda: ts(ublki[0:B], uposi[0:B], 4, None, ALU.arith_shift_right)
            yield lambda: nc.vector.tensor_copy(ublk, ublki[0:B])
            yield lambda: stt(uoff, ublk, -16.0, upos, ALU.mult, ALU.add)
            yield lambda: tt(eq, ublk.unsqueeze(1).to_broadcast([B, NU, NKEY]),
                             row("unum").unsqueeze(2).to_broadcast([B, NU, NKEY]), ALU.is_equal)
            yield lambda: tt(eq, eq, tw.unsqueeze(2).to_broadcast([B, NU, NKEY]), ALU.mult)
            yield lambda: nc.vector.tensor_reduce(krow, eq.rearrange("p s j -> p j s"), AXX, ALU.add)
            yield lambda: stt(krow, krow, 16.0, uoff, ALU.mult, ALU.add)
            yield lambda: ts(t0w, row("wslot"), rr, float(1 - WIN), ALU.subtract, ALU.add)
            yield lambda: ts(b16, tw[:, NU - NWR:NU], 16.0, None, ALU.mult)
            yield lambda: ts(wtm, t0w, -1.0, 0.0, ALU.mult, ALU.max)
            yield lambda: tt(wlo, b16, wtm, ALU.add)
            yield lambda: ts(wtm, t0w, -1.0, float(S - 1), ALU.mult, ALU.add)
            yield lambda: ts(wtm, wtm, float(BLK - 1), None, ALU.min)
            yield lambda: tt(whi, b16, wtm, ALU.add)
            yield lambda: ts(wval, t0w, row("seq32", 1), 1.0 + BIG, ALU.add, ALU.add)
            yield lambda: tt(wval, wval, b16, ALU.subtract)
            for k, v in enumerate((wlo, whi, wval)):
                yield lambda k=k, v=v: tt(spread[:, k], v.unsqueeze(1).to_broadcast([B, B, NWR]),
                                          row("seqeq").unsqueeze(2).to_broadcast([B, B, NWR]), ALU.mult)
            yield lambda: tt(last32, krow[:, P:NKEY].unsqueeze(1).to_broadcast([B, 4, S]),
                             row("seqmod").unsqueeze(2).to_broadcast([B, 4, S]), ALU.mult)

            def from_tensor():
                dve.wait_ge(sem("prep_spread"), 1)
                return nc.vector.tensor_copy(key_row, ps[:, 3, 0:NGT])
            yield from_tensor
            yield lambda: nc.vector.tensor_copy(writer, ps[:, 3, 64:64 + 3 * B * NWR].rearrange("p (k x) -> p k x", k=3))
            yield lambda: nc.vector.tensor_copy(key_rowi, key_row)
            for i in range(0, NGT, WT):
                shape = [P, WT, B * NWR]
                keys = key_row[:, i:i + WT].unsqueeze(2).to_broadcast(shape)
                lo, hi, val = [writer[:, k].unsqueeze(1).to_broadcast(shape) for k in range(3)]
                yield lambda lo=lo, keys=keys: tt(m1, lo, keys, ALU.is_le)
                yield lambda hi=hi, keys=keys: tt(m2, hi, keys, ALU.is_ge)
                yield lambda: tt(m1, m1, m2, ALU.mult)
                yield lambda val=val: tt(m1, m1, val, ALU.mult)
                yield lambda i=i: nc.vector.tensor_reduce(wbest[:, i:i + WT], m1, AXX, ALU.max)
            yield lambda: stt(wbest, wbest, -(BIG + 1.0), key_row, ALU.add, ALU.add)
            yield lambda: ts(wneg, wbest, 0.0, float(2 ** 20), ALU.is_lt, ALU.mult)
            yield lambda: tt(new_row, wbest, wneg, ALU.add)
            yield lambda: nc.vector.tensor_copy(new_rowi, new_row)
            yield lambda: ts(thr, ints[:, 17 + B:17 + 2 * B], -STEP, float(WIN - 1) * STEP, ALU.mult, ALU.add)
            yield lambda: ts(tokpos, ints[:, NT:2 * NT], const("tok"), None, ALU.add)
            a3, k3 = [x.rearrange("p (g f) -> p g f", g=NT) for x in (ang, angk)]
            yield lambda: tt(a3, tokpos.unsqueeze(2).to_broadcast([P, NT, 16]),
                             const("inv").unsqueeze(1).to_broadcast([P, NT, 16]), ALU.mult)
            yield lambda: ts(angk, ang, 1.0 / (2 * PI), 12582912.0, ALU.mult, ALU.add)
            yield lambda: ts(angk, angk, -12582912.0, None, ALU.add)
            c1 = 6.28125
            c2 = float(np.float32(np.float16(2 * np.pi - c1)))
            for c in (c1, c2, 2 * np.pi - c1 - c2):
                yield lambda c=c: stt(ang, angk, -float(c), ang, ALU.mult, ALU.add)
            yield lambda: ts(angc, ang, PI / 2, None, ALU.add)
            yield lambda: ts(angk, angc, PI, -2 * PI, ALU.is_gt, ALU.mult)
            yield lambda: tt(angc, angc, angk, ALU.add)
            lim = float(np.nextafter(np.float32(np.pi), np.float32(0)))
            yield lambda: ts(angc, angc, lim, -lim, ALU.min, ALU.max)
            yield lambda: ts(ang, ang, lim, -lim, ALU.min, ALU.max)
            nb = slice(0, NBANK * NH)
            bw, own = const("bw_all")[nb], const("bw_own")[nb]
            cmx, cex, cso, cown = [rms[nb, i:i + 1] for i in range(4)]
            c4 = rms[nb, 8:12]
            yield lambda: nc.vector.tensor_reduce(cmx, bw, AXX, ALU.max)
            yield lambda: ts(c4, bw, cmx, None, ALU.subtract)
            yield lambda: ts(cown, own, cmx, None, ALU.subtract)

        N_PREP = sum(1 for _ in prep_steps(None))
        N_SPREAD = 8 + NU + 9 + 9 + 4
        PREP_A = 5

        def prep_run(dve):
            steps = prep_steps(dve)
            done = [0]

            def run(n):
                for _ in range(n):
                    step = next(steps, None)
                    if step is None:
                        return
                    if done[0] == 0:
                        dve.wait_ge(sem("ld_ints"), 16)
                    else:
                        dve.wait_ge(sem("prep_step"), done[0])
                    step().then_inc(sem("prep_step"), 1)
                    done[0] += 1
            return run

        bdm = cut(wmid, 4096 + 1024, NBANK * KC * P).rearrange("p (n c e) -> p n c e", n=NBANK, c=KC)
        lin_wq = cut(wmid, 4096, 512).rearrange("p (c o) -> p c o", c=KC)
        lin_wo = cut(wmid, 4096 + 512, 512).rearrange("p (c o) -> p c o", c=KC)
        nrc = cut(wmid, 4096 + 2048, KC * NBANK * NH).rearrange("p (c m) -> p c m", c=KC)
        sel = const("sel").rearrange("p (n c o) -> p n c o", n=NBANK, c=KC)
        sig = cut(work, 4096, 2048).rearrange("p (c t) -> p c t", c=KC)
        sigq = cut(work, 6144, 2048).rearrange("p (r t) -> p r t", r=4)
        comb = cut(work, 8192, 2048).rearrange("p (c t) -> p c t", c=KC)
        neg = cut(work, 0, 1024).rearrange("p (r t) -> p r t", r=2)
        expo = cut(work, 1024, 1024).rearrange("p (r t) -> p r t", r=2)
        rnorm = work[0:NBANK * NH, 10240:11264]
        LIN = [(c, n) for c in range(KC) for n in range(2)]
        MEM = [(m, n, c) for m in range(NBANK) for n in range(2) for c in range(KC)]

        def lin_tensor(pe):
            pe.wait_ge(sem("ld_wL"), 16)
            pe.wait_ge(sem("attB_out"), 4)
            for u, (c, n) in enumerate(LIN):
                for k in range(KC):
                    mm = nc.tensor.matmul(ps[:, 4 + u, :], lin_wq[:, k, c * P:(c + 1) * P],
                                          yT[:, k, n * HALF:(n + 1) * HALF], start=(k == 0), stop=(k == KC - 1))
                mm.then_inc(sem("lin_q"), 1)
            pe.wait_ge(sem("lin_sig"), 4)
            for n in range(2):
                for c in range(KC):
                    mm = nc.tensor.matmul(ps[0:NBANK * NH, n, :], nrc[:, c, :], sig[:, c, n * HALF:(n + 1) * HALF],
                                          start=(c == 0), stop=(c == KC - 1))
                mm.then_inc(sem("lin_norm"), 1)

            def memories(u):
                m, n, c = MEM[u]
                pe.wait_ge(sem("lin_scaled"), u + 1)
                nc.tensor.matmul(ps[:, 2 * c + n, :], bdm[:, m, c, :], sigq[:, u % 4, :],
                                 start=(m == 0), stop=(m == NBANK - 1)).then_inc(sem("lin_mem"), 1)

            pe.wait_ge(sem("lin_share"), 2)
            for u, (m, n, c) in enumerate(MEM):
                if u >= 4:
                    pe.wait_ge(sem("lin_scaled"), u - 3)
                nc.tensor.matmul(ps[:, 4 + u % 4, :], sel[0:NBANK * NH, m, c, :], rnorm[:, n * HALF:(n + 1) * HALF],
                                 start=True, stop=True).then_inc(sem("lin_spread"), 1)
                if u >= 2:
                    memories(u - 2)
            memories(len(MEM) - 2)
            memories(len(MEM) - 1)
            pe.wait_ge(sem("lin_comb"), 4)
            for u, (c, n) in enumerate(LIN):
                for k in range(KC):
                    mm = nc.tensor.matmul(ps[:, 4 + u, :], lin_wo[:, k, c * P:(c + 1) * P],
                                          comb[:, k, n * HALF:(n + 1) * HALF], start=(k == 0), stop=(k == KC - 1))
                mm.then_inc(sem("lin_proj"), 1)

        def lin_vector(dve):
            nb = slice(0, NBANK * NH)
            c4, csum, cactive = rms[nb, 8:12], rms[nb, 4:5], rms[nb, 5:6]
            dve.wait_ge(sem("lin_cexp"), 2)
            nc.vector.tensor_reduce(csum, c4, AXX, ALU.add).then_inc(sem("lin_coef"), 1)
            nc.vector.tensor_reduce(cactive, const("norm_all")[nb], AXX, ALU.add).then_inc(sem("lin_coef"), 1)
            dve.wait_ge(sem("lin_coef"), 2)
            nc.vector.reciprocal(rms[nb, 6:7], csum).then_inc(sem("lin_coef"), 1)
            nc.vector.tensor_scalar(cactive, cactive, 1e-6, None, ALU.is_ge).then_inc(sem("lin_coef"), 1)
            dve.wait_ge(sem("lin_coef"), 4)
            nc.vector.scalar_tensor_tensor(coef[nb], rms[nb, 6:7], cactive, rms[nb, 3:4], ALU.mult,
                                           ALU.mult).then_inc(sem("lin_coef"), 1)

            def sigma(u):
                c, n = LIN[u]
                dve.wait_ge(sem("lin_exp"), u + 1)
                nc.vector.scalar_tensor_tensor(sig[:, c, n * HALF:(n + 1) * HALF], ps[:, 4 + u, :], 0.0,
                                               expo[:, u % 2, :], ALU.max, ALU.add).then_inc(sem("lin_sig"), 1)

            for u in range(4):
                dve.wait_ge(sem("lin_q"), u + 1)
                if u >= 2:
                    dve.wait_ge(sem("lin_exp"), u - 1)
                nc.vector.tensor_scalar(neg[:, u % 2, :], ps[:, 4 + u, :], 0.0, None, ALU.min).then_inc(sem("lin_neg"), 1)
                if u >= 1:
                    sigma(u - 1)
            sigma(3)
            for n in range(2):
                h = slice(n * HALF, (n + 1) * HALF)
                dve.wait_ge(sem("lin_norm"), n + 1)
                nc.vector.tensor_scalar(rnorm[:, h], ps[nb, n, :], 1e-6, None, ALU.max).then_inc(sem("lin_clip"), 1)
                dve.wait_ge(sem("lin_clip"), n + 1)
                nc.vector.reciprocal(rnorm[:, h], rnorm[:, h]).then_inc(sem("lin_rec"), 1)
                dve.wait_ge(sem("lin_rec"), n + 1)
                dve.wait_ge(sem("lin_coef"), 5)
                nc.vector.tensor_scalar(rnorm[:, h], rnorm[:, h], coef[nb], None, ALU.mult).then_inc(sem("lin_share"), 1)
            for u, (m, n, c) in enumerate(MEM):
                dve.wait_ge(sem("lin_spread"), u + 1)
                if u >= 4:
                    dve.wait_ge(sem("lin_mem"), u - 3)
                nc.vector.tensor_tensor(sigq[:, u % 4, :], ps[:, 4 + u % 4, :], sig[:, c, n * HALF:(n + 1) * HALF],
                                        ALU.mult).then_inc(sem("lin_scaled"), 1)
            for u, (c, n) in enumerate(LIN):
                dve.wait_ge(sem("lin_proj"), u + 1)
                to = xT[:, c, n * HALF:(n + 1) * HALF]
                nc.vector.tensor_tensor(to, ps[:, 4 + u, :], to, ALU.add).then_inc(sem("lin_out"), 1)

        def lin_scalar(act):
            nb = slice(0, NBANK * NH)
            act.wait_ge(sem("prep_step"), N_PREP)
            nc.scalar.activation(rms[nb, 8:12], rms[nb, 8:12], ACT.Exp).then_inc(sem("lin_cexp"), 1)
            nc.scalar.activation(rms[nb, 3:4], rms[nb, 3:4], ACT.Exp).then_inc(sem("lin_cexp"), 1)
            for u in range(4):
                act.wait_ge(sem("lin_neg"), u + 1)
                if u >= 2:
                    act.wait_ge(sem("lin_sig"), u - 1)
                nc.scalar.activation(expo[:, u % 2, :], neg[:, u % 2, :], ACT.Exp).then_inc(sem("lin_exp"), 1)
            act.wait_ge(sem("lin_mem"), len(MEM))
            for u, (c, n) in enumerate(LIN):
                nc.scalar.activation(comb[:, c, n * HALF:(n + 1) * HALF], ps[:, 2 * c + n, :],
                                     ACT.Copy).then_inc(sem("lin_comb"), 1)

        qmask = cut(work, 0, 8192).rearrange("p (b g h t) -> p b g h t", b=B, g=GRP, h=2)
        newkv = cut(work, 8192, 2048).rearrange("p (g f) -> p g f", g=NT)
        kT = cut(work, 10240, 640).rearrange("p (b j) -> p b j", b=4)
        kv = cut(work, 11264, NGT * 256).rearrange("p (i f) -> p i f", i=NGT)
        raw = cut(wmid, 0, 3072).rearrange("p (g k f) -> p g k f", g=NT, k=12)
        qtok = cut(wmid, 3072, 2048).rearrange("p (g f) -> p g f", g=NT)
        rot = cut(wmid, 5120, 768).rearrange("p (m k f) -> p m k f", m=4, k=12)
        sqr = cut(work, 0, 3072).rearrange("p (g f) -> p g f", g=NT)
        pT = cut(wmid, 0, 1024).rearrange("p (b a q) -> p b a q", b=4, a=2)
        plast = cut(wmid, 1024, 256).rearrange("p (a b j) -> p a b j", a=2, b=4)
        plastT = cut(wmid, 1280, 1024).rearrange("p (a b q) -> p a b q", a=2, b=4)
        psc = cut(wmid, 2304, 640).rearrange("p (r a j) -> p r a j", r=2, a=2)
        pex = cut(wmid, 5120, 640).rearrange("p (r a j) -> p r a j", r=2, a=2)
        pmk = cut(wmid, 5888, 320).rearrange("p (r j) -> p r j", r=2)
        pst = small_buf(B * 6).rearrange("p (b x) -> p b x", b=B)
        oT = cut(wmid, 3072, 2048).rearrange("p (h t) -> p h t", h=2)
        cT = cut(work, 0, 2048).rearrange("p (c t) -> p c t", c=KC)
        page_w = cut(wpage, 0, 1024).rearrange("p (c o) -> p c o", c=KC)
        page_wo = cut(wpage, 1024, 512).rearrange("p (c o) -> p c o", c=KC)
        gsc = small_buf(KC * PHD).rearrange("p (a f) -> p a f", a=2)

        def page_tensor(pe):
            pe.wait_ge(sem("ld_wP"), 16)
            pe.wait_ge(sem("lin_out"), 4)
            for g in range(NT):
                for k in range(KC):
                    mm = nc.tensor.matmul(ps[:, g, :], xT[:, k, g * P:(g + 1) * P], page_w[:, k, :],
                                          start=(k == 0), stop=(k == KC - 1))
                mm.then_inc(sem("page_proj"), 1)
            for hh in range(2):
                for g in range(NT):
                    pe.wait_ge(sem("page_rot"), 4 * (g + 1))
                    pe.wait_ge(sem("page_raw"), 3 * NT)
                    tr = nc.tensor.transpose(ps[:, 2 * hh + g // 4, (g % 4) * P:(g % 4 + 1) * P],
                                             qtok[:, g, hh * P:(hh + 1) * P], ident)
                    if g % 4 == 3:
                        tr.then_inc(sem("page_qt"), 1)
            pe.wait_ge(sem("page_qm"), 16)

            def keys(q4):
                pe.wait_ge(sem(f"overlay{q4}"), 16 * 5)
                if q4:
                    pe.wait_ge(sem("page_kT"), 2 * q4)
                for j in range(4):
                    nc.tensor.transpose(ps[:, 0, j * P:(j + 1) * P], kv[:, 4 * q4 + j, 0:P], ident)
                nc.tensor.transpose(ps[:, 1, 0:P], kv[:, B + q4, 0:P], ident).then_inc(sem("page_k"), 1)

            def scores(b):
                pe.wait_ge(sem("page_kT"), 2 * (b // 4) + 2)
                if b >= 2:
                    pe.wait_ge(sem("page_scaled"), b - 1)
                for a in range(2):
                    mm = nc.tensor.matmul(ps[:, 2 + b % 2, a * NKEY:(a + 1) * NKEY],
                                          qmask[:, b, 2 * a:2 * a + 2, :, :].rearrange("p g h t -> p (g h t)"),
                                          kT[:, b % 4, :], start=True, stop=True)
                mm.then_inc(sem("page_scores"), 1)

            def turn(b):
                pe.wait_ge(sem("page_norm"), 2 * (b + 1))
                if b >= 2:
                    pe.wait_ge(sem("page_pT"), b - 1)
                for a in range(2):
                    tr = nc.tensor.transpose(ps[:, 4 + b % 2, a * P:(a + 1) * P], pex[:, b % 2, a, 0:P], ident)
                tr.then_inc(sem("page_turned"), 1)

            def turn_last(q4):
                if q4:
                    pe.wait_ge(sem("page_lT"), 4 * q4)
                for a in range(2):
                    tr = nc.tensor.transpose(ps[:, 6, a * P:(a + 1) * P],
                                             plast[:, a, :, :].rearrange("p b j -> p (b j)"), ident)
                tr.then_inc(sem("page_lturned"), 1)

            def values(q4):
                pe.wait_ge(sem("page_lT"), 4 * q4 + 4)
                pe.wait_ge(sem("page_pT"), 4 * q4 + 4)
                if q4:
                    pe.wait_ge(sem("page_o"), q4)
                for g in range(GRP):
                    o = slice(32 * g, 32 * g + 32)
                    q = slice((g % 2) * 64, (g % 2) * 64 + 64)
                    v = slice(P + 32 * g, P + 32 * g + 32)
                    nc.tensor.matmul(ps[o, 7, 0:256].rearrange("p (b q) -> p b q", b=4), kv[:, B + q4, v],
                                     plastT[:, g // 2, :, q], start=True, stop=False)
                    for j in range(4):
                        mm = nc.tensor.matmul(ps[o, 7, 64 * j:64 * j + 64], kv[:, 4 * q4 + j, v], pT[:, j, g // 2, q],
                                              start=False, stop=(j == 3))
                mm.then_inc(sem("page_pv"), 1)

            for b in range(B + 2):
                if b < B:
                    if b % 4 == 0:
                        keys(b // 4)
                    scores(b)
                if 1 <= b <= B:
                    turn(b - 1)
                if b >= 4 and b % 4 == 0:
                    turn_last(b // 4 - 1)
                if b >= 4 and b % 4 == 1:
                    values(b // 4 - 1)
            pe.wait_ge(sem("page_o"), B // 4)
            for c in range(KC):
                for n in range(2):
                    for k in range(KC):
                        mm = nc.tensor.matmul(ps[:, 2 * c + n, :], page_wo[:, k, c * P:(c + 1) * P],
                                              oT[:, k, n * HALF:(n + 1) * HALF], start=(k == 0), stop=(k == KC - 1))
                    mm.then_inc(sem("page_wo"), 1)

        def page_vector(dve):
            tt, stt = nc.vector.tensor_tensor, nc.vector.scalar_tensor_tensor
            nc.vector.tensor_scalar(gsc[:, 0, :], const("qscale"), 1.0, None, ALU.add).then_inc(sem("page_gain"), 1)
            nc.vector.tensor_scalar(gsc[:, 1, :], const("kscale"), 1.0, None, ALU.add).then_inc(sem("page_gain"), 1)
            for g in range(NT):
                dve.wait_ge(sem("page_raw"), 3 * g + 3)
                nc.vector.tensor_reduce(rms[:, 12 * g:12 * g + 12], sqr[:, g, :].rearrange("p (k f) -> p k f", k=12),
                                        AXX, ALU.add).then_inc(sem("page_ms"), 1)
            dve.wait_ge(sem("page_ms"), NT)
            nc.vector.tensor_scalar(rms[:, :], rms[:, :], 1.0 / PHD, 1e-6, ALU.mult, ALU.add).then_inc(sem("page_ms"), 1)
            dve.wait_ge(sem("page_sqrt"), 1)
            nc.vector.reciprocal(rms[:, :], rms[:, :]).then_inc(sem("page_ms"), 1)
            dve.wait_ge(sem("page_ms"), NT + 2)
            dve.wait_ge(sem("page_gain"), 2)
            dve.wait_ge(sem("rope_ready"), 2)
            for g in range(NT):
                x = raw[:, g]
                tt(x, x, rms[:, 12 * g:12 * g + 12].unsqueeze(2).to_broadcast([P, 12, PHD]), ALU.mult)\
                    .then_inc(sem("page_unit"), 1)
                dve.wait_ge(sem("page_unit"), g + 1)
                tt(x[:, 0:8], x[:, 0:8], gsc[:, 0:1, :].to_broadcast([P, 8, PHD]), ALU.mult).then_inc(sem("page_gained"), 1)
                tt(x[:, 8:12], x[:, 8:12], gsc[:, 1:2, :].to_broadcast([P, 4, PHD]), ALU.mult)\
                    .then_inc(sem("page_gained"), 1)
                dve.wait_ge(sem("page_gained"), 2 * g + 2)
                if g:
                    dve.wait_ge(sem("page_rot"), 4 * g)
                cb, sb_ = [t[:, g:g + 1, :].to_broadcast([P, 12, 16]) for t in (cosb, sinb)]
                lo, hi = x[:, :, 0:16], x[:, :, 16:32]
                for m, (a, w) in enumerate(((lo, cb), (hi, sb_), (hi, cb), (lo, sb_))):
                    tt(rot[:, m], a, w, ALU.mult).then_inc(sem("page_rmul"), 1)
                dve.wait_ge(sem("page_rmul"), 4 * g + 4)
                q = qtok[:, g, :].rearrange("p (k f) -> p k f", k=8)
                k = newkv[:, g, 0:P].rearrange("p (k f) -> p k f", k=4)
                for o, s0, s1 in ((q, 0, 8), (k, 8, 12)):
                    tt(o[:, :, 0:16], rot[:, 0, s0:s1], rot[:, 1, s0:s1], ALU.subtract).then_inc(sem("page_rot"), 1)
                    tt(o[:, :, 16:32], rot[:, 2, s0:s1], rot[:, 3, s0:s1], ALU.add).then_inc(sem("page_rot"), 1)
            for n in range(2):
                dve.wait_ge(sem("page_qt"), n + 1)
                for g in range(GRP):
                    nc.vector.tensor_scalar(qmask[:, 16 * n:16 * n + 16, g, 0, :],
                                            ps[:, n, :].rearrange("p (b t) -> p b t", t=S),
                                            const("quad")[:, g:g + 1], None, ALU.mult).then_inc(sem("page_qm"), 1)

            def before(b):
                stt(pmk[:, b % 2, :], const("jstep"), thr[:, b:b + 1], const("band"), ALU.subtract, ALU.min)\
                    .then_inc(sem("page_mask"), 1)
                dve.wait_ge(sem("page_mask"), b + 1)
                dve.wait_ge(sem("page_scores"), b + 1)
                stt(psc[:, b % 2], ps[:, 2 + b % 2, 0:2 * NKEY].rearrange("p (a j) -> p a j", a=2), 1.0 / 16,
                    pmk[:, b % 2:b % 2 + 1, :].to_broadcast([P, 2, NKEY]), ALU.mult, ALU.add).then_inc(sem("page_scaled"), 1)
                dve.wait_ge(sem("page_scaled"), b + 1)
                nc.vector.tensor_reduce(pst[:, b, 0:2], psc[:, b % 2], AXX, ALU.max, negate=True)\
                    .then_inc(sem("page_max"), 1)

            def after(b):
                dve.wait_ge(sem("page_exp"), 2 * b + 2)
                nc.vector.reciprocal(pst[:, b, 4:6], pst[:, b, 2:4]).then_inc(sem("page_rec"), 1)
                dve.wait_ge(sem("page_rec"), b + 1)
                r = pst[:, b, 4:6].unsqueeze(2)
                if b % 4 == 0 and b:
                    dve.wait_ge(sem("page_lturned"), b // 4)
                x = pex[:, b % 2]
                tt(plast[:, :, b % 4, :], x[:, :, P:NKEY], r.to_broadcast([P, 2, S]), ALU.mult).then_inc(sem("page_norm"), 1)
                tt(x[:, :, 0:P], x[:, :, 0:P], r.to_broadcast([P, 2, P]), ALU.mult).then_inc(sem("page_norm"), 1)

            def keep(b):
                dve.wait_ge(sem("page_turned"), b + 1)
                if b % 4 == 0 and b:
                    dve.wait_ge(sem("page_pv"), b // 4)
                nc.vector.tensor_copy(pT[:, b % 4], ps[:, 4 + b % 2, 0:2 * P].rearrange("p (a q) -> p a q", a=2))\
                    .then_inc(sem("page_pT"), 1)

            for b in range(B + 2):
                if b < B:
                    before(b)
                if 1 <= b <= B:
                    after(b - 1)
                if b >= 2:
                    keep(b - 2)
            for c in range(KC):
                for n in range(2):
                    dve.wait_ge(sem("page_wo"), 2 * c + n + 1)
                    nc.vector.tensor_copy(cT[:, c, n * HALF:(n + 1) * HALF], ps[:, 2 * c + n, :]).then_inc(sem("page_out"), 1)

        def page_scalar(act):
            for g in range(NT):
                act.wait_ge(sem("page_proj"), g + 1)
                nc.scalar.activation(sqr[:, g, :], ps[:, g, 0:3 * P], ACT.Square).then_inc(sem("page_raw"), 1)
                nc.scalar.activation(raw[:, g].rearrange("p k f -> p (k f)"), ps[:, g, 0:3 * P], ACT.Copy)\
                    .then_inc(sem("page_raw"), 1)
                nc.scalar.activation(newkv[:, g, P:2 * P], ps[:, g, 3 * P:4 * P], ACT.Copy).then_inc(sem("page_raw"), 1)
            act.wait_ge(sem("page_ms"), NT + 1)
            nc.scalar.activation(rms[:, :], rms[:, :], ACT.Sqrt).then_inc(sem("page_sqrt"), 1)
            for n in range(2):
                act.wait_ge(sem("page_qt"), 2 + n + 1)
                for g in range(GRP):
                    nc.scalar.activation(qmask[:, 16 * n:16 * n + 16, g, 1, :],
                                         ps[:, 2 + n, :].rearrange("p (b t) -> p b t", t=S), ACT.Copy,
                                         scale=const("quad")[:, g:g + 1]).then_inc(sem("page_qm"), 1)

            def keep_last(q4):
                act.wait_ge(sem("page_lturned"), q4 + 1)
                if q4:
                    act.wait_ge(sem("page_pv"), q4)
                for j in range(4):
                    nc.scalar.activation(plastT[:, :, j, :], ps[:, 6, 0:2 * P].rearrange("p (a q) -> p a q", a=2),
                                         ACT.Copy, scale=const("quad")[:, j:j + 1]).then_inc(sem("page_lT"), 1)

            def keep_output(q4):
                act.wait_ge(sem("page_pv"), q4 + 1)
                nc.scalar.activation(oT[:, :, q4 * P:(q4 + 1) * P].rearrange("p h (b t) -> p b h t", b=4),
                                     ps[:, 7, 0:256].rearrange("p (b h t) -> p b h t", b=4, h=2),
                                     ACT.Copy).then_inc(sem("page_o"), 1)

            for b in range(B):
                if b % 4 == 0:
                    act.wait_ge(sem("page_k"), b // 4 + 1)
                    if b:
                        act.wait_ge(sem("page_scores"), b)
                    nc.scalar.activation(kT[:, :, 0:P], ps[:, 0, :].rearrange("p (b j) -> p b j", b=4), ACT.Copy)\
                        .then_inc(sem("page_kT"), 1)
                    nc.scalar.activation(kT[:, :, P:NKEY], ps[:, 1, 0:P].rearrange("p (b j) -> p b j", b=4), ACT.Copy)\
                        .then_inc(sem("page_kT"), 1)
                act.wait_ge(sem("page_max"), b + 1)
                if b >= 2:
                    act.wait_ge(sem("page_turned"), b - 1)
                    act.wait_ge(sem("page_norm"), 2 * b - 2)
                for a in range(2):
                    nc.scalar.activation(pex[:, b % 2, a, :], psc[:, b % 2, a, :], ACT.Exp, bias=pst[:, b, a:a + 1],
                                         accum_out=pst[:, b, 2 + a:3 + a]).then_inc(sem("page_exp"), 1)
                if b % 4 == 0 and b:
                    keep_last(b // 4 - 1)
                if b % 4 == 2 and b > 2:
                    keep_output(b // 4 - 1)
            keep_last(B // 4 - 1)
            keep_output(B // 4 - 1)

        wr = wrt[:, :].rearrange("p (c e) -> p c e", c=KC)
        routew = work[0:NE, 9728:9728 + T]
        r0 = 2048
        logit = cut(work, r0, P).rearrange("p (g e) -> p g e", g=NT)
        prb = cut(work, r0 + 128, P).rearrange("p (g e) -> p g e", g=NT)
        wgt = cut(work, r0 + 256, P).rearrange("p (g e) -> p g e", g=NT)
        oh = cut(work, r0 + 384, P).rearrange("p (g e) -> p g e", g=NT)
        best = cut(work, r0 + 512, 64).rearrange("p (g x) -> p g x", g=NT)
        bidx = cut(work, r0 + 576, 64).rearrange("p (g x) -> p g x", g=NT)
        rst = cut(work, r0 + 640, 64).rearrange("p (g x) -> p g x", g=NT)
        bidxu = int_buf(64).rearrange("p (g x) -> p g x", g=NT)

        def route_tensor_first(pe):
            pe.wait_ge(sem("ld_wR"), 16)
            pe.wait_ge(sem("page_out"), 4)
            for g in range(NT):
                for k in range(KC):
                    mm = nc.tensor.matmul(ps[:, 2, g * NE:(g + 1) * NE], cT[:, k, g * P:(g + 1) * P], wr[:, k, :],
                                          start=(k == 0), stop=(k == KC - 1))
            mm.then_inc(sem("route_logit"), 1)

        def route_tensor(pe, i):
            if i != 1:
                return
            pe.wait_ge(sem("route_w"), 1)
            for g in range(NT):
                tr = nc.tensor.transpose(ps[0:NE, 2 + g // 4, (g % 4) * P:(g % 4 + 1) * P], wgt[:, g, :], ident)
                if g % 4 == 3:
                    tr.then_inc(sem("route_turned"), 1)

        def route_vector(dve):
            tt = nc.vector.tensor_tensor
            bc = lambda a: a.unsqueeze(2).to_broadcast([P, NT, NE])
            step = [0]

            def link(ins):
                ins.then_inc(sem("route_step"), 1)
                step[0] += 1
                dve.wait_ge(sem("route_step"), step[0])

            dve.wait_ge(sem("route_logit"), 1)
            link(tt(logit, ps[:, 2, 0:P].rearrange("p (g e) -> p g e", g=NT),
                    const("rbias").unsqueeze(1).to_broadcast([P, NT, NE]), ALU.add))
            link(nc.vector.tensor_reduce(rst[:, :, 0], logit, AXX, ALU.max))
            tt(logit, logit, bc(rst[:, :, 0]), ALU.subtract).then_inc(sem("route_shift"), 1)
            dve.wait_ge(sem("route_exp"), 1)
            link(nc.vector.tensor_reduce(rst[:, :, 1], prb, AXX, ALU.add))
            link(nc.vector.reciprocal(rst[:, :, 2], rst[:, :, 1]))
            link(tt(prb, prb, bc(rst[:, :, 2]), ALU.mult))
            for g in range(NT):
                link(nc.vector.max(best[:, g, :], prb[:, g, :]))
                link(nc.vector.max_index(bidxu[:, g, :].bitcast(U32), best[:, g, :], prb[:, g, :]))
            link(nc.vector.tensor_copy(bidx, bidxu))
            e3 = const("e16").unsqueeze(1).to_broadcast([P, NT, NE])
            link(tt(oh, e3, bc(bidx[:, :, 0]), ALU.is_equal))
            link(tt(wgt, e3, bc(bidx[:, :, 1]), ALU.is_equal))
            link(tt(wgt, wgt, oh, ALU.add))
            link(tt(wgt, wgt, prb, ALU.mult))
            link(nc.vector.scalar_tensor_tensor(rst[:, :, 3], best[:, :, 0], 1e-9, best[:, :, 1], ALU.add, ALU.add))
            link(nc.vector.reciprocal(rst[:, :, 4], rst[:, :, 3]))
            tt(wgt, wgt, bc(rst[:, :, 4]), ALU.mult).then_inc(sem("route_w"), 1)
            for n in range(2):
                dve.wait_ge(sem("route_turned"), n + 1)
                nc.vector.tensor_copy(routew[:, n * HALF:(n + 1) * HALF], ps[0:NE, 2 + n, :]).then_inc(sem("route_kept"), 1)

        def route_scalar(act):
            act.wait_ge(sem("route_shift"), 1)
            nc.scalar.activation(prb, logit, ACT.Exp).then_inc(sem("route_exp"), 1)

        att_a = Attention("attA", xnT, 0, ("mix_out", 4), "ld_wA", True, xT)
        att_b = Attention("attB", xT, 2048, ("ffnB_out", 4), "ld_wB", False, yT)

        def weights(base, *shapes):
            got = []
            for k, n in shapes:
                got.append(cut(wbig, base, k * n).rearrange("p (k n) -> p k n", k=k))
                base += k * n
            return got

        ag, au, wgA, wuA, bg, bu, wdA, adn, bd = weights(
            0, (KC, P), (KC, P), (KC, HID), (KC, HID), (1, HID), (1, HID), (HID // P, D), (HID // P, P), (1, D))
        wgB, wuB, wdB = weights(wF_d.shape[1], (KC, HID), (KC, HID), (HID // P, D))
        moe_cols = (NE + 1) * P
        wgE, wuE, wdE = weights(0, (KC, moe_cols), (KC, moe_cols), (NE + 1, D))
        lora = {"first": [ag, au], "second": [bg[:, 0, :], bu[:, 0, :]], "down_first": adn, "down_second": bd[:, 0, :]}

        state = {}

        def prep_vector(per_unit):
            def run(dve, i):
                if "prep" not in state:
                    state["prep"] = prep_run(dve)
                state["prep"](per_unit)
            return run

        def prep_tensor(pe, i):
            if i != -(-N_SPREAD // PREP_A) + 1:
                return
            pe.wait_ge(sem("prep_step"), N_SPREAD)
            nc.tensor.transpose(ps[:, 3, 0:B], krow[:, 0:P], ident[0:B, 0:B])
            nc.tensor.matmul(ps[:, 3, B:NGT], last32.rearrange("p q j -> p (q j)"), row("seqdiv"), start=True, stop=True)
            nc.tensor.matmul(ps[:, 3, 64:64 + 3 * B * NWR], row("ones"), spread.rearrange("p k b s -> p (k b s)"),
                             start=True, stop=True).then_inc(sem("prep_spread"), 1)

        def angles_scalar(act, i):
            if i != 15:
                return
            act.wait_ge(sem("prep_step"), N_PREP)
            nc.scalar.activation(sinb.rearrange("p g f -> p (g f)"), ang[:, :], ACT.Sin).then_inc(sem("rope_ready"), 1)
            nc.scalar.activation(cosb.rearrange("p g f -> p (g f)"), angc[:, :], ACT.Sin).then_inc(sem("rope_ready"), 1)

        ffn_a = Gated("ffnA", xT, wgA, wuA, wdA, HID // P, ("attA_out", 4), "ld_wF", lora=lora, add=False, out_to=yT,
                      extra_tensor=prep_tensor, extra_vector=prep_vector(PREP_A))
        ffn_b = Gated("ffnB", yT, wgB, wuB, wdB, HID // P, ("ffnA_out", 4), "ld_wG", add=True, out_to=xT,
                      extra_vector=prep_vector(6), extra_scalar=angles_scalar)
        moe = Gated("moe", cT, wgE, wuE, wdE, NE + 1, ("page_out", 4), "ld_wE", routed=NE, add=True, out_to=xT,
                    extra_tensor=route_tensor)

        block = ctx.enter_context(nc.Block())

        @block.sync
        def _(sp):
            sp.dma_start(ints[:, :], ints_d).then_inc(sem("ld_ints"), 16)
            sp.dma_start(x_tok.rearrange("p g f -> p (g f)"), x_tok_d).then_inc(sem("ld_x_tok"), 16)
            sp.wait_ge(sem("mix_gather"), 16 * NT)
            sp.dma_start(small[:, :], small_d).then_inc(sem("ld_small"), 16)
            sp.dma_start(wmid[:, 0:2048], wA_d).then_inc(sem("ld_wA"), 16)
            sp.dma_start(xT.rearrange("p c t -> p (c t)"), x_feat_d).then_inc(sem("ld_x_feat"), 16)
            n = wF_d.shape[1]
            sp.dma_start(wbig[:, 0:n], wF_d).then_inc(sem("ld_wF"), 16)
            sp.dma_start(wbig[:, n:n + wG_d.shape[1]], wG_d).then_inc(sem("ld_wG"), 16)
            sp.dma_start(wmid[:, 2048:4096], wB_d).then_inc(sem("ld_wB"), 16)
            sp.dma_start(wmid[:, 4096:4096 + wL_d.shape[1]], wL_d).then_inc(sem("ld_wL"), 16)
            sp.dma_start(wrt[:, :], wR_d).then_inc(sem("ld_wR"), 16)
            sp.wait_ge(sem("ffnB_out"), 4)
            sp.dma_start(wpage, wP_d).then_inc(sem("ld_wP"), 16)
            sp.dma_start(wbig[:, 0:wE_d.shape[1]], wE_d).then_inc(sem("ld_wE"), 16)
            for g in range(NT):
                sp.wait_ge(sem("page_rot"), 4 * g + 4)
                sp.wait_ge(sem("page_raw"), 3 * g + 3)
                sp.dma_start(new_kv[g * P:(g + 1) * P, :], newkv[:, g, :]).then_inc(sem("page_new"), 16)
            sp.wait_ge(sem("route_kept"), 2)
            sp.dma_start(route_d[:, :], routew[:, :]).then_inc(sem("route_stored"), 16)
            sp.wait_ge(sem("route_stored"), 16)
            for n in range(2):
                for e in range(NE):
                    r = n * NE + e
                    if r >= 4:
                        old = r - 4
                        sp.wait_ge(sem("moe_act_ready"), (old // NE) * (NE + 1) + old % NE + 1)
                    sp.dma_start(share[:, r % 4, :], route_d[e:e + 1, n * HALF:(n + 1) * HALF].to_broadcast([P, HALF]))\
                        .then_inc(sem(f"share{r % 4}"), 16)
            for n in range(2):
                sp.wait_ge(sem("moe_out"), 2 * n + 2)
                sp.dma_start(out.rearrange("(c p) t -> p c t", p=P)[:, :, n * HALF:(n + 1) * HALF],
                             xT[:, :, n * HALF:(n + 1) * HALF]).then_inc(sem("stored"), 16)
            sp.wait_ge(sem("stored"), 32)

        @block.gpsimd
        def _(pool):
            def gather(dst, table, rows, bound=None):
                return nc.gpsimd.indirect_dma_start(
                    dst, None, table, bass.IndirectOffsetOnAxis(ap=rows.bitcast(U32), axis=0),
                    **({} if bound is None else {"bounds_check": bound, "oob_is_err": False}))

            pool.wait_ge(sem("mix_rows"), 1)
            for g in range(NT):
                gather(mix_w[:, g, :], mix_table, mix_rows[:, g:g + 1]).then_inc(sem("mix_gather"), 16)
            nc.gpsimd.memset(vpar.rearrange("p g a h d -> p (g a h d)"), 0.0).then_inc(sem("zeroed"), 1)
            nc.gpsimd.memset(pdiag.rearrange("p r h q -> p (r h q)"), 0.0).then_inc(sem("zeroed"), 1)
            pool.wait_ge(sem("attB_out"), 4)
            pool.wait_ge(sem("prep_step"), N_PREP)
            order = [t for q4 in range(B // 4) for t in [B + q4] + list(range(4 * q4, 4 * q4 + 4))]
            for t in order:
                gather(kv[:, t, :], cache, key_rowi[:, t:t + 1]).then_inc(sem("cached"), 16)
            pool.wait_ge(sem("cached"), 16 * NGT)
            pool.wait_ge(sem("page_new"), 16 * NT)
            for n, t in enumerate(order):
                gather(kv[:, t, :], new_kv, new_rowi[:, t:t + 1], T - 1).then_inc(sem(f"overlay{n // 5}"), 16)
            moe.gpsimd(pool)

        @block.scalar
        def _(act):
            act.wait_ge(sem("mix_var"), 1)
            nc.scalar.activation(rstd[:, :], rstd[:, :], ACT.Sqrt).then_inc(sem("mix_sqrt"), 1)
            att_a.scalar(act)
            ffn_a.scalar(act)
            ffn_b.scalar(act)
            att_b.scalar(act)
            lin_scalar(act)
            page_scalar(act)
            route_scalar(act)
            moe.scalar(act)

        @block.vector
        def _(dve):
            dve.wait_ge(sem("ld_ints"), 16)
            nc.vector.scalar_tensor_tensor(mix_rows, ints[:, 0:NT], 32.0, ints[:, ints_d.shape[1] - NT:ints_d.shape[1]],
                                           ALU.mult, ALU.add).then_inc(sem("mix_rows"), 1)
            dve.wait_ge(sem("ld_small"), 16)
            nc.vector.tensor_scalar(admask[:, :], ints[:, 2 * NT:2 * NT + B], const("adapter"), None, ALU.is_equal)\
                .then_inc(sem("masks"), 1)
            nc.vector.tensor_scalar(temps[:, :], const("temp"), 4.0, 0.25, ALU.min, ALU.mult).then_inc(sem("masks"), 1)
            for g in range(NT):
                dve.wait_ge(sem("mixed"), (g | 1) + 1)
                m = ps[:, g // 2, (g % 2) * D:(g % 2 + 1) * D]
                nc.vector.bn_stats(stats[:, g, :], m).then_inc(sem("mix_stats"), 1)
                dve.wait_ge(sem("mix_stats"), g + 1)
                nc.vector.bn_aggr(meanvar[:, g, :], stats[:, g, :]).then_inc(sem("mix_aggr"), 1)
            dve.wait_ge(sem("mix_aggr"), NT)
            nc.vector.tensor_scalar(rstd[:, :], meanvar[:, :, 1], 1e-5, None, ALU.add).then_inc(sem("mix_var"), 1)
            dve.wait_ge(sem("mix_sqrt"), 1)
            nc.vector.reciprocal(rstd[:, :], rstd[:, :]).then_inc(sem("mix_rstd"), 1)
            dve.wait_ge(sem("mix_rstd"), 1)
            for g in range(NT):
                nc.vector.tensor_scalar(xn_tok[:, g, :], ps[:, g // 2, (g % 2) * D:(g % 2 + 1) * D],
                                        meanvar[:, g, 0:1], rstd[:, g:g + 1], ALU.subtract, ALU.mult)\
                    .then_inc(sem("mix_norm"), 1)
            for c in range(KC):
                for h in range(2):
                    dve.wait_ge(sem("mix_turned"), 2 * c + h + 1)
                    nc.vector.tensor_scalar(xnT[:, c, h * HALF:(h + 1) * HALF], ps[:, 4 + 2 * c + h, :],
                                            const("ln_g")[:, c:c + 1], const("ln_b")[:, c:c + 1], ALU.mult, ALU.add)\
                        .then_inc(sem("mix_out"), 1)
            att_a.vector(dve)
            dve.wait_ge(sem("masks"), 2)
            ffn_a.vector(dve)
            ffn_b.vector(dve)
            att_b.vector(dve)
            lin_vector(dve)
            page_vector(dve)
            route_vector(dve)
            moe.vector(dve)

        @block.tensor
        def _(pe):
            pe.wait_ge(sem("ld_x_tok"), 16)
            pe.wait_ge(sem("mix_gather"), 16 * NT)
            for g in range(NT):
                for j in range(4):
                    q = slice(32 * j, 32 * j + 32)
                    mm = nc.tensor.matmul(ps[q, g // 2, (g % 2) * D:(g % 2 + 1) * D], mix_w[q, g, :], x_tok[q, g, :],
                                          start=True, stop=True)
                mm.then_inc(sem("mixed"), 1)
            pe.wait_ge(sem("ld_small"), 16)
            for c in range(KC):
                for g in range(NT):
                    pe.wait_ge(sem("mix_norm"), g + 1)
                    tr = nc.tensor.transpose(ps[:, 4 + 2 * c + g // 4, (g % 4) * P:(g % 4 + 1) * P],
                                             xn_tok[:, g, c * P:(c + 1) * P], ident)
                    if g % 4 == 3:
                        tr.then_inc(sem("mix_turned"), 1)
            att_a.tensor(pe)
            ffn_a.tensor(pe)
            ffn_b.tensor(pe)
            att_b.tensor(pe)
            lin_tensor(pe)
            page_tensor(pe)
            route_tensor_first(pe)
            moe.tensor(pe)


def kernel(**inputs):
    import concourse.bacc as _bacc
    from concourse.bass_utils import run_bass_kernel_spmd as _run

    nc = _bacc.Bacc("TRN2", target_bir_lowering=False, num_devices=1)
    arrays, args = {}, []
    packed, small_at = layout({k: np.asarray(v) for k, v in inputs.items()})
    for name in ("x_tok", "x_feat", "mix_table", "small", "ints", "wA", "wB", "wF", "wG", "wL", "wP", "cache", "wR", "wE"):
        a = np.ascontiguousarray(packed[name])
        arrays[f"in_{name}_dram"] = a
        args.append(nc.dram_tensor(f"in_{name}_dram", a.shape, mybir.dt.from_np(a.dtype), kind="ExternalInput").ap())
    args.append(nc.dram_tensor("out_0_dram", (D, T), F32, kind="ExternalOutput").ap())
    program(nc, small_at, *args)
    r = _run(nc, [arrays], core_ids=[0])
    return r.results[0]["out_0_dram"].T.reshape(B, S, D)
```

```python
from contextlib import ExitStack

import numpy as np

import concourse.bass as bass
from concourse import mybir

F32 = mybir.dt.float32
F32R = mybir.dt.float32r
I32 = mybir.dt.int32
U32 = mybir.dt.uint32
ALU = mybir.AluOpType
ACT = mybir.ActivationFunctionType
AXX = mybir.AxisListType.X

P = 128
B, S, D = 32, 32, 256
T = B * S
KC = D // P
NT = T // P
HALF = T // 2
NH, HD = 16, 16
HID = 1024
NAD, RANK = 8, 16
NBANK = 4
NE = 16
GRP, PHD = 4, 32
BLK, WIN, NSLOT = 16, 128, 257
NKEY = WIN + S
NU = (NKEY + BLK - 1) // BLK + 1
KVROWS = 16 * NSLOT * BLK
NGT = B + B * S // P
NWR = 4
NEG = -1.0e30
BIG = float(2 ** 17)
STEP = float(2 ** 100)
PI = float(np.pi)


def constants():
    p = np.arange(P)
    c = {}
    c["ident"] = np.eye(P, dtype=np.float32)
    m = np.where(np.arange(S)[None, :] > (p % S)[:, None], NEG, 0.0).astype(np.float32)
    c["causal"] = np.tile(m, (1, NH))
    c["parity"] = ((p[:, None] // HD) % 2 == np.arange(2)[None, :]).astype(np.float32)
    c["adapter"] = (p[:, None] // RANK).astype(np.float32)
    c["quad"] = (p[:, None] // 32 == np.arange(4)[None, :]).astype(np.float32)
    j = np.arange(NKEY)[None, :]
    t = (p % S)[:, None]
    c["band"] = np.where((j >= t) & (j <= t + WIN - 1), 0.0, NEG).astype(np.float32)
    c["jstep"] = np.broadcast_to(j.astype(np.float32) * np.float32(STEP), (P, NKEY))
    c["tok"] = t.astype(np.float32)
    half = PHD // 2
    inv = np.float32(1.0) / np.float32(10000.0) ** (np.arange(half, dtype=np.float32) / np.float32(half))
    c["inv"] = np.broadcast_to(inv.astype(np.float32)[None, :], (P, half))
    c["ones"] = np.ones((P, P), np.float32)
    c["e16"] = np.broadcast_to(np.arange(NE, dtype=np.float32)[None, :], (P, NE))
    sel = np.zeros((P, NBANK, KC, P), np.float32)
    for n in range(NBANK):
        for h in range(NH):
            cc, r = divmod(h * HD, P)
            sel[n * NH + h, n, cc, r:r + HD] = 1.0
    c["slots"] = np.broadcast_to(np.arange(NSLOT, dtype=np.float32)[None, :], (P, NSLOT))
    c["jnum"] = np.broadcast_to(j.astype(np.float32), (P, NKEY))
    c["unum"] = np.broadcast_to(np.arange(NU, dtype=np.float32)[None, :], (P, NU))
    c["seqeq"] = (p[:, None] == np.arange(B)[None, :]).astype(np.float32)
    c["seqmod"] = (p[:, None] % 4 == np.arange(4)[None, :]).astype(np.float32)
    c["seqdiv"] = (p[:, None] // 4 == np.arange(B // 4)[None, :]).astype(np.float32)
    c["seq32"] = (p[:, None] * 32).astype(np.float32)
    c["wslot"] = np.broadcast_to((16.0 * np.arange(NU - NWR, NU)).astype(np.float32)[None, :], (P, NWR))
    c["sel"] = sel.reshape(P, NBANK * KC * P)
    return c


def chunks(w):
    k = w.shape[0] // P
    return w.reshape(k, P, -1).transpose(1, 0, 2).reshape(P, -1)


def rows(v):
    return np.broadcast_to(v.reshape(1, -1), (P, v.size))


def layout(i):
    f = {}
    x = i["x"]
    f["x_tok"] = chunks(x.reshape(T, D))
    f["x_feat"] = chunks(x.reshape(T, D).T)
    f["mix_table"] = i["L0_cond_weights"].reshape(-1, 32)
    small = dict(constants())
    small["ln_g"], small["ln_b"] = chunks(i["L0_attn_ln_g"][:, None]), chunks(i["L0_attn_ln_b"][:, None])
    for n in ("bq", "bk", "bo"):
        small[n] = chunks(i["L0_attn_" + n][:, None])
    small["bv"] = rows(i["L0_attn_bv"])
    small["temp"] = np.repeat(i["cond_1"].reshape(B // 4, 4), 32, axis=1).T
    small["qscale"], small["kscale"] = rows(i["L1_cond2_q_norm_scale"]), rows(i["L1_cond2_k_norm_scale"])
    small["rbias"] = rows(i["L1_ffn_bias"])
    bw = i["L1_attn_bank_weights"]
    z = np.zeros((P, NBANK), np.float32)
    z[:64] = np.tile(bw, (NBANK, 1))
    small["bw_all"] = z
    z = np.zeros((P, 1), np.float32)
    z[:64, 0] = bw.T.reshape(-1)
    small["bw_own"] = z
    nrm = i["L1_attn_memory_norms"]
    z = np.zeros((P, NH * HD), np.float32)
    z[:64] = np.repeat(nrm.reshape(NBANK, -1), NH, axis=0)
    small["norm_all"] = z
    at, cols = {}, []
    n = 0
    for k, v in small.items():
        at[k] = (n, n + v.shape[1])
        n += v.shape[1]
        cols.append(v)
    f["small"] = np.concatenate(cols, axis=1)
    ints = [np.repeat(i["itok_B_1_198"].reshape(B // 4, 4), 32, axis=1).T,
            np.repeat(i["itok_B_37_3939"].reshape(B // 4, 4), 32, axis=1).T,
            rows(i["itok_B_0_7"])]
    pad = np.zeros((P, 1 + B + NSLOT), i["itok_B_37_3939"].dtype)
    pad[:B, 0] = i["itok_B_37_3939"]
    pad[:, 1:1 + B] = rows(i["itok_B_37_3939"])
    pad[:B, 1 + B:] = i["itok_Bx257_0_4111"]
    chan = np.broadcast_to((np.arange(P) % 32)[:, None], (P, NT)).astype(pad.dtype)
    f["ints"] = np.concatenate(ints + [pad, chan], axis=1)
    f["wA"] = np.concatenate([chunks(i["L0_attn_" + n]) for n in ("Wq", "Wk", "Wv", "Wo")], axis=1)
    f["wB"] = np.concatenate([chunks(i["L1_cond_" + n].T) for n in ("Wq", "Wk", "Wv", "Wo")], axis=1)
    ad = i["L0_cond2_Ag"], i["L0_cond2_Au"], i["L0_cond2_Ad"]
    ag, au, adn = [chunks(a.transpose(1, 0, 2).reshape(a.shape[1], -1)) for a in ad]
    bg, bu, bd = [i["L0_cond2_" + n].reshape(NAD * RANK, -1) for n in ("Bg", "Bu", "Bd")]
    wd = np.concatenate([chunks(i["L0_cond2_Wd"]).reshape(P, HID // P, D), adn.reshape(P, HID // P, P)], axis=2)
    f["wF"] = np.concatenate([ag, au, chunks(i["L0_cond2_Wg"]), chunks(i["L0_cond2_Wu"]), bg, bu,
                              wd.reshape(P, -1), bd], axis=1)
    f["wG"] = np.concatenate([chunks(i["L0_ffn_w_gate"].T), chunks(i["L0_ffn_w_up"].T),
                              chunks(i["L0_ffn_w_down"].T)], axis=1)
    mem = i["L1_attn_memories"]
    bdm = np.zeros((P, NBANK, KC, P), np.float32)
    nrc = np.zeros((P, KC, NBANK * NH), np.float32)
    for h in range(NH):
        c, r = divmod(h * HD, P)
        bdm[r:r + HD, :, c, r:r + HD] = mem[:, h].transpose(1, 0, 2)
        nrc[r:r + HD, c, h::NH] = nrm[:, h].T
    f["wL"] = np.concatenate([chunks(i["L1_attn_Wq"].T), chunks(i["L1_attn_Wo"].T),
                              bdm.reshape(P, -1), nrc.reshape(P, -1)], axis=1)
    wq = i["L1_cond2_Wq"].reshape(GRP, 2, PHD, D).transpose(1, 0, 2, 3).reshape(D, D)
    wo = i["L1_cond2_Wo"].reshape(D, GRP, 2, PHD).transpose(0, 2, 1, 3).reshape(D, D)
    proj = np.concatenate([wq, i["L1_cond2_Wk"], i["L1_cond2_Wv"]], axis=0).T
    f["wP"] = np.concatenate([chunks(proj), chunks(wo.T)], axis=1)
    kv = [i["L1_cond2_" + n].transpose(0, 2, 1, 3).reshape(KVROWS, GRP * PHD) for n in ("k_blocks", "v_blocks")]
    f["cache"] = np.concatenate(kv, axis=1)
    gate = np.concatenate([i["L1_ffn_Wg"].transpose(1, 0, 2).reshape(D, -1), i["L1_ffn_sWg"]], axis=1)
    up = np.concatenate([i["L1_ffn_Wu"].transpose(1, 0, 2).reshape(D, -1), i["L1_ffn_sWu"]], axis=1)
    down = np.concatenate([i["L1_ffn_Wd"].reshape(-1, D), i["L1_ffn_sWd"]], axis=0)
    f["wR"] = chunks(i["L1_ffn_Wr"].T)
    f["wE"] = np.concatenate([chunks(gate), chunks(up), chunks(down)], axis=1)
    return f, at


def program(nc, small_at, x_tok_d, x_feat_d, mix_table, small_d, ints_d, wA_d, wB_d, wF_d, wG_d, wL_d, wP_d,
            cache, wR_d, wE_d, out):
    new_kv = nc.dram_tensor("new_kv", [T, 2 * P], F32).ap()
    route_d = nc.dram_tensor("route", [NE, T], F32).ap()

    with ExitStack() as ctx:
        sems = {}

        def sem(name):
            if name not in sems:
                sems[name] = ctx.enter_context(nc.semaphore(name))
            return sems[name]

        def sb(name, cols, dt=F32):
            return ctx.enter_context(nc.sbuf_tensor(name, [P, cols], dt))

        small = sb("small", small_d.shape[1])
        ints = sb("ints", ints_d.shape[1], I32)
        xT = sb("xT", KC * T)[:, :].rearrange("p (c t) -> p c t", c=KC)
        wbig = sb("wbig", wF_d.shape[1] + wG_d.shape[1])
        wmid = sb("wmid", wA_d.shape[1] + wB_d.shape[1] + wL_d.shape[1])
        wmid_at = nc.sbuf_base - 4 * wmid.shape[1]
        wpage = wbig[:, wE_d.shape[1]:wE_d.shape[1] + wP_d.shape[1]]
        wrt = sb("wrt", wR_d.shape[1])
        work = sb("work", 21504)
        work_at = nc.sbuf_base - 4 * work.shape[1]
        prep = sb("prep", 2048)
        prepi = sb("prepi", 640, I32)
        ps = ctx.enter_context(nc.psum_tensor("ps", [P, 8, 512], F32))

        def const(name):
            a, b = small_at[name]
            return small[:, a:b]

        def cut(t, at, n):
            return t[:, at:at + n]

        ident = const("ident")
        xnT = cut(work, 0, 2048).rearrange("p (c t) -> p c t", c=KC)
        attT = xnT
        yT = cut(work, 2048, 2048).rearrange("p (c t) -> p c t", c=KC)
        kpar = cut(work, 4096, 4096).rearrange("p (c a t) -> p c a t", c=KC, a=2)
        qT = cut(work, 8192, 2048).rearrange("p (c t) -> p c t", c=KC)
        scor = cut(work, 10240, 1536).rearrange("p (r x) -> p r x", r=3)
        prob = cut(work, 11776, 1536).rearrange("p (r x) -> p r x", r=3)
        vpar = cut(work, 13312, 4096).rearrange("p (g a h d) -> p g a h d", g=NT, a=2, h=8)
        pdiag = cut(work, 17408, 4096).rearrange("p (r h q) -> p r h q", r=2, h=NH)
        x_tok = cut(work, 4096, 2048).rearrange("p (g f) -> p g f", g=NT)
        xn_tok = cut(work, 6144, 2048).rearrange("p (g f) -> p g f", g=NT)
        mix_w = cut(work, 8192, 256).rearrange("p (g f) -> p g f", g=NT)

        at = [0]

        def small_buf(n):
            at[0] += n
            return cut(prep, at[0] - n, n)

        stats = small_buf(NT * 6).rearrange("p (g s) -> p g s", g=NT)
        meanvar = small_buf(NT * 2).rearrange("p (g s) -> p g s", g=NT)
        rstd = small_buf(NT)
        ati = [0]

        def int_buf(n):
            ati[0] += n
            return cut(prepi, ati[0] - n, n)

        mix_rows = int_buf(NT)
        admask = small_buf(B)
        temps = small_buf(NT)
        amax = small_buf(NT * NH).rearrange("p (g h) -> p g h", g=NT)
        asum = small_buf(NT * NH).rearrange("p (g h) -> p g h", g=NT)
        arec = small_buf(NT * NH).rearrange("p (g h) -> p g h", g=NT)
        cosb = small_buf(NT * 16).rearrange("p (g f) -> p g f", g=NT)
        sinb = small_buf(NT * 16).rearrange("p (g f) -> p g f", g=NT)
        key_row = small_buf(NGT)
        key_rowi = int_buf(NGT)
        new_row = small_buf(NGT)
        new_rowi = int_buf(NGT)
        thr = small_buf(B)
        coef = small_buf(1)
        rms = small_buf(NT * 12)
        ang = small_buf(NT * 16)
        angk = small_buf(NT * 16)
        angc = small_buf(NT * 16)
        tokpos = small_buf(NT)

        def split_buf(name, base, at, cols):
            return nc.alloc_sbuf_tensor_at(name, [P, cols], F32R, offset=base + 4 * at)[:, :]

        xs = split_buf("x_split", work_at, 13312, 4096).rearrange("p (s c t) -> p s c t", s=2, c=KC)
        gus = split_buf("gate_up_split", work_at, 17408, 2048).rearrange("p (r s m n) -> p r s m n", r=2, s=2, m=4)
        dns = split_buf("down_split", work_at, 19456, 1536).rearrange("p (r s n) -> p r s n", r=2, s=2)
        hs = split_buf("hidden_split", wmid_at, 0, 2048).rearrange("p (r s t) -> p r s t", r=2, s=2)
        THREE = ((0, 0), (0, 1), (1, 0))

        gated = cut(work, 4096, 1024).rearrange("p (r x) -> p r x", r=2)
        hid = cut(work, 5120, 1536).rearrange("p (r x) -> p r x", r=3)
        zlow = cut(work, 6656, 2048).rearrange("p (m t) -> p m t", m=2)
        zdown = cut(work, 8704, 512)
        rawact = cut(work, 6656, 1024).rearrange("p (r x) -> p r x", r=2)
        share = cut(work, 7680, 2048).rearrange("p (r x) -> p r x", r=2)
        ATT_TOTAL = dict(k_done=4, q_done=4, v_done=4, k_kept=8, q_kept=4, v_kept=8, scores_done=2, scaled=NT, max_done=NT,
                         shifted=NT, exp_done=NT, sum_done=NT, rec_done=NT, normed=NT, p_ready=4 * NT, pv_done=NT,
                         o_kept=NT, proj_done=4, out=4)

        class Attention:

            def __init__(self, inp, w_at, in_ready, load, biased, out_to):
                self.inp, self.in_ready, self.load, self.biased, self.out_to = inp, in_ready, load, biased, out_to
                w = cut(wmid, w_at, 2048).rearrange("p (m c o) -> p m c o", m=4, c=KC)
                self.wq, self.wk, self.wv, self.wo = [w[:, m] for m in range(4)]

            def s(self, name):
                return sem("att_" + name)

            def wait(self, engine, name, count):
                engine.wait_ge(self.s(name), count + (0 if self.biased else ATT_TOTAL[name]))

            def tensor(self, pe):
                s, inp = self.s, self.inp
                pe.wait_ge(sem(self.load), 16)
                pe.wait_ge(sem(self.in_ready[0]), self.in_ready[1])
                for c in range(KC):
                    for n in range(2):
                        for k in range(KC):
                            mm = nc.tensor.matmul(ps[:, 2 * c + n, :], self.wk[:, k, c * P:(c + 1) * P],
                                                  inp[:, k, n * HALF:(n + 1) * HALF], start=(k == 0), stop=(k == KC - 1))
                        mm.then_inc(s("k_done"), 1)
                for c in range(KC):
                    for n in range(2):
                        for k in range(KC):
                            mm = nc.tensor.matmul(ps[:, 4 + 2 * c + n, :], self.wq[:, k, c * P:(c + 1) * P],
                                                  inp[:, k, n * HALF:(n + 1) * HALF], start=(k == 0), stop=(k == KC - 1))
                        mm.then_inc(s("q_done"), 1)
                for g in range(NT):
                    if g % 2 == 0:
                        self.wait(pe, "k_kept", 2 * (g // 2) + 2)
                    for k in range(KC):
                        mm = nc.tensor.matmul(ps[:, g // 2, (g % 2) * D:(g % 2 + 1) * D], inp[:, k, g * P:(g + 1) * P],
                                              self.wv[:, k, :], start=(k == 0), stop=(k == KC - 1))
                    if g % 2:
                        mm.then_inc(s("v_done"), 1)
                for hf in range(2):
                    self.wait(pe, "q_kept", 4)
                    self.wait(pe, "k_kept", 8)
                    if hf:
                        self.wait(pe, "v_kept", 8)
                    for g4 in range(4):
                        for c in range(KC):
                            for pr in range(4):
                                for j in range(4):
                                    t0 = (4 * (4 * hf + g4) + j) * S
                                    mm = nc.tensor.matmul(
                                        ps[32 * j:32 * j + 32, 4 * (1 - hf) + pr, (2 * g4 + c) * 64:(2 * g4 + c + 1) * 64],
                                        qT[32 * pr:32 * pr + 32, c, t0:t0 + S], kpar[32 * pr:32 * pr + 32, c, :, t0:t0 + S],
                                        start=True, stop=True)
                    mm.then_inc(s("scores_done"), 1)
                for g in range(NT):
                    self.wait(pe, "p_ready", 4 * (g + 1))
                    if g == 0:
                        self.wait(pe, "scaled", 4)
                        self.wait(pe, "v_kept", 8)
                    if g >= 4:
                        self.wait(pe, "o_kept", g - 3)
                    for c in range(KC):
                        for pr in range(4):
                            for a in range(2):
                                mm = nc.tensor.matmul(ps[32 * pr:32 * pr + 32, 4 + g % 4, c * P:(c + 1) * P],
                                                      vpar[:, g, a, 4 * c + pr, :], pdiag[:, g % 2, 4 * pr + 2 * c + a, :],
                                                      start=(a == 0), stop=(a == 1))
                    mm.then_inc(s("pv_done"), 1)
                self.wait(pe, "o_kept", NT)
                for n in range(2):
                    for c in range(KC):
                        for k in range(KC):
                            mm = nc.tensor.matmul(ps[:, 2 * c + n, :], self.wo[:, k, c * P:(c + 1) * P],
                                                  attT[:, k, n * HALF:(n + 1) * HALF], start=(k == 0), stop=(k == KC - 1))
                        mm.then_inc(s("proj_done"), 1)

            def vector(self, dve):
                s = self.s
                for c in range(KC):
                    for n in range(2):
                        self.wait(dve, "k_done", 2 * c + n + 1)
                        for a in range(2):
                            o = kpar[:, c, a, n * HALF:(n + 1) * HALF]
                            par = const("parity")[:, a:a + 1]
                            if self.biased:
                                nc.vector.tensor_scalar(o, ps[:, 2 * c + n, :], const("bk")[:, c:c + 1], par,
                                                        ALU.add, ALU.mult).then_inc(s("k_kept"), 1)
                            else:
                                nc.vector.tensor_scalar(o, ps[:, 2 * c + n, :], par, None, ALU.mult).then_inc(s("k_kept"), 1)
                dve.wait_ge(sem("zeroed"), 2 if self.biased else 4)
                for i in range(4):
                    self.wait(dve, "v_done", i + 1)
                    v = ps[:, i, :].rearrange("p (g h a d) -> p g h a d", g=2, h=8, a=2)
                    bv = const("bv").rearrange("p (h a d) -> p h a d", h=8, a=2)
                    for a in range(2):
                        if self.biased:
                            for g in range(2):
                                ins = nc.vector.tensor_tensor(vpar[:, 2 * i + g, a, :, a * HD:(a + 1) * HD],
                                                              v[:, g, :, a, :], bv[:, :, a, :], ALU.add)
                            ins.then_inc(s("v_kept"), 1)
                        else:
                            nc.vector.tensor_copy(vpar[:, 2 * i:2 * i + 2, a, :, a * HD:(a + 1) * HD],
                                                  v[:, :, :, a, :]).then_inc(s("v_kept"), 1)

                def up_to_exponent(g):
                    hf, g4, r = g // 4, g % 4, g % 3
                    self.wait(dve, "scores_done", hf + 1)
                    if g >= 3:
                        self.wait(dve, "exp_done", g - 2)
                    scale = 0.25 if self.biased else temps[:, g:g + 1]
                    o = scor[:, r, :].rearrange("p (b x) -> p b x", b=4)
                    nc.vector.scalar_tensor_tensor(o, ps[:, 4 * (1 - hf):4 * (1 - hf) + 4, g4 * P:(g4 + 1) * P], scale,
                                                   const("causal").rearrange("p (b x) -> p b x", b=4),
                                                   ALU.mult, ALU.add).then_inc(s("scaled"), 1)
                    self.wait(dve, "scaled", g + 1)
                    sc = scor[:, r, :].rearrange("p (h k) -> p h k", h=NH)
                    nc.vector.tensor_reduce(amax[:, g, :], sc, AXX, ALU.max).then_inc(s("max_done"), 1)

                def sums(g):
                    r = g % 3
                    self.wait(dve, "exp_done", g + 1)
                    pr = prob[:, r, :].rearrange("p (h k) -> p h k", h=NH)
                    nc.vector.tensor_reduce(asum[:, g, :], pr, AXX, ALU.add).then_inc(s("sum_done"), 1)
                    self.wait(dve, "sum_done", g + 1)
                    nc.vector.reciprocal(arec[:, g, :], asum[:, g, :]).then_inc(s("rec_done"), 1)

                def turn(g):
                    pr = prob[:, g % 3, :].rearrange("p (h k) -> p h k", h=NH)
                    self.wait(dve, "normed", g + 1)
                    if g >= 2:
                        self.wait(dve, "pv_done", g - 1)
                    for j in range(4):
                        q = slice(32 * j, 32 * j + 32)
                        nc.vector.transpose(pdiag[q, g % 2, :, q], pr[q]).then_inc(s("p_ready"), 1)

                for g in range(NT + 2):
                    if g < NT:
                        up_to_exponent(g)
                    if 1 <= g <= NT:
                        sums(g - 1)
                    if g >= 2:
                        turn(g - 2)
                for n in range(2):
                    for c in range(KC):
                        self.wait(dve, "proj_done", 2 * n + c + 1)
                        to = self.out_to[:, c, n * HALF:(n + 1) * HALF]
                        if self.biased:
                            if c == 0 and n == 0:
                                dve.wait_ge(sem("ld_x_feat"), 16)
                            nc.vector.scalar_tensor_tensor(to, ps[:, 2 * c + n, :], const("bo")[:, c:c + 1], to,
                                                           ALU.add, ALU.add).then_inc(s("out"), 1)
                        else:
                            nc.vector.tensor_copy(to, ps[:, 2 * c + n, :]).then_inc(s("out"), 1)

            def scalar(self, act):
                s = self.s
                for c in range(KC):
                    for n in range(2):
                        self.wait(act, "q_done", 2 * c + n + 1)
                        bias = const("bq")[:, c:c + 1] if self.biased else 0.0
                        nc.scalar.activation(qT[:, c, n * HALF:(n + 1) * HALF], ps[:, 4 + 2 * c + n, :], ACT.Identity,
                                             bias=bias).then_inc(s("q_kept"), 1)

                def keep_output(g):
                    self.wait(act, "pv_done", g + 1)
                    nc.scalar.activation(attT[:, :, g * P:(g + 1) * P],
                                         ps[:, 4 + g % 4, 0:D].rearrange("p (c t) -> p c t", c=KC),
                                         ACT.Copy).then_inc(s("o_kept"), 1)

                for g in range(NT):
                    self.wait(act, "shifted", g + 1)
                    if g >= 3:
                        self.wait(act, "p_ready", 4 * (g - 2))
                    nc.scalar.activation(prob[:, g % 3, :], scor[:, g % 3, :], ACT.Exp).then_inc(s("exp_done"), 1)
                    if g >= 3:
                        keep_output(g - 3)
                keep_output(NT - 3)
                keep_output(NT - 2)
                keep_output(NT - 1)

            def gpsimd(self, pool):
                s = self.s
                for g in range(NT + 1):
                    if g < NT:
                        sc = scor[:, g % 3, :].rearrange("p (h k) -> p h k", h=NH)
                        self.wait(pool, "max_done", g + 1)
                        nc.gpsimd.tensor_tensor(sc, sc, amax[:, g, :].unsqueeze(2).to_broadcast([P, NH, S]),
                                                ALU.subtract).then_inc(s("shifted"), 1)
                    if g >= 1:
                        pr = prob[:, (g - 1) % 3, :].rearrange("p (h k) -> p h k", h=NH)
                        self.wait(pool, "rec_done", g)
                        nc.gpsimd.tensor_tensor(pr, pr, arec[:, g - 1, :].unsqueeze(2).to_broadcast([P, NH, S]),
                                                ALU.mult).then_inc(s("normed"), 1)

        class Gated:

            def __init__(self, earlier, inp, gate_up, down, nj, in_ready, load, gu_free, dn_free, lora=None, routed=0,
                         add=False, out_to=None, extra_tensor=None, extra_vector=None, extra_scalar=None,
                         before_vector=None):
                self.earlier, self.inp, self.gate_up, self.down, self.nj = earlier, inp, gate_up, down, nj
                self.in_ready, self.load, self.lora, self.routed = in_ready, load, lora, routed
                self.gu_free, self.dn_free = gu_free, dn_free
                self.add, self.out_to, self.before_vector = add, out_to, before_vector
                self.extra_tensor, self.extra_vector, self.extra_scalar = extra_tensor, extra_vector, extra_scalar
                self.blocks = ([nj - 1] if routed else []) + list(range(nj - 1 if routed else nj))
                self.following = None
                self.early = 0
                if lora:
                    self.units = [(n, p) for n in range(2) for p in range(nj)]
                    self.splits = [j for n in range(2) for j in self.blocks]
                else:
                    self.units = [(n, p) for p in range(nj) for n in range(2)]
                    self.splits = self.blocks
                self.n_units, self.n_splits = len(self.units), len(self.splits)
                self.dn_cols = D + P if lora else D

            def s(self, name):
                return sem("ffn_" + name)

            def count(self, name, n):
                for layer in self.earlier:
                    n += (4 if name in ("out", "x_hi", "x_lo") else
                          layer.n_splits if name in ("gu_hi", "gu_lo", "dn_hi", "dn_lo") else
                          0 if name in ("z_done", "z_ready", "zd_ready", "sum_done", "raw_ready") else layer.n_units)
                return n

            def wait(self, engine, name, n):
                engine.wait_ge(self.s(name), self.count(name, n))

            def acc(self, n, oc):
                return ps[:, oc if self.lora else 2 * n + oc, :]

            def split_of(self, i):
                return i if self.lora else i // 2

            def tensor(self, pe):
                s, inp = self.s, self.inp
                pe.wait_ge(sem(self.load), 16)
                if self.lora:
                    for n in range(2):
                        pe.wait_ge(sem(self.in_ready[0]), self.in_ready[1] + 2 * n + 2)
                        for m in range(2):
                            for k in range(KC):
                                mm = nc.tensor.matmul(ps[:, 4 + 2 * m + n, :], self.lora["first"][m][:, k, :],
                                                      inp[:, k, n * HALF:(n + 1) * HALF], start=(k == 0), stop=(k == KC - 1))
                            mm.then_inc(s("z_done"), 1)

                def gate_up(i):
                    n, p = self.units[i]
                    w = self.split_of(i)
                    self.wait(pe, "gu_lo", w + 1)
                    self.wait(pe, "x_lo", 2 * n + 2)
                    if self.lora:
                        self.wait(pe, "z_ready", 4 if i < 2 else 2 * n + 2)
                    if i >= 2:
                        self.wait(pe, "h_ready", i - 1)
                    for m in range(2):
                        o = ps[:, 4 + 2 * (i % 2) + m, :]
                        for k in range(KC):
                            for a, b in THREE:
                                mm = nc.tensor.matmul(o, gus[:, w % 2, a, 2 * m + k, :], xs[:, b, k, n * HALF:(n + 1) * HALF],
                                                      start=(k == 0 and a == b), stop=(k == KC - 1 and a == 1 and not self.lora))
                        if self.lora:
                            j = self.blocks[p]
                            mm = nc.tensor.matmul(o, self.lora["second"][m][:, j * P:(j + 1) * P],
                                                  zlow[:, m, n * HALF:(n + 1) * HALF], start=False, stop=True)
                        mm.then_inc(s("gate_done" if m == 0 else "up_done"), 1)

                def down(i):
                    n, p = self.units[i]
                    w = self.split_of(i)
                    self.wait(pe, "dn_lo", w + 1)
                    if p == 0 and n == 1:
                        if self.lora:
                            self.wait(pe, "out", 2)
                        elif self.extra_tensor:
                            pe.wait_ge(sem("route_kept"), 2)
                    self.wait(pe, "h_hi", i + 1)
                    cols = [(self.acc(n, oc), slice(oc * P, (oc + 1) * P), not self.lora) for oc in range(KC)]
                    if self.lora:
                        cols.append((ps[:, 2, :], slice(D, D + P), True))
                    for o, c, closes in cols:
                        for a in range(2):
                            nc.tensor.matmul(o, dns[:, w % 2, a, c], hs[:, i % 2, 0, :], start=(p == 0 and a == 0), stop=False)
                    self.wait(pe, "h_lo", i + 1)
                    for o, c, closes in cols:
                        mm = nc.tensor.matmul(o, dns[:, w % 2, 0, c], hs[:, i % 2, 1, :], start=False,
                                              stop=(p == self.nj - 1 and closes))
                    mm.then_inc(s("down_done"), 1)

                def adapters(n):
                    self.wait(pe, "zd_ready", n + 1)
                    for oc in range(KC):
                        mm = nc.tensor.matmul(self.acc(n, oc), self.lora["down_second"][:, oc * P:(oc + 1) * P],
                                              zdown[:, :], start=False, stop=True)
                    mm.then_inc(s("sum_done"), 1)

                for i in range(self.n_units):
                    gate_up(i)
                    if self.extra_tensor:
                        self.extra_tensor(pe, i)
                    if self.lora and i == self.nj + 1:
                        adapters(0)
                    if i >= 1:
                        down(i - 1)
                down(self.n_units - 1)
                if self.lora:
                    adapters(1)

            def x_split_vector(self, dve, n):
                s = self.s
                h = slice(n * HALF, (n + 1) * HALF)
                for c in range(KC):
                    self.wait(dve, "x_hi", 2 * n + c + 1)
                    nc.vector.tensor_tensor(xs[:, 1, c, h], self.inp[:, c, h], xs[:, 0, c, h].bitcast(F32),
                                            ALU.subtract).then_inc(s("x_lo"), 1)

            def x_split_scalar(self, act, n):
                h = slice(n * HALF, (n + 1) * HALF)
                for c in range(KC):
                    act.wait_ge(sem(self.in_ready[0]), self.in_ready[1] + 2 * n + c + 1)
                    nc.scalar.activation(xs[:, 0, c, h], self.inp[:, c, h], ACT.Copy).then_inc(self.s("x_hi"), 1)

            def keep_sums(self, dve, n):
                s = self.s
                if self.lora:
                    self.wait(dve, "sum_done", n + 1)
                else:
                    self.wait(dve, "down_done", self.n_units - 1 + n)
                for oc in range(KC):
                    to = self.out_to[:, oc, n * HALF:(n + 1) * HALF]
                    if self.add:
                        nc.vector.tensor_tensor(to, self.acc(n, oc), to, ALU.add).then_inc(s("out"), 1)
                    else:
                        nc.vector.tensor_copy(to, self.acc(n, oc)).then_inc(s("out"), 1)

            def keep_adapters(self, dve, n):
                s = self.s
                self.wait(dve, "down_done", self.nj * (n + 1))
                nc.vector.tensor_tensor(zdown[:, :].rearrange("p (b t) -> p b t", t=S),
                                        ps[:, 2, :].rearrange("p (b t) -> p b t", t=S),
                                        admask[:, 16 * n:16 * n + 16].unsqueeze(2).to_broadcast([P, 16, S]),
                                        ALU.mult).then_inc(s("zd_ready"), 1)

            def vector(self, dve):
                s = self.s
                for n in range(2):
                    if n >= self.early:
                        self.x_split_vector(dve, n)
                    if self.lora:
                        for m in range(2):
                            self.wait(dve, "z_done", 2 * n + m + 1)
                            nc.vector.tensor_tensor(
                                zlow[:, m, n * HALF:(n + 1) * HALF].rearrange("p (b t) -> p b t", t=S),
                                ps[:, 4 + 2 * m + n, :].rearrange("p (b t) -> p b t", t=S),
                                admask[:, 16 * n:16 * n + 16].unsqueeze(2).to_broadcast([P, 16, S]),
                                ALU.mult).then_inc(s("z_ready"), 1)
                if self.before_vector:
                    self.before_vector(dve)
                for i in range(self.n_units):
                    self.wait(dve, "up_done", i + 1)
                    self.wait(dve, "act_ready", i + 1)
                    nc.vector.tensor_tensor(hid[:, i % 3, :], ps[:, 5 + 2 * (i % 2), :], gated[:, i % 2, :],
                                            ALU.mult).then_inc(s("h_ready"), 1)
                    if self.lora and i == self.nj + 1:
                        self.keep_sums(dve, 0)
                    self.wait(dve, "h_hi", i + 1)
                    nc.vector.tensor_tensor(hs[:, i % 2, 1, :], hid[:, i % 3, :], hs[:, i % 2, 0, :].bitcast(F32),
                                            ALU.subtract).then_inc(s("h_lo"), 1)
                    if self.lora and i == self.nj:
                        self.keep_adapters(dve, 0)
                    if self.following and i == self.nj + 2:
                        self.following.x_split_vector(dve, 0)
                    if self.extra_vector:
                        self.extra_vector(dve, i)
                if self.lora:
                    self.keep_adapters(dve, 1)
                else:
                    self.keep_sums(dve, 0)
                self.keep_sums(dve, 1)

            def split_gate_up(self, act, k):
                s, j = self.s, self.splits[k]
                if k >= 2:
                    self.wait(act, "up_done", k - 1 if self.lora else 2 * k - 2)
                nc.scalar.activation(gus[:, k % 2, 0], self.gate_up[:, :, j * P:(j + 1) * P], ACT.Copy)\
                    .then_inc(s("gu_hi"), 1)

            def split_down(self, act, k):
                s, j = self.s, self.splits[k]
                if k >= 2:
                    self.wait(act, "down_done", k - 1 if self.lora else 2 * k - 2)
                nc.scalar.activation(dns[:, k % 2, 0, 0:self.dn_cols], self.down[:, j, :], ACT.Copy).then_inc(s("dn_hi"), 1)

            def schedule(self, i):
                if self.lora:
                    gu, dn = i + 2, i + 1
                else:
                    gu, dn = (i // 2 + 1, None) if i % 2 == 0 else (None, i // 2 + 1)
                keep = lambda k: k if k is not None and k < self.n_splits else None
                return keep(gu), keep(dn)

            def first_splits(self):
                return (0, 1) if self.lora else (0,)

            def scalar(self, act):
                s = self.s
                act.wait_ge(sem(self.load), 16)
                act.wait_ge(sem(self.gu_free[0]), self.gu_free[1])
                for k in self.first_splits():
                    self.split_gate_up(act, k)
                act.wait_ge(sem(self.dn_free[0]), self.dn_free[1])
                self.split_down(act, 0)
                for n in range(self.early, 2):
                    self.x_split_scalar(act, n)
                if self.routed:
                    route_scalar(act)
                for i, (n, p) in enumerate(self.units):
                    self.wait(act, "gate_done", i + 1)
                    if i >= 2:
                        self.wait(act, "h_ready", i - 1)
                    routed = self.routed and p > 0
                    dst = rawact[:, i % 2, :] if routed else gated[:, i % 2, :]
                    nc.scalar.activation(dst, ps[:, 4 + 2 * (i % 2), :], ACT.Silu).then_inc(
                        s("raw_ready" if routed else "act_ready"), 1)
                    gu, dn = self.schedule(i)
                    if gu is not None:
                        self.split_gate_up(act, gu)
                    self.wait(act, "h_ready", i + 1)
                    if i >= 2:
                        self.wait(act, "down_done", i - 1)
                    nc.scalar.activation(hs[:, i % 2, 0, :], hid[:, i % 3, :], ACT.Copy).then_inc(s("h_hi"), 1)
                    if dn is not None:
                        self.split_down(act, dn)
                    if self.following and i == self.nj + 2:
                        self.following.x_split_scalar(act, 0)
                    if self.extra_scalar:
                        self.extra_scalar(act, i)

            def lo_gate_up(self, pool, k):
                s, j = self.s, self.splits[k]
                self.wait(pool, "gu_hi", k + 1)
                nc.gpsimd.tensor_tensor(gus[:, k % 2, 1], self.gate_up[:, :, j * P:(j + 1) * P],
                                        gus[:, k % 2, 0].bitcast(F32), ALU.subtract).then_inc(s("gu_lo"), 1)

            def lo_down(self, pool, k):
                s, j = self.s, self.splits[k]
                self.wait(pool, "dn_hi", k + 1)
                nc.gpsimd.tensor_tensor(dns[:, k % 2, 1, 0:self.dn_cols], self.down[:, j, :],
                                        dns[:, k % 2, 0, 0:self.dn_cols].bitcast(F32), ALU.subtract).then_inc(s("dn_lo"), 1)

            def gpsimd(self, pool):
                s = self.s
                pool.wait_ge(sem(self.load), 16)
                for k in self.first_splits():
                    self.lo_gate_up(pool, k)
                self.lo_down(pool, 0)
                for i, (n, p) in enumerate(self.units):
                    if self.routed and p > 0:
                        e = p - 1
                        if n == 0:
                            pool.wait_ge(sem(f"share{e % 2}"), 16 * (e // 2 + 1))
                        self.wait(pool, "raw_ready", i - 1)
                        self.wait(pool, "h_ready", i - 1)
                        nc.gpsimd.tensor_tensor(gated[:, i % 2, :], rawact[:, i % 2, :],
                                                share[:, e % 2, n * HALF:(n + 1) * HALF], ALU.mult)\
                            .then_inc(s("act_ready"), 1)
                    gu, dn = self.schedule(i)
                    if gu is not None:
                        self.lo_gate_up(pool, gu)
                    if dn is not None:
                        self.lo_down(pool, dn)

        tmp_at = [9216]

        def tmp(n, rows=B):
            tmp_at[0] += n
            return work[0:rows, tmp_at[0] - n:tmp_at[0]]

        tab, first, tw, ulen, base, rr = tmp(NSLOT), tmp(NU), tmp(NU), tmp(1), tmp(1), tmp(1)
        upos, ublk, uoff, krow = tmp(NKEY), tmp(NKEY), tmp(NKEY), tmp(NKEY)
        eq_at = tmp_at[0]
        eq = tmp(NU * NKEY).rearrange("p (s j) -> p s j", s=NU)
        last32 = tmp(P).rearrange("p (q j) -> p q j", q=4)
        spread = tmp(3 * B * NWR).rearrange("p (k b s) -> p k b s", k=3, b=B)
        t0w, b16, wlo, whi, wval, wtm = tmp(NWR), tmp(NWR), tmp(NWR), tmp(NWR), tmp(NWR), tmp(NWR)
        writer = tmp(3 * B * NWR, P).rearrange("p (k x) -> p k x", k=3)
        wbest = tmp(NGT, P)
        wneg = tmp(NGT, P)
        WT = 5
        m1 = work[:, eq_at:eq_at + WT * B * NWR].rearrange("p (i x) -> p i x", i=WT)
        m2 = work[:, eq_at + WT * B * NWR:eq_at + 2 * WT * B * NWR].rearrange("p (i x) -> p i x", i=WT)
        assert tmp_at[0] <= 13312 and 2 * WT * B * NWR <= NU * NKEY
        basei, uposi, ublki = int_buf(2), int_buf(NKEY), int_buf(NKEY)
        len_b = ints[0:B, 16 + B:17 + B]
        tab_b = ints[0:B, 17 + 2 * B:17 + 2 * B + NSLOT]

        def row(name, n=None):
            c = const(name)[0:B, :]
            return c if n is None else c[:, 0:n]

        def prep_steps(dve):
            ts, tt, stt = nc.vector.tensor_scalar, nc.vector.tensor_tensor, nc.vector.scalar_tensor_tensor

            yield lambda: ts(ulen, len_b, float(1 - WIN), None, ALU.add)
            yield lambda: ts(basei[0:B, 0:1], len_b, float(1 - WIN), None, ALU.add)
            yield lambda: ts(basei[0:B, 1:2], basei[0:B, 0:1], 4, None, ALU.arith_shift_right)
            yield lambda: nc.vector.tensor_copy(base, basei[0:B, 1:2])
            yield lambda: stt(rr, base, -16.0, ulen, ALU.mult, ALU.add)
            yield lambda: nc.vector.tensor_copy(tab, tab_b)
            yield lambda: ts(first, row("unum"), base, 0.0, ALU.add, ALU.max)
            yield lambda: ts(first, first, float(NSLOT - 1), None, ALU.min)
            for u in range(NU):
                yield lambda u=u: stt(eq[:, 0:2, :].rearrange("p a b -> p (a b)")[:, 0:NSLOT], row("slots"),
                                      first[:, u:u + 1], tab, ALU.is_equal, ALU.mult, accum_out=tw[:, u:u + 1])
            yield lambda: ts(upos, row("jnum"), rr, None, ALU.add)
            yield lambda: nc.vector.tensor_copy(uposi[0:B], upos)
            yield lambda: ts(ublki[0:B], uposi[0:B], 4, None, ALU.arith_shift_right)
            yield lambda: nc.vector.tensor_copy(ublk, ublki[0:B])
            yield lambda: stt(uoff, ublk, -16.0, upos, ALU.mult, ALU.add)
            yield lambda: tt(eq, ublk.unsqueeze(1).to_broadcast([B, NU, NKEY]),
                             row("unum").unsqueeze(2).to_broadcast([B, NU, NKEY]), ALU.is_equal)
            yield lambda: tt(eq, eq, tw.unsqueeze(2).to_broadcast([B, NU, NKEY]), ALU.mult)
            yield lambda: nc.vector.tensor_reduce(krow, eq.rearrange("p s j -> p j s"), AXX, ALU.add)
            yield lambda: stt(krow, krow, 16.0, uoff, ALU.mult, ALU.add)
            yield lambda: ts(t0w, row("wslot"), rr, float(1 - WIN), ALU.subtract, ALU.add)
            yield lambda: ts(b16, tw[:, NU - NWR:NU], 16.0, None, ALU.mult)
            yield lambda: ts(wtm, t0w, -1.0, 0.0, ALU.mult, ALU.max)
            yield lambda: tt(wlo, b16, wtm, ALU.add)
            yield lambda: ts(wtm, t0w, -1.0, float(S - 1), ALU.mult, ALU.add)
            yield lambda: ts(wtm, wtm, float(BLK - 1), None, ALU.min)
            yield lambda: tt(whi, b16, wtm, ALU.add)
            yield lambda: ts(wval, t0w, row("seq32", 1), 1.0 + BIG, ALU.add, ALU.add)
            yield lambda: tt(wval, wval, b16, ALU.subtract)
            for k, v in enumerate((wlo, whi, wval)):
                yield lambda k=k, v=v: tt(spread[:, k], v.unsqueeze(1).to_broadcast([B, B, NWR]),
                                          row("seqeq").unsqueeze(2).to_broadcast([B, B, NWR]), ALU.mult)
            yield lambda: tt(last32, krow[:, P:NKEY].unsqueeze(1).to_broadcast([B, 4, S]),
                             row("seqmod").unsqueeze(2).to_broadcast([B, 4, S]), ALU.mult)

            def from_tensor():
                dve.wait_ge(sem("prep_spread"), 1)
                return nc.vector.tensor_copy(key_row, ps[:, 3, 0:NGT])
            yield from_tensor
            yield lambda: nc.vector.tensor_copy(writer, ps[:, 3, 64:64 + 3 * B * NWR].rearrange("p (k x) -> p k x", k=3))
            yield lambda: nc.vector.tensor_copy(key_rowi, key_row)
            for i in range(0, NGT, WT):
                shape = [P, WT, B * NWR]
                keys = key_row[:, i:i + WT].unsqueeze(2).to_broadcast(shape)
                lo, hi, val = [writer[:, k].unsqueeze(1).to_broadcast(shape) for k in range(3)]
                yield lambda lo=lo, keys=keys: tt(m1, lo, keys, ALU.is_le)
                yield lambda hi=hi, keys=keys: tt(m2, hi, keys, ALU.is_ge)
                yield lambda: tt(m1, m1, m2, ALU.mult)
                yield lambda val=val: tt(m1, m1, val, ALU.mult)
                yield lambda i=i: nc.vector.tensor_reduce(wbest[:, i:i + WT], m1, AXX, ALU.max)
            yield lambda: stt(wbest, wbest, -(BIG + 1.0), key_row, ALU.add, ALU.add)
            yield lambda: ts(wneg, wbest, 0.0, float(2 ** 20), ALU.is_lt, ALU.mult)
            yield lambda: tt(new_row, wbest, wneg, ALU.add)
            yield lambda: nc.vector.tensor_copy(new_rowi, new_row)
            yield lambda: ts(thr, ints[:, 17 + B:17 + 2 * B], -STEP, float(WIN - 1) * STEP, ALU.mult, ALU.add)
            yield lambda: ts(tokpos, ints[:, NT:2 * NT], const("tok"), None, ALU.add)
            a3, k3 = [x.rearrange("p (g f) -> p g f", g=NT) for x in (ang, angk)]
            yield lambda: tt(a3, tokpos.unsqueeze(2).to_broadcast([P, NT, 16]),
                             const("inv").unsqueeze(1).to_broadcast([P, NT, 16]), ALU.mult)
            yield lambda: ts(angk, ang, 1.0 / (2 * PI), 12582912.0, ALU.mult, ALU.add)
            yield lambda: ts(angk, angk, -12582912.0, None, ALU.add)
            c1 = 6.28125
            c2 = float(np.float32(np.float16(2 * np.pi - c1)))
            for c in (c1, c2, 2 * np.pi - c1 - c2):
                yield lambda c=c: stt(ang, angk, -float(c), ang, ALU.mult, ALU.add)
            yield lambda: ts(angc, ang, PI / 2, None, ALU.add)
            yield lambda: ts(angk, angc, PI, -2 * PI, ALU.is_gt, ALU.mult)
            yield lambda: tt(angc, angc, angk, ALU.add)
            lim = float(np.nextafter(np.float32(np.pi), np.float32(0)))
            yield lambda: ts(angc, angc, lim, -lim, ALU.min, ALU.max)
            yield lambda: ts(ang, ang, lim, -lim, ALU.min, ALU.max)
            nb = slice(0, NBANK * NH)
            bw, own = const("bw_all")[nb], const("bw_own")[nb]
            cmx, cex, cso, cown = [rms[nb, i:i + 1] for i in range(4)]
            c4 = rms[nb, 8:12]
            yield lambda: nc.vector.tensor_reduce(cmx, bw, AXX, ALU.max)
            yield lambda: ts(c4, bw, cmx, None, ALU.subtract)
            yield lambda: ts(cown, own, cmx, None, ALU.subtract)

        N_PREP = sum(1 for _ in prep_steps(None))
        N_SPREAD = 8 + NU + 9 + 9 + 4
        PREP_A = 5

        def prep_run(dve):
            steps = prep_steps(dve)
            done = [0]

            def run(n):
                for _ in range(n):
                    step = next(steps, None)
                    if step is None:
                        return
                    if done[0] == 0:
                        dve.wait_ge(sem("ld_ints"), 16)
                    else:
                        dve.wait_ge(sem("prep_step"), done[0])
                    step().then_inc(sem("prep_step"), 1)
                    done[0] += 1
            return run

        bdm = cut(wmid, 4096 + 1024, NBANK * KC * P).rearrange("p (n c e) -> p n c e", n=NBANK, c=KC)
        lin_wq = cut(wmid, 4096, 512).rearrange("p (c o) -> p c o", c=KC)
        lin_wo = cut(wmid, 4096 + 512, 512).rearrange("p (c o) -> p c o", c=KC)
        nrc = cut(wmid, 4096 + 2048, KC * NBANK * NH).rearrange("p (c m) -> p c m", c=KC)
        sel = const("sel").rearrange("p (n c o) -> p n c o", n=NBANK, c=KC)
        sig = cut(work, 4096, 2048).rearrange("p (c t) -> p c t", c=KC)
        sigq = cut(work, 6144, 2048).rearrange("p (r t) -> p r t", r=4)
        comb = cut(work, 8192, 2048).rearrange("p (c t) -> p c t", c=KC)
        neg = cut(work, 0, 1024).rearrange("p (r t) -> p r t", r=2)
        expo = cut(work, 1024, 1024).rearrange("p (r t) -> p r t", r=2)
        rnorm = work[0:NBANK * NH, 10240:11264]
        sel_r = split_buf("select", wmid_at, 0, 1024).rearrange("p (n c o) -> p n c o", n=NBANK, c=KC)
        rnorms = split_buf("shares_split", work_at, 2048, 2048).rearrange("p (s t) -> p s t", s=2)
        LIN = [(c, n) for c in range(KC) for n in range(2)]
        MEM = [(m, n, c) for m in range(NBANK) for n in range(2) for c in range(KC)]

        def lin_tensor(pe):
            pe.wait_ge(sem("ld_wL"), 16)
            pe.wait_ge(sem("att_out"), 2 * ATT_TOTAL["out"])
            for u, (c, n) in enumerate(LIN):
                for k in range(KC):
                    mm = nc.tensor.matmul(ps[:, 4 + u, :], lin_wq[:, k, c * P:(c + 1) * P],
                                          yT[:, k, n * HALF:(n + 1) * HALF], start=(k == 0), stop=(k == KC - 1))
                mm.then_inc(sem("lin_q"), 1)
            pe.wait_ge(sem("lin_sig"), 4)
            for n in range(2):
                for c in range(KC):
                    mm = nc.tensor.matmul(ps[0:NBANK * NH, n, :], nrc[:, c, :], sig[:, c, n * HALF:(n + 1) * HALF],
                                          start=(c == 0), stop=(c == KC - 1))
                mm.then_inc(sem("lin_norm"), 1)

            def memories(u):
                m, n, c = MEM[u]
                pe.wait_ge(sem("lin_scaled"), u + 1)
                nc.tensor.matmul(ps[:, 2 * c + n, :], bdm[:, m, c, :], sigq[:, u % 4, :],
                                 start=(m == 0), stop=(m == NBANK - 1)).then_inc(sem("lin_mem"), 1)

            pe.wait_ge(sem("sel_ready"), 1)
            pe.wait_ge(sem("lin_share"), 2)
            for u, (m, n, c) in enumerate(MEM):
                if u >= 4:
                    pe.wait_ge(sem("lin_scaled"), u - 3)
                for part in range(2):
                    mm = nc.tensor.matmul(ps[:, 4 + u % 4, :], sel_r[0:NBANK * NH, m, c, :],
                                          rnorms[0:NBANK * NH, part, n * HALF:(n + 1) * HALF],
                                          start=(part == 0), stop=(part == 1))
                mm.then_inc(sem("lin_spread"), 1)
                if u >= 2:
                    memories(u - 2)
            memories(len(MEM) - 2)
            memories(len(MEM) - 1)
            pe.wait_ge(sem("lin_comb"), 4)
            for u, (c, n) in enumerate(LIN):
                for k in range(KC):
                    mm = nc.tensor.matmul(ps[:, 4 + u, :], lin_wo[:, k, c * P:(c + 1) * P],
                                          comb[:, k, n * HALF:(n + 1) * HALF], start=(k == 0), stop=(k == KC - 1))
                mm.then_inc(sem("lin_proj"), 1)

        def lin_vector(dve):
            nb = slice(0, NBANK * NH)
            c4, csum, cactive = rms[nb, 8:12], rms[nb, 4:5], rms[nb, 5:6]
            dve.wait_ge(sem("lin_cexp"), 2)
            nc.vector.tensor_reduce(csum, c4, AXX, ALU.add).then_inc(sem("lin_coef"), 1)
            nc.vector.tensor_reduce(cactive, const("norm_all")[nb], AXX, ALU.add).then_inc(sem("lin_coef"), 1)
            dve.wait_ge(sem("lin_coef"), 2)
            nc.vector.reciprocal(rms[nb, 6:7], csum).then_inc(sem("lin_coef"), 1)
            nc.vector.tensor_scalar(cactive, cactive, 1e-6, None, ALU.is_ge).then_inc(sem("lin_coef"), 1)
            dve.wait_ge(sem("lin_coef"), 4)
            nc.vector.scalar_tensor_tensor(coef[nb], rms[nb, 6:7], cactive, rms[nb, 3:4], ALU.mult,
                                           ALU.mult).then_inc(sem("lin_coef"), 1)

            def sigma(u):
                c, n = LIN[u]
                dve.wait_ge(sem("lin_exp"), u + 1)
                nc.vector.scalar_tensor_tensor(sig[:, c, n * HALF:(n + 1) * HALF], ps[:, 4 + u, :], 0.0,
                                               expo[:, u % 2, :], ALU.max, ALU.add).then_inc(sem("lin_sig"), 1)

            for u in range(4):
                dve.wait_ge(sem("lin_q"), u + 1)
                if u >= 2:
                    dve.wait_ge(sem("lin_exp"), u - 1)
                nc.vector.tensor_scalar(neg[:, u % 2, :], ps[:, 4 + u, :], 0.0, None, ALU.min).then_inc(sem("lin_neg"), 1)
                if u >= 1:
                    sigma(u - 1)
            sigma(3)
            for n in range(2):
                h = slice(n * HALF, (n + 1) * HALF)
                dve.wait_ge(sem("lin_norm"), n + 1)
                nc.vector.tensor_scalar(rnorm[:, h], ps[nb, n, :], 1e-6, None, ALU.max).then_inc(sem("lin_clip"), 1)
                dve.wait_ge(sem("lin_clip"), n + 1)
                nc.vector.reciprocal(rnorm[:, h], rnorm[:, h]).then_inc(sem("lin_rec"), 1)
                dve.wait_ge(sem("lin_rec"), n + 1)
                dve.wait_ge(sem("lin_coef"), 5)
                nc.vector.tensor_scalar(rnorm[:, h], rnorm[:, h], coef[nb], None, ALU.mult).then_inc(sem("lin_scale"), 1)
                dve.wait_ge(sem("lin_hi"), n + 1)
                nc.vector.tensor_tensor(rnorms[nb, 1, h], rnorm[:, h], rnorms[nb, 0, h].bitcast(F32), ALU.subtract)\
                    .then_inc(sem("lin_share"), 1)
            for u, (m, n, c) in enumerate(MEM):
                dve.wait_ge(sem("lin_spread"), u + 1)
                if u >= 4:
                    dve.wait_ge(sem("lin_mem"), u - 3)
                nc.vector.tensor_tensor(sigq[:, u % 4, :], ps[:, 4 + u % 4, :], sig[:, c, n * HALF:(n + 1) * HALF],
                                        ALU.mult).then_inc(sem("lin_scaled"), 1)
            for u, (c, n) in enumerate(LIN):
                dve.wait_ge(sem("lin_proj"), u + 1)
                to = xT[:, c, n * HALF:(n + 1) * HALF]
                nc.vector.tensor_tensor(to, ps[:, 4 + u, :], to, ALU.add).then_inc(sem("lin_out"), 1)

        def lin_scalar(act):
            nb = slice(0, NBANK * NH)
            act.wait_ge(sem("prep_step"), N_PREP)
            nc.scalar.activation(rms[nb, 8:12], rms[nb, 8:12], ACT.Exp).then_inc(sem("lin_cexp"), 1)
            nc.scalar.activation(rms[nb, 3:4], rms[nb, 3:4], ACT.Exp).then_inc(sem("lin_cexp"), 1)
            for u in range(4):
                act.wait_ge(sem("lin_neg"), u + 1)
                if u >= 2:
                    act.wait_ge(sem("lin_sig"), u - 1)
                nc.scalar.activation(expo[:, u % 2, :], neg[:, u % 2, :], ACT.Exp).then_inc(sem("lin_exp"), 1)
            for n in range(2):
                h = slice(n * HALF, (n + 1) * HALF)
                act.wait_ge(sem("lin_scale"), n + 1)
                nc.scalar.activation(rnorms[nb, 0, h], rnorm[:, h], ACT.Copy).then_inc(sem("lin_hi"), 1)
            act.wait_ge(sem("lin_mem"), len(MEM))
            for u, (c, n) in enumerate(LIN):
                nc.scalar.activation(comb[:, c, n * HALF:(n + 1) * HALF], ps[:, 2 * c + n, :],
                                     ACT.Copy).then_inc(sem("lin_comb"), 1)

        qmask = cut(work, 0, 8192).rearrange("p (b g h t) -> p b g h t", b=B, g=GRP, h=2)
        newkv = cut(work, 8192, 2048).rearrange("p (g f) -> p g f", g=NT)
        kTs = [cut(work, a, 640).rearrange("p (b j) -> p b j", b=4) for a in (10240, 8192)]
        kv = cut(work, 11264, NGT * 256).rearrange("p (i f) -> p i f", i=NGT)
        raw = cut(wmid, 0, 3072).rearrange("p (g k f) -> p g k f", g=NT, k=12)
        qtok = cut(wmid, 3072, 2048).rearrange("p (g f) -> p g f", g=NT)
        rot = cut(wmid, 5120, 768).rearrange("p (m k f) -> p m k f", m=4, k=12)
        sqr = cut(work, 0, 3072).rearrange("p (g f) -> p g f", g=NT)
        pT = cut(wmid, 0, 1024).rearrange("p (b a q) -> p b a q", b=4, a=2)
        plast = cut(wmid, 1024, 256).rearrange("p (a b j) -> p a b j", a=2, b=4)
        plastT = cut(wmid, 1280, 1024).rearrange("p (a b q) -> p a b q", a=2, b=4)
        psc = cut(wmid, 2304, 640).rearrange("p (r a j) -> p r a j", r=2, a=2)
        pex = cut(wmid, 5120, 640).rearrange("p (r a j) -> p r a j", r=2, a=2)
        pmk = cut(wmid, 5888, 320).rearrange("p (r j) -> p r j", r=2)
        pst = small_buf(B * 6).rearrange("p (b x) -> p b x", b=B)
        oT = cut(wmid, 3072, 2048).rearrange("p (h t) -> p h t", h=2)
        cT = cut(work, 0, 2048).rearrange("p (c t) -> p c t", c=KC)
        page_w = cut(wpage, 0, 1024).rearrange("p (c o) -> p c o", c=KC)
        page_wo = cut(wpage, 1024, 512).rearrange("p (c o) -> p c o", c=KC)
        gsc = small_buf(KC * PHD).rearrange("p (a f) -> p a f", a=2)

        ROT_DVE = 5
        rot_pool = cut(work, 3072, 768).rearrange("p (m k f) -> p m k f", m=4, k=12)

        def rotate(eng, unit, tiles, rot, tag):
            tt = unit.tensor_tensor
            eng.wait_ge(sem("page_ms"), NT + 2)
            eng.wait_ge(sem("page_gain"), 2)
            eng.wait_ge(sem("rope_ready"), 2)
            for i, g in enumerate(tiles):
                eng.wait_ge(sem("page_raw"), 3 * g + 3)
                x = raw[:, g]
                tt(x, x, rms[:, 12 * g:12 * g + 12].unsqueeze(2).to_broadcast([P, 12, PHD]), ALU.mult)\
                    .then_inc(sem(tag + "_unit"), 1)
                eng.wait_ge(sem(tag + "_unit"), i + 1)
                tt(x[:, 0:8], x[:, 0:8], gsc[:, 0:1, :].to_broadcast([P, 8, PHD]), ALU.mult)\
                    .then_inc(sem(tag + "_gained"), 1)
                tt(x[:, 8:12], x[:, 8:12], gsc[:, 1:2, :].to_broadcast([P, 4, PHD]), ALU.mult)\
                    .then_inc(sem(tag + "_gained"), 1)
                eng.wait_ge(sem(tag + "_gained"), 2 * i + 2)
                if i:
                    eng.wait_ge(sem(tag + "_rot"), 4 * i)
                cb, sb_ = [t[:, g:g + 1, :].to_broadcast([P, 12, 16]) for t in (cosb, sinb)]
                lo, hi = x[:, :, 0:16], x[:, :, 16:32]
                for m, (a, w) in enumerate(((lo, cb), (hi, sb_), (hi, cb), (lo, sb_))):
                    tt(rot[:, m], a, w, ALU.mult).then_inc(sem(tag + "_rmul"), 1)
                eng.wait_ge(sem(tag + "_rmul"), 4 * i + 4)
                q = qtok[:, g, :].rearrange("p (k f) -> p k f", k=8)
                k = newkv[:, g, 0:P].rearrange("p (k f) -> p k f", k=4)
                for o, s0, s1 in ((q, 0, 8), (k, 8, 12)):
                    tt(o[:, :, 0:16], rot[:, 0, s0:s1], rot[:, 1, s0:s1], ALU.subtract).then_inc(sem(tag + "_rot"), 1)
                    tt(o[:, :, 16:32], rot[:, 2, s0:s1], rot[:, 3, s0:s1], ALU.add).then_inc(sem(tag + "_rot"), 1)

        def wait_rotated(eng, g):
            if g < ROT_DVE:
                eng.wait_ge(sem("page_rot"), 4 * (g + 1))
            else:
                eng.wait_ge(sem("pagepool_rot"), 4 * (g - ROT_DVE + 1))

        def page_tensor(pe):
            pe.wait_ge(sem("ld_wP"), 16)
            pe.wait_ge(sem("lin_out"), 4)
            for g in range(NT):
                for k in range(KC):
                    mm = nc.tensor.matmul(ps[:, g, :], xT[:, k, g * P:(g + 1) * P], page_w[:, k, :],
                                          start=(k == 0), stop=(k == KC - 1))
                mm.then_inc(sem("page_proj"), 1)
            for hh in range(2):
                for g in range(NT):
                    wait_rotated(pe, g)
                    pe.wait_ge(sem("page_raw"), 3 * NT)
                    tr = nc.tensor.transpose(ps[:, 2 * hh + g // 4, (g % 4) * P:(g % 4 + 1) * P],
                                             qtok[:, g, hh * P:(hh + 1) * P], ident)
                    if g % 4 == 3:
                        tr.then_inc(sem("page_qt"), 1)
            pe.wait_ge(sem("page_qm"), 16)

            def keys(q4):
                pe.wait_ge(sem(f"overlay{q4}"), 16 * 5)
                if q4:
                    pe.wait_ge(sem("page_kT"), 2 * q4)
                for j in range(4):
                    nc.tensor.transpose(ps[:, 0, j * P:(j + 1) * P], kv[:, 4 * q4 + j, 0:P], ident)
                nc.tensor.transpose(ps[:, 1, 0:P], kv[:, B + q4, 0:P], ident).then_inc(sem("page_k"), 1)

            def scores(b):
                pe.wait_ge(sem("page_kT"), 2 * (b // 4) + 2)
                if b >= 2:
                    pe.wait_ge(sem("page_scaled"), b - 1)
                for a in range(2):
                    mm = nc.tensor.matmul(ps[:, 2 + b % 2, a * NKEY:(a + 1) * NKEY],
                                          qmask[:, b, 2 * a:2 * a + 2, :, :].rearrange("p g h t -> p (g h t)"),
                                          kTs[b // 4 % 2][:, b % 4, :], start=True, stop=True)
                mm.then_inc(sem("page_scores"), 1)

            def turn(b):
                pe.wait_ge(sem("page_norm"), 2 * (b + 1))
                if b >= 2:
                    pe.wait_ge(sem("page_pT"), b - 1)
                for a in range(2):
                    tr = nc.tensor.transpose(ps[:, 4 + b % 2, a * P:(a + 1) * P], pex[:, b % 2, a, 0:P], ident)
                tr.then_inc(sem("page_turned"), 1)

            def turn_last(q4):
                if q4:
                    pe.wait_ge(sem("page_lT"), 4 * q4)
                for a in range(2):
                    tr = nc.tensor.transpose(ps[:, 6, a * P:(a + 1) * P],
                                             plast[:, a, :, :].rearrange("p b j -> p (b j)"), ident)
                tr.then_inc(sem("page_lturned"), 1)

            def values(q4):
                pe.wait_ge(sem("page_lT"), 4 * q4 + 4)
                pe.wait_ge(sem("page_pT"), 4 * q4 + 4)
                if q4:
                    pe.wait_ge(sem("page_o"), q4)
                for g in range(GRP):
                    o = slice(32 * g, 32 * g + 32)
                    q = slice((g % 2) * 64, (g % 2) * 64 + 64)
                    v = slice(P + 32 * g, P + 32 * g + 32)
                    nc.tensor.matmul(ps[o, 7, 0:256].rearrange("p (b q) -> p b q", b=4), kv[:, B + q4, v],
                                     plastT[:, g // 2, :, q], start=True, stop=False)
                    for j in range(4):
                        mm = nc.tensor.matmul(ps[o, 7, 64 * j:64 * j + 64], kv[:, 4 * q4 + j, v], pT[:, j, g // 2, q],
                                              start=False, stop=(j == 3))
                mm.then_inc(sem("page_pv"), 1)

            keys(0)
            scores(0)
            for b in range(B + 2):
                if b + 1 < B:
                    scores(b + 1)
                if 1 <= b <= B:
                    turn(b - 1)
                if b % 4 == 1 and b // 4 + 1 < B // 4:
                    keys(b // 4 + 1)
                if b >= 4 and b % 4 == 0:
                    turn_last(b // 4 - 1)
                if b >= 4 and b % 4 == 1:
                    values(b // 4 - 1)
            pe.wait_ge(sem("page_o"), B // 4)
            for n in range(2):
                for c in range(KC):
                    for k in range(KC):
                        mm = nc.tensor.matmul(ps[:, 2 * c + n, :], page_wo[:, k, c * P:(c + 1) * P],
                                              oT[:, k, n * HALF:(n + 1) * HALF], start=(k == 0), stop=(k == KC - 1))
                    mm.then_inc(sem("page_wo"), 1)

        def page_vector(dve):
            tt, stt = nc.vector.tensor_tensor, nc.vector.scalar_tensor_tensor
            nc.vector.tensor_scalar(gsc[:, 0, :], const("qscale"), 1.0, None, ALU.add).then_inc(sem("page_gain"), 1)
            nc.vector.tensor_scalar(gsc[:, 1, :], const("kscale"), 1.0, None, ALU.add).then_inc(sem("page_gain"), 1)
            for g in range(NT):
                dve.wait_ge(sem("page_raw"), 3 * g + 3)
                nc.vector.tensor_reduce(rms[:, 12 * g:12 * g + 12], sqr[:, g, :].rearrange("p (k f) -> p k f", k=12),
                                        AXX, ALU.add).then_inc(sem("page_ms"), 1)
            dve.wait_ge(sem("page_ms"), NT)
            nc.vector.tensor_scalar(rms[:, :], rms[:, :], 1.0 / PHD, 1e-6, ALU.mult, ALU.add).then_inc(sem("page_ms"), 1)
            dve.wait_ge(sem("page_sqrt"), 1)
            nc.vector.reciprocal(rms[:, :], rms[:, :]).then_inc(sem("page_ms"), 1)
            rotate(dve, nc.vector, range(0, ROT_DVE), rot, "page")
            wait_rotated(dve, NT - 1)
            for n in range(2):
                dve.wait_ge(sem("page_qt"), n + 1)
                for g in range(GRP):
                    nc.vector.tensor_scalar(qmask[:, 16 * n:16 * n + 16, g, 0, :],
                                            ps[:, n, :].rearrange("p (b t) -> p b t", t=S),
                                            const("quad")[:, g:g + 1], None, ALU.mult).then_inc(sem("page_qm"), 1)

            def before(b):
                stt(pmk[:, b % 2, :], const("jstep"), thr[:, b:b + 1], const("band"), ALU.subtract, ALU.min)\
                    .then_inc(sem("page_mask"), 1)
                dve.wait_ge(sem("page_mask"), b + 1)
                dve.wait_ge(sem("page_scores"), b + 1)
                stt(psc[:, b % 2], ps[:, 2 + b % 2, 0:2 * NKEY].rearrange("p (a j) -> p a j", a=2), 1.0 / 16,
                    pmk[:, b % 2:b % 2 + 1, :].to_broadcast([P, 2, NKEY]), ALU.mult, ALU.add).then_inc(sem("page_scaled"), 1)
                dve.wait_ge(sem("page_scaled"), b + 1)
                nc.vector.tensor_reduce(pst[:, b, 0:2], psc[:, b % 2], AXX, ALU.max, negate=True)\
                    .then_inc(sem("page_max"), 1)

            def after(b):
                dve.wait_ge(sem("page_exp"), 2 * b + 2)
                nc.vector.reciprocal(pst[:, b, 4:6], pst[:, b, 2:4]).then_inc(sem("page_rec"), 1)
                dve.wait_ge(sem("page_rec"), b + 1)
                r = pst[:, b, 4:6].unsqueeze(2)
                if b % 4 == 0 and b:
                    dve.wait_ge(sem("page_lturned"), b // 4)
                x = pex[:, b % 2]
                tt(plast[:, :, b % 4, :], x[:, :, P:NKEY], r.to_broadcast([P, 2, S]), ALU.mult).then_inc(sem("page_norm"), 1)
                tt(x[:, :, 0:P], x[:, :, 0:P], r.to_broadcast([P, 2, P]), ALU.mult).then_inc(sem("page_norm"), 1)

            def keep(b):
                dve.wait_ge(sem("page_turned"), b + 1)
                if b % 4 == 0 and b:
                    dve.wait_ge(sem("page_pv"), b // 4)
                nc.vector.tensor_copy(pT[:, b % 4], ps[:, 4 + b % 2, 0:2 * P].rearrange("p (a q) -> p a q", a=2))\
                    .then_inc(sem("page_pT"), 1)

            for b in range(B + 2):
                if b < B:
                    before(b)
                if 1 <= b <= B:
                    after(b - 1)
                if b >= 2:
                    keep(b - 2)
            for n in range(2):
                for c in range(KC):
                    dve.wait_ge(sem("page_wo"), 2 * n + c + 1)
                    nc.vector.tensor_copy(cT[:, c, n * HALF:(n + 1) * HALF], ps[:, 2 * c + n, :]).then_inc(sem("page_out"), 1)

        def page_scalar(act):
            for g in range(NT):
                act.wait_ge(sem("page_proj"), g + 1)
                nc.scalar.activation(sqr[:, g, :], ps[:, g, 0:3 * P], ACT.Square).then_inc(sem("page_raw"), 1)
                nc.scalar.activation(raw[:, g].rearrange("p k f -> p (k f)"), ps[:, g, 0:3 * P], ACT.Copy)\
                    .then_inc(sem("page_raw"), 1)
                nc.scalar.activation(newkv[:, g, P:2 * P], ps[:, g, 3 * P:4 * P], ACT.Copy).then_inc(sem("page_raw"), 1)
            act.wait_ge(sem("page_ms"), NT + 1)
            nc.scalar.activation(rms[:, :], rms[:, :], ACT.Sqrt).then_inc(sem("page_sqrt"), 1)
            wait_rotated(act, NT - 1)
            for n in range(2):
                act.wait_ge(sem("page_qt"), 2 + n + 1)
                for g in range(GRP):
                    nc.scalar.activation(qmask[:, 16 * n:16 * n + 16, g, 1, :],
                                         ps[:, 2 + n, :].rearrange("p (b t) -> p b t", t=S), ACT.Copy,
                                         scale=const("quad")[:, g:g + 1]).then_inc(sem("page_qm"), 1)

            def keep_last(q4):
                act.wait_ge(sem("page_lturned"), q4 + 1)
                if q4:
                    act.wait_ge(sem("page_pv"), q4)
                for j in range(4):
                    nc.scalar.activation(plastT[:, :, j, :], ps[:, 6, 0:2 * P].rearrange("p (a q) -> p a q", a=2),
                                         ACT.Copy, scale=const("quad")[:, j:j + 1]).then_inc(sem("page_lT"), 1)

            def keep_output(q4):
                act.wait_ge(sem("page_pv"), q4 + 1)
                nc.scalar.activation(oT[:, :, q4 * P:(q4 + 1) * P].rearrange("p h (b t) -> p b h t", b=4),
                                     ps[:, 7, 0:256].rearrange("p (b h t) -> p b h t", b=4, h=2),
                                     ACT.Copy).then_inc(sem("page_o"), 1)

            def keep_keys(q4):
                kT = kTs[q4 % 2]
                act.wait_ge(sem("page_k"), q4 + 1)
                if q4 == 1:
                    act.wait_ge(sem("page_new"), 16 * NT)
                if q4 >= 2:
                    act.wait_ge(sem("page_scores"), 4 * q4 - 4)
                nc.scalar.activation(kT[:, :, 0:P], ps[:, 0, :].rearrange("p (b j) -> p b j", b=4), ACT.Copy)\
                    .then_inc(sem("page_kT"), 1)
                nc.scalar.activation(kT[:, :, P:NKEY], ps[:, 1, 0:P].rearrange("p (b j) -> p b j", b=4), ACT.Copy)\
                    .then_inc(sem("page_kT"), 1)

            keep_keys(0)
            for b in range(B):
                act.wait_ge(sem("page_max"), b + 1)
                if b >= 2:
                    act.wait_ge(sem("page_turned"), b - 1)
                    act.wait_ge(sem("page_norm"), 2 * b - 2)
                for a in range(2):
                    nc.scalar.activation(pex[:, b % 2, a, :], psc[:, b % 2, a, :], ACT.Exp, bias=pst[:, b, a:a + 1],
                                         accum_out=pst[:, b, 2 + a:3 + a]).then_inc(sem("page_exp"), 1)
                if b % 4 == 0 and b:
                    keep_last(b // 4 - 1)
                if b % 4 == 2 and b // 4 + 1 < B // 4:
                    keep_keys(b // 4 + 1)
                if b % 4 == 2 and b > 2:
                    keep_output(b // 4 - 1)
            keep_last(B // 4 - 1)
            keep_output(B // 4 - 1)

        wr = wrt[:, :].rearrange("p (c e) -> p c e", c=KC)
        routew = work[0:NE, 9728:9728 + T]
        r0 = 2048
        logit = cut(work, r0, P).rearrange("p (g e) -> p g e", g=NT)
        prb = cut(work, r0 + 128, P).rearrange("p (g e) -> p g e", g=NT)
        wgt = cut(work, r0 + 256, P).rearrange("p (g e) -> p g e", g=NT)
        oh = cut(work, r0 + 384, P).rearrange("p (g e) -> p g e", g=NT)
        best = cut(work, r0 + 512, 64).rearrange("p (g x) -> p g x", g=NT)
        bidx = cut(work, r0 + 576, 64).rearrange("p (g x) -> p g x", g=NT)
        rst = cut(work, r0 + 640, 64).rearrange("p (g x) -> p g x", g=NT)
        bidxu = int_buf(64).rearrange("p (g x) -> p g x", g=NT)

        def route_tensor_first(pe):
            pe.wait_ge(sem("ld_wR"), 16)
            pe.wait_ge(sem("page_out"), 4)
            for g in range(NT):
                for k in range(KC):
                    mm = nc.tensor.matmul(ps[:, 2, g * NE:(g + 1) * NE], cT[:, k, g * P:(g + 1) * P], wr[:, k, :],
                                          start=(k == 0), stop=(k == KC - 1))
            mm.then_inc(sem("route_logit"), 1)

        def route_tensor(pe, i):
            if i != 1:
                return
            pe.wait_ge(sem("route_w"), 1)
            for g in range(NT):
                tr = nc.tensor.transpose(ps[0:NE, 2 + g // 4, (g % 4) * P:(g % 4 + 1) * P], wgt[:, g, :], ident)
                if g % 4 == 3:
                    tr.then_inc(sem("route_turned"), 1)

        def route_vector(dve):
            tt = nc.vector.tensor_tensor
            bc = lambda a: a.unsqueeze(2).to_broadcast([P, NT, NE])
            step = [0]

            def link(ins):
                ins.then_inc(sem("route_step"), 1)
                step[0] += 1
                dve.wait_ge(sem("route_step"), step[0])

            dve.wait_ge(sem("route_logit"), 1)
            link(tt(logit, ps[:, 2, 0:P].rearrange("p (g e) -> p g e", g=NT),
                    const("rbias").unsqueeze(1).to_broadcast([P, NT, NE]), ALU.add))
            link(nc.vector.tensor_reduce(rst[:, :, 0], logit, AXX, ALU.max))
            tt(logit, logit, bc(rst[:, :, 0]), ALU.subtract).then_inc(sem("route_shift"), 1)
            dve.wait_ge(sem("route_exp"), 1)
            link(nc.vector.tensor_reduce(rst[:, :, 1], prb, AXX, ALU.add))
            link(nc.vector.reciprocal(rst[:, :, 2], rst[:, :, 1]))
            link(tt(prb, prb, bc(rst[:, :, 2]), ALU.mult))
            for g in range(NT):
                link(nc.vector.max(best[:, g, :], prb[:, g, :]))
                link(nc.vector.max_index(bidxu[:, g, :].bitcast(U32), best[:, g, :], prb[:, g, :]))
            link(nc.vector.tensor_copy(bidx, bidxu))
            e3 = const("e16").unsqueeze(1).to_broadcast([P, NT, NE])
            link(tt(oh, e3, bc(bidx[:, :, 0]), ALU.is_equal))
            link(tt(wgt, e3, bc(bidx[:, :, 1]), ALU.is_equal))
            link(tt(wgt, wgt, oh, ALU.add))
            link(tt(wgt, wgt, prb, ALU.mult))
            link(nc.vector.scalar_tensor_tensor(rst[:, :, 3], best[:, :, 0], 1e-9, best[:, :, 1], ALU.add, ALU.add))
            link(nc.vector.reciprocal(rst[:, :, 4], rst[:, :, 3]))
            tt(wgt, wgt, bc(rst[:, :, 4]), ALU.mult).then_inc(sem("route_w"), 1)
            for n in range(2):
                dve.wait_ge(sem("route_turned"), n + 1)
                nc.vector.tensor_copy(routew[:, n * HALF:(n + 1) * HALF], ps[0:NE, 2 + n, :]).then_inc(sem("route_kept"), 1)

        def route_scalar(act):
            act.wait_ge(sem("route_shift"), 1)
            nc.scalar.activation(prb, logit, ACT.Exp).then_inc(sem("route_exp"), 1)

        att_a = Attention(xnT, 0, ("mix_out", 4), "ld_wA", True, xT)
        att_b = Attention(xT, 2048, ("ffn_out", 8), "ld_wB", False, yT)

        def weights(base, *shapes):
            got = []
            for k, n in shapes:
                got.append(cut(wbig, base, k * n).rearrange("p (k n) -> p k n", k=k))
                base += k * n
            return got

        ag, au, wguA, bg, bu, wdA, bd = weights(
            0, (KC, P), (KC, P), (2 * KC, HID), (1, HID), (1, HID), (HID // P, D + P), (1, D))
        wguB, wdB = weights(wF_d.shape[1], (2 * KC, HID), (HID // P, D))
        moe_cols = (NE + 1) * P
        wguE, wdE = weights(0, (2 * KC, moe_cols), (NE + 1, D))
        lora = {"first": [ag, au], "second": [bg[:, 0, :], bu[:, 0, :]], "down_second": bd[:, 0, :]}

        state = {}

        def prep_vector(per_unit):
            def run(dve, i):
                if "prep" not in state:
                    state["prep"] = prep_run(dve)
                state["prep"](per_unit)
            return run

        def prep_tensor(pe, i):
            if i != -(-N_SPREAD // PREP_A):
                return
            pe.wait_ge(sem("prep_step"), N_SPREAD)
            nc.tensor.transpose(ps[:, 3, 0:B], krow[:, 0:P], ident[0:B, 0:B])
            nc.tensor.matmul(ps[:, 3, B:NGT], last32.rearrange("p q j -> p (q j)"), row("seqdiv"), start=True, stop=True)
            nc.tensor.matmul(ps[:, 3, 64:64 + 3 * B * NWR], row("ones"), spread.rearrange("p k b s -> p (k b s)"),
                             start=True, stop=True).then_inc(sem("prep_spread"), 1)

        def angles_scalar(act, i):
            if i != 15:
                return
            act.wait_ge(sem("prep_step"), N_PREP)
            nc.scalar.activation(sinb.rearrange("p g f -> p (g f)"), ang[:, :], ACT.Sin).then_inc(sem("rope_ready"), 1)
            nc.scalar.activation(cosb.rearrange("p g f -> p (g f)"), angc[:, :], ACT.Sin).then_inc(sem("rope_ready"), 1)

        ffn_a = Gated([], xT, wguA, wdA, HID // P, ("att_out", 0), "ld_wF", ("att_pv_done", NT), ("att_pv_done", NT),
                      lora=lora, out_to=yT, extra_tensor=prep_tensor, extra_vector=prep_vector(PREP_A))
        ffn_b = Gated([ffn_a], yT, wguB, wdB, HID // P, ("ffn_out", 0), "ld_wG", ("ffn_up_done", 15), ("ffn_down_done", 15),
                      add=True, out_to=xT, extra_vector=prep_vector(6), extra_scalar=angles_scalar)
        ffn_a.following, ffn_b.early = ffn_b, 1
        moe = Gated([ffn_a, ffn_b], cT, wguE, wdE, NE + 1, ("page_out", 0), "ld_wE", ("page_pv", B // 4), ("page_pv", B // 4),
                    routed=NE, add=True, out_to=xT, extra_tensor=route_tensor, before_vector=route_vector)

        block = ctx.enter_context(nc.Block())

        @block.sync
        def _(sp):
            sp.dma_start(ints[:, :], ints_d).then_inc(sem("ld_ints"), 16)
            sp.dma_start(x_tok.rearrange("p g f -> p (g f)"), x_tok_d).then_inc(sem("ld_x_tok"), 16)
            sp.wait_ge(sem("mix_gather"), 16 * NT)
            sp.dma_start(small[:, :], small_d).then_inc(sem("ld_small"), 16)
            sp.dma_start(wmid[:, 0:2048], wA_d).then_inc(sem("ld_wA"), 16)
            sp.dma_start(xT.rearrange("p c t -> p (c t)"), x_feat_d).then_inc(sem("ld_x_feat"), 16)
            n = wF_d.shape[1]
            sp.dma_start(wbig[:, 0:n], wF_d).then_inc(sem("ld_wF"), 16)
            sp.dma_start(wbig[:, n:n + wG_d.shape[1]], wG_d).then_inc(sem("ld_wG"), 16)
            sp.dma_start(wmid[:, 2048:4096], wB_d).then_inc(sem("ld_wB"), 16)
            sp.dma_start(wmid[:, 4096:4096 + wL_d.shape[1]], wL_d).then_inc(sem("ld_wL"), 16)
            sp.dma_start(wrt[:, :], wR_d).then_inc(sem("ld_wR"), 16)
            sp.wait_ge(sem("ffn_out"), 8)
            sp.dma_start(wpage, wP_d).then_inc(sem("ld_wP"), 16)
            sp.dma_start(wbig[:, 0:wE_d.shape[1]], wE_d).then_inc(sem("ld_wE"), 16)
            for g in range(NT):
                wait_rotated(sp, g)
                sp.wait_ge(sem("page_raw"), 3 * g + 3)
                sp.dma_start(new_kv[g * P:(g + 1) * P, :], newkv[:, g, :]).then_inc(sem("page_new"), 16)
            sp.wait_ge(sem("route_kept"), 2)
            sp.dma_start(route_d[:, :], routew[:, :]).then_inc(sem("route_stored"), 16)
            sp.wait_ge(sem("route_stored"), 16)
            for e in range(NE):
                if e >= 2:
                    sp.wait_ge(sem("ffn_act_ready"), moe.count("act_ready", 2 * e))
                sp.dma_start(share[:, e % 2, :], route_d[e:e + 1, :].to_broadcast([P, T]))\
                    .then_inc(sem(f"share{e % 2}"), 16)
            for n in range(2):
                sp.wait_ge(sem("ffn_out"), moe.count("out", 2 * n + 2))
                sp.dma_start(out.rearrange("(c p) t -> p c t", p=P)[:, :, n * HALF:(n + 1) * HALF],
                             xT[:, :, n * HALF:(n + 1) * HALF]).then_inc(sem("stored"), 16)
            sp.wait_ge(sem("stored"), 32)

        @block.gpsimd
        def _(pool):
            def gather(dst, table, rows, bound=None):
                return nc.gpsimd.indirect_dma_start(
                    dst, None, table, bass.IndirectOffsetOnAxis(ap=rows.bitcast(U32), axis=0),
                    **({} if bound is None else {"bounds_check": bound, "oob_is_err": False}))

            pool.wait_ge(sem("mix_rows"), 1)
            for g in range(NT):
                gather(mix_w[:, g, :], mix_table, mix_rows[:, g:g + 1]).then_inc(sem("mix_gather"), 16)
            nc.gpsimd.memset(vpar.rearrange("p g a h d -> p (g a h d)"), 0.0).then_inc(sem("zeroed"), 1)
            nc.gpsimd.memset(pdiag.rearrange("p r h q -> p (r h q)"), 0.0).then_inc(sem("zeroed"), 1)
            att_a.gpsimd(pool)
            ffn_a.gpsimd(pool)
            ffn_b.gpsimd(pool)
            pool.wait_ge(sem("ffn_down_done"), ffn_b.count("down_done", 16))
            nc.gpsimd.memset(vpar.rearrange("p g a h d -> p (g a h d)"), 0.0).then_inc(sem("zeroed"), 1)
            nc.gpsimd.memset(pdiag.rearrange("p r h q -> p (r h q)"), 0.0).then_inc(sem("zeroed"), 1)
            att_b.gpsimd(pool)
            pool.wait_ge(sem("att_out"), 2 * ATT_TOTAL["out"])
            pool.wait_ge(sem("prep_step"), N_PREP)
            order = [t for q4 in range(B // 4) for t in [B + q4] + list(range(4 * q4, 4 * q4 + 4))]
            for t in order:
                gather(kv[:, t, :], cache, key_rowi[:, t:t + 1]).then_inc(sem("cached"), 16)
            rotate(pool, nc.gpsimd, range(ROT_DVE, NT), rot_pool, "pagepool")
            pool.wait_ge(sem("cached"), 16 * NGT)
            pool.wait_ge(sem("page_new"), 16 * NT)
            for n, t in enumerate(order):
                gather(kv[:, t, :], new_kv, new_rowi[:, t:t + 1], T - 1).then_inc(sem(f"overlay{n // 5}"), 16)
            moe.gpsimd(pool)

        @block.scalar
        def _(act):
            act.wait_ge(sem("mix_var"), 1)
            nc.scalar.activation(rstd[:, :], rstd[:, :], ACT.Sqrt).then_inc(sem("mix_sqrt"), 1)
            att_a.scalar(act)
            ffn_a.scalar(act)
            ffn_b.scalar(act)
            act.wait_ge(sem("ffn_down_done"), ffn_b.count("down_done", 16))
            nb = slice(0, NBANK * NH)
            nc.scalar.activation(sel_r[nb].rearrange("p n c o -> p (n c o)"), const("sel")[nb], ACT.Copy)\
                .then_inc(sem("sel_ready"), 1)
            att_b.scalar(act)
            lin_scalar(act)
            page_scalar(act)
            moe.scalar(act)

        @block.vector
        def _(dve):
            dve.wait_ge(sem("ld_ints"), 16)
            nc.vector.scalar_tensor_tensor(mix_rows, ints[:, 0:NT], 32.0, ints[:, ints_d.shape[1] - NT:ints_d.shape[1]],
                                           ALU.mult, ALU.add).then_inc(sem("mix_rows"), 1)
            dve.wait_ge(sem("ld_small"), 16)
            nc.vector.tensor_scalar(admask[:, :], ints[:, 2 * NT:2 * NT + B], const("adapter"), None, ALU.is_equal)\
                .then_inc(sem("masks"), 1)
            nc.vector.tensor_scalar(temps[:, :], const("temp"), 4.0, 0.25, ALU.min, ALU.mult).then_inc(sem("masks"), 1)
            for g in range(NT):
                dve.wait_ge(sem("mixed"), (g | 1) + 1)
                m = ps[:, g // 2, (g % 2) * D:(g % 2 + 1) * D]
                nc.vector.bn_stats(stats[:, g, :], m).then_inc(sem("mix_stats"), 1)
                dve.wait_ge(sem("mix_stats"), g + 1)
                nc.vector.bn_aggr(meanvar[:, g, :], stats[:, g, :]).then_inc(sem("mix_aggr"), 1)
            dve.wait_ge(sem("mix_aggr"), NT)
            nc.vector.tensor_scalar(rstd[:, :], meanvar[:, :, 1], 1e-5, None, ALU.add).then_inc(sem("mix_var"), 1)
            dve.wait_ge(sem("mix_sqrt"), 1)
            nc.vector.reciprocal(rstd[:, :], rstd[:, :]).then_inc(sem("mix_rstd"), 1)
            dve.wait_ge(sem("mix_rstd"), 1)
            for g in range(NT):
                nc.vector.tensor_scalar(xn_tok[:, g, :], ps[:, g // 2, (g % 2) * D:(g % 2 + 1) * D],
                                        meanvar[:, g, 0:1], rstd[:, g:g + 1], ALU.subtract, ALU.mult)\
                    .then_inc(sem("mix_norm"), 1)
            for c in range(KC):
                for h in range(2):
                    dve.wait_ge(sem("mix_turned"), 2 * c + h + 1)
                    nc.vector.tensor_scalar(xnT[:, c, h * HALF:(h + 1) * HALF], ps[:, 4 + 2 * c + h, :],
                                            const("ln_g")[:, c:c + 1], const("ln_b")[:, c:c + 1], ALU.mult, ALU.add)\
                        .then_inc(sem("mix_out"), 1)
            att_a.vector(dve)
            dve.wait_ge(sem("masks"), 2)
            ffn_a.vector(dve)
            ffn_b.vector(dve)
            att_b.vector(dve)
            lin_vector(dve)
            page_vector(dve)
            moe.vector(dve)

        @block.tensor
        def _(pe):
            pe.wait_ge(sem("ld_x_tok"), 16)
            pe.wait_ge(sem("mix_gather"), 16 * NT)
            for g in range(NT):
                for j in range(4):
                    q = slice(32 * j, 32 * j + 32)
                    mm = nc.tensor.matmul(ps[q, g // 2, (g % 2) * D:(g % 2 + 1) * D], mix_w[q, g, :], x_tok[q, g, :],
                                          start=True, stop=True)
                mm.then_inc(sem("mixed"), 1)
            pe.wait_ge(sem("ld_small"), 16)
            for c in range(KC):
                for g in range(NT):
                    pe.wait_ge(sem("mix_norm"), g + 1)
                    tr = nc.tensor.transpose(ps[:, 4 + 2 * c + g // 4, (g % 4) * P:(g % 4 + 1) * P],
                                             xn_tok[:, g, c * P:(c + 1) * P], ident)
                    if g % 4 == 3:
                        tr.then_inc(sem("mix_turned"), 1)
            att_a.tensor(pe)
            ffn_a.tensor(pe)
            ffn_b.tensor(pe)
            att_b.tensor(pe)
            lin_tensor(pe)
            page_tensor(pe)
            route_tensor_first(pe)
            moe.tensor(pe)


def kernel(**inputs):
    import concourse.bacc as _bacc
    from concourse.bass_utils import run_bass_kernel_spmd as _run

    nc = _bacc.Bacc("TRN2", target_bir_lowering=False, num_devices=1)
    arrays, args = {}, []
    packed, small_at = layout({k: np.asarray(v) for k, v in inputs.items()})
    for name in ("x_tok", "x_feat", "mix_table", "small", "ints", "wA", "wB", "wF", "wG", "wL", "wP", "cache", "wR", "wE"):
        a = np.ascontiguousarray(packed[name])
        arrays[f"in_{name}_dram"] = a
        args.append(nc.dram_tensor(f"in_{name}_dram", a.shape, mybir.dt.from_np(a.dtype), kind="ExternalInput").ap())
    args.append(nc.dram_tensor("out_0_dram", (D, T), F32, kind="ExternalOutput").ap())
    program(nc, small_at, *args)
    r = _run(nc, [arrays], core_ids=[0])
    return r.results[0]["out_0_dram"].T.reshape(B, S, D)
```
